# Optimizing a Trainium2 kernel written in Bass

```python
import numpy as np
import jax
import jax.numpy as jnp

def _softmax(x, axis=-1):
    return jax.nn.softmax(x, axis=axis)

def _gelu(x):
    return jax.nn.gelu(x, approximate=True)

def _silu(x):
    return jax.nn.silu(x)

def _sigmoid(x):
    return jax.nn.sigmoid(x)

def _layernorm(x, axis=-1, eps=1e-05):
    m = jnp.mean(x, axis=axis, keepdims=True)
    v = jnp.var(x, axis=axis, keepdims=True)
    return (x - m) / jnp.sqrt(v + eps)

def _scatter_add(tgt, idx, src, axis=0):
    return tgt.at[idx].add(src)

def _segment_sum(src, seg, n):
    return jax.ops.segment_sum(src, seg, n)
kernel_name = 'mk_sandwich_d2_jaxref_r8_801855'

def setup_inputs(seed: int=0):
    np.random.seed(seed)
    _w = jnp.asarray

    def _L0_attn_setup():
        import jax, jax.numpy as jnp
        import numpy as np
        EMBED = 128
        HEADS = 16
        key = jax.random.key(seed)
        ks = jax.random.split(key, 6)
        N, S = (1, 512)
        half = EMBED // 2
        x = jax.random.normal(ks[0], (N, S, EMBED), dtype=jnp.float32)
        Wq = jax.random.normal(ks[1], (half, half), dtype=jnp.float32) * 0.02
        Wk = jax.random.normal(ks[2], (half, half), dtype=jnp.float32) * 0.02
        Wv = jax.random.normal(ks[3], (half, half), dtype=jnp.float32) * 0.02
        Wo = jax.random.normal(ks[4], (EMBED, half), dtype=jnp.float32) * 0.02
        bo = jnp.zeros((EMBED,), dtype=jnp.float32)
        return {'x': x, 'Wq': Wq, 'Wk': Wk, 'Wv': Wv, 'Wo': Wo, 'bo': bo}
    _L0_attn_in = _L0_attn_setup()

    def _L0_ffn_setup():
        import jax, jax.numpy as jnp
        import numpy as np
        import math
        D = 128
        H = 16
        E = 8
        TOPK = 2
        LAT = D // 2
        KPH = LAT // H
        HD = D // H

        def _forward(hs, q_w, q_b, k_w, k_b, v_w, v_b, o_w, o_b, router_w, router_b, w1, b1, w2, b2):
            B, S, _ = hs.shape
            Q = (hs @ q_w + q_b).reshape(B, S, H, HD).transpose(0, 2, 1, 3)
            K = (hs @ k_w + k_b).reshape(B, S, H, KPH).transpose(0, 2, 1, 3)
            V = (hs @ v_w + v_b).reshape(B, S, H, KPH).transpose(0, 2, 1, 3)
            scores = jnp.einsum('bhsk,bhtk->bhst', Q[..., :KPH], K) / math.sqrt(KPH)
            attn = jax.nn.softmax(scores, axis=-1)
            ao = jnp.einsum('bhst,bhtv->bhsv', attn, V)
            ao = ao.transpose(0, 2, 1, 3).reshape(B, S, H * KPH)
            ao = jnp.concatenate([ao, jnp.zeros((B, S, D - LAT), ao.dtype)], axis=-1)
            mla_out = ao @ o_w + o_b
            probs = jax.nn.softmax(mla_out @ router_w + router_b, axis=-1)
            topw, topi = jax.lax.top_k(probs, TOPK)
            topw = topw / (topw.sum(-1, keepdims=True) + 1e-08)
            combine = jnp.sum(jax.nn.one_hot(topi, E, dtype=probs.dtype) * topw[..., None], axis=-2)
            h1 = jnp.einsum('bsd,edf->ebsf', mla_out, w1) + b1[:, None, None, :]
            h1 = jax.nn.gelu(h1, approximate=False)
            h2 = jnp.einsum('ebsf,efd->ebsd', h1, w2) + b2[:, None, None, :]
            moe_out = jnp.einsum('bse,ebsd->bsd', combine, h2)
            return hs + 0.3 * moe_out
        key = jax.random.key(seed)
        ks = jax.random.split(key, 16)
        s = 0.02
        inp = {'hidden_states': jax.random.normal(ks[0], (2, 256, D), jnp.float32), 'q_w': jax.random.normal(ks[1], (D, D), jnp.float32) * s, 'q_b': jnp.zeros((D,), jnp.float32), 'k_w': jax.random.normal(ks[2], (D, LAT), jnp.float32) * s, 'k_b': jnp.zeros((LAT,), jnp.float32), 'v_w': jax.random.normal(ks[3], (D, LAT), jnp.float32) * s, 'v_b': jnp.zeros((LAT,), jnp.float32), 'o_w': jax.random.normal(ks[4], (D, D), jnp.float32) * s, 'o_b': jnp.zeros((D,), jnp.float32), 'router_w': jax.random.normal(ks[5], (D, E), jnp.float32) * s, 'router_b': jnp.zeros((E,), jnp.float32), 'w1': jax.random.normal(ks[6], (E, D, 2 * D), jnp.float32) * s, 'b1': jnp.zeros((E, 2 * D), jnp.float32), 'w2': jax.random.normal(ks[7], (E, 2 * D, D), jnp.float32) * s, 'b2': jnp.zeros((E, D), jnp.float32)}
        return inp
    _L0_ffn_in = _L0_ffn_setup()

    def _L1_attn_setup():
        import jax, jax.numpy as jnp
        import numpy as np
        B, T, C = (4, 256, 128)
        NUM_HEADS = 16
        OUT_DIM = 128
        HEAD_DIM = OUT_DIM // NUM_HEADS
        key = jax.random.key(seed)
        kx, kk, kq, kv, kp = jax.random.split(key, 5)
        return {'x': jax.random.normal(kx, (B, T, C), dtype=jnp.float32), 'W_key': jax.random.normal(kk, (OUT_DIM, C), dtype=jnp.float32), 'W_query': jax.random.normal(kq, (OUT_DIM, C), dtype=jnp.float32), 'W_value': jax.random.normal(kv, (OUT_DIM, C), dtype=jnp.float32), 'W_proj': jax.random.normal(kp, (OUT_DIM, OUT_DIM), dtype=jnp.float32)}
    _L1_attn_in = _L1_attn_setup()

    def _L1_ffn_setup():
        import jax, jax.numpy as jnp
        import numpy as np
        E = 16
        K = 4
        G = 4
        TG = 2
        NS = 2
        H = 128
        I = 176
        SCALE = 1.0

        def _gate(x2d, gate_w, gate_bias):
            T = x2d.shape[0]
            logits = x2d.astype(jnp.float32) @ gate_w.astype(jnp.float32).T
            scores = jax.nn.sigmoid(logits)
            sfc = scores + gate_bias[None, :]
            grp = sfc.reshape(T, G, E // G)
            top2, _ = jax.lax.top_k(grp, 2)
            group_scores = top2.sum(-1)
            _, gidx = jax.lax.top_k(group_scores, TG)
            gmask = jnp.zeros((T, G), sfc.dtype).at[jnp.arange(T)[:, None], gidx].set(1.0)
            smask = jnp.repeat(gmask, E // G, axis=1) > 0
            tmp = jnp.where(smask, sfc, 0.0)
            _, topk_idx = jax.lax.top_k(tmp, K)
            topk_w = jnp.take_along_axis(scores, topk_idx, axis=1)
            topk_w = topk_w / (topk_w.sum(-1, keepdims=True) + 1e-20)
            return (topk_idx, topk_w * SCALE)
        key = jax.random.key(seed)
        ks = jax.random.split(key, 8)
        bound = 1.0 / np.sqrt(H)
        return {'hidden_states': jax.random.normal(ks[0], (1, 128, H), jnp.float32), 'gate_w': jax.random.uniform(ks[1], (E, H), jnp.float32, -bound, bound), 'gate_bias': jnp.zeros((E,), jnp.float32), 'gate_proj': jax.random.normal(ks[2], (E, I, H), jnp.float32) * 0.02, 'up_proj': jax.random.normal(ks[3], (E, I, H), jnp.float32) * 0.02, 'down_proj': jax.random.normal(ks[4], (E, H, I), jnp.float32) * 0.02, 'shared_gate_w': jax.random.normal(ks[5], (I * NS, H), jnp.float32) * 0.02, 'shared_up_w': jax.random.normal(ks[6], (I * NS, H), jnp.float32) * 0.02, 'shared_down_w': jax.random.normal(ks[7], (H, I * NS), jnp.float32) * 0.02}
    _L1_ffn_in = _L1_ffn_setup()
    _d = {'L0_attn_x': _L0_attn_in['x'], 'L0_attn_Wq': _L0_attn_in['Wq'], 'L0_attn_Wk': _L0_attn_in['Wk'], 'L0_attn_Wv': _L0_attn_in['Wv'], 'L0_attn_Wo': _L0_attn_in['Wo'], 'L0_attn_bo': _L0_attn_in['bo'], 'L0_ffn_q_w': _L0_ffn_in['q_w'], 'L0_ffn_q_b': _L0_ffn_in['q_b'], 'L0_ffn_k_w': _L0_ffn_in['k_w'], 'L0_ffn_k_b': _L0_ffn_in['k_b'], 'L0_ffn_v_w': _L0_ffn_in['v_w'], 'L0_ffn_v_b': _L0_ffn_in['v_b'], 'L0_ffn_o_w': _L0_ffn_in['o_w'], 'L0_ffn_o_b': _L0_ffn_in['o_b'], 'L0_ffn_router_w': _L0_ffn_in['router_w'], 'L0_ffn_router_b': _L0_ffn_in['router_b'], 'L0_ffn_w1': _L0_ffn_in['w1'], 'L0_ffn_b1': _L0_ffn_in['b1'], 'L0_ffn_w2': _L0_ffn_in['w2'], 'L0_ffn_b2': _L0_ffn_in['b2'], 'L1_attn_W_key': _L1_attn_in['W_key'], 'L1_attn_W_query': _L1_attn_in['W_query'], 'L1_attn_W_value': _L1_attn_in['W_value'], 'L1_attn_W_proj': _L1_attn_in['W_proj'], 'L1_ffn_gate_w': _L1_ffn_in['gate_w'], 'L1_ffn_gate_bias': _L1_ffn_in['gate_bias'], 'L1_ffn_gate_proj': _L1_ffn_in['gate_proj'], 'L1_ffn_up_proj': _L1_ffn_in['up_proj'], 'L1_ffn_down_proj': _L1_ffn_in['down_proj'], 'L1_ffn_shared_gate_w': _L1_ffn_in['shared_gate_w'], 'L1_ffn_shared_up_w': _L1_ffn_in['shared_up_w'], 'L1_ffn_shared_down_w': _L1_ffn_in['shared_down_w']}
    _x0 = _d['L0_attn_x']
    _d['L0_attn_x'] = jax.random.normal(jax.random.fold_in(jax.random.key(seed), 1), (4, 1024, 128), dtype=_x0.dtype)
    del _x0
    return _d

def reference(L0_attn_x, L0_attn_Wq, L0_attn_Wk, L0_attn_Wv, L0_attn_Wo, L0_attn_bo, L0_ffn_q_w, L0_ffn_q_b, L0_ffn_k_w, L0_ffn_k_b, L0_ffn_v_w, L0_ffn_v_b, L0_ffn_o_w, L0_ffn_o_b, L0_ffn_router_w, L0_ffn_router_b, L0_ffn_w1, L0_ffn_b1, L0_ffn_w2, L0_ffn_b2, L1_attn_W_key, L1_attn_W_query, L1_attn_W_value, L1_attn_W_proj, L1_ffn_gate_w, L1_ffn_gate_bias, L1_ffn_gate_proj, L1_ffn_up_proj, L1_ffn_down_proj, L1_ffn_shared_gate_w, L1_ffn_shared_up_w, L1_ffn_shared_down_w):

    def _L0_attn_ref(x, Wq, Wk, Wv, Wo, bo):
        import jax, jax.numpy as jnp
        import numpy as np
        EMBED = 128
        HEADS = 16
        N, S, E = x.shape
        H = HEADS
        Dh = E // 2 // H
        scale = float(E // H) ** 0.5
        left = x[..., :E // 2]
        q = (left @ Wq.T).reshape(N, S, H, Dh)
        k = (left @ Wk.T).reshape(N, S, H, Dh)
        v = (left @ Wv.T).reshape(N, S, H, Dh)
        energy = jnp.einsum('nqhd,nkhd->nqkh', q, k)
        att = jax.nn.softmax(energy / scale, axis=2)
        out = jnp.einsum('nqkh,nkhd->nqhd', att, v)
        out = out.reshape(N, S, E // 2)
        return out @ Wo.T + bo

    def _L0_ffn_ref(hidden_states, q_w, q_b, k_w, k_b, v_w, v_b, o_w, o_b, router_w, router_b, w1, b1, w2, b2):
        import jax, jax.numpy as jnp
        import numpy as np
        import math
        D = 128
        H = 16
        E = 8
        TOPK = 2
        LAT = D // 2
        KPH = LAT // H
        HD = D // H

        def _forward(hs, q_w, q_b, k_w, k_b, v_w, v_b, o_w, o_b, router_w, router_b, w1, b1, w2, b2):
            B, S, _ = hs.shape
            Q = (hs @ q_w + q_b).reshape(B, S, H, HD).transpose(0, 2, 1, 3)
            K = (hs @ k_w + k_b).reshape(B, S, H, KPH).transpose(0, 2, 1, 3)
            V = (hs @ v_w + v_b).reshape(B, S, H, KPH).transpose(0, 2, 1, 3)
            scores = jnp.einsum('bhsk,bhtk->bhst', Q[..., :KPH], K) / math.sqrt(KPH)
            attn = jax.nn.softmax(scores, axis=-1)
            ao = jnp.einsum('bhst,bhtv->bhsv', attn, V)
            ao = ao.transpose(0, 2, 1, 3).reshape(B, S, H * KPH)
            ao = jnp.concatenate([ao, jnp.zeros((B, S, D - LAT), ao.dtype)], axis=-1)
            mla_out = ao @ o_w + o_b
            probs = jax.nn.softmax(mla_out @ router_w + router_b, axis=-1)
            topw, topi = jax.lax.top_k(probs, TOPK)
            topw = topw / (topw.sum(-1, keepdims=True) + 1e-08)
            combine = jnp.sum(jax.nn.one_hot(topi, E, dtype=probs.dtype) * topw[..., None], axis=-2)
            h1 = jnp.einsum('bsd,edf->ebsf', mla_out, w1) + b1[:, None, None, :]
            h1 = jax.nn.gelu(h1, approximate=False)
            h2 = jnp.einsum('ebsf,efd->ebsd', h1, w2) + b2[:, None, None, :]
            moe_out = jnp.einsum('bse,ebsd->bsd', combine, h2)
            return hs + 0.3 * moe_out
        return _forward(hidden_states, q_w, q_b, k_w, k_b, v_w, v_b, o_w, o_b, router_w, router_b, w1, b1, w2, b2)

    def _L1_attn_ref(x, W_key, W_query, W_value, W_proj):
        import jax, jax.numpy as jnp
        import numpy as np
        B, T, C = (4, 256, 128)
        NUM_HEADS = 16
        OUT_DIM = 128
        HEAD_DIM = OUT_DIM // NUM_HEADS
        b, t, c = x.shape
        h, hd = (NUM_HEADS, HEAD_DIM)
        inv_sqrt_c = c ** (-0.5)

        def proj(W):
            return jnp.einsum('btc,oc->bto', x, W).reshape(b, t, h, hd).transpose(0, 2, 1, 3) * inv_sqrt_c
        k = proj(W_key)
        q = proj(W_query)
        v = proj(W_value)
        scores = jnp.einsum('bhqd,bhkd->bhqk', q, k) * hd ** (-0.5)
        causal = jnp.tril(jnp.ones((t, t), dtype=bool))
        scores = jnp.where(causal, scores, -jnp.inf)
        weight = jax.nn.softmax(scores, axis=-1)
        out = jnp.einsum('bhqk,bhkd->bhqd', weight, v)
        out = out.transpose(0, 2, 1, 3).reshape(b, t, h * hd)
        out = jnp.einsum('bto,po->btp', out, W_proj) * W_proj.shape[-1] ** (-0.5)
        return out

    def _L1_ffn_ref(hidden_states, gate_w, gate_bias, gate_proj, up_proj, down_proj, shared_gate_w, shared_up_w, shared_down_w):
        import jax, jax.numpy as jnp
        import numpy as np
        E = 16
        K = 4
        G = 4
        TG = 2
        NS = 2
        H = 128
        I = 176
        SCALE = 1.0

        def _gate(x2d, gate_w, gate_bias):
            T = x2d.shape[0]
            logits = x2d.astype(jnp.float32) @ gate_w.astype(jnp.float32).T
            scores = jax.nn.sigmoid(logits)
            sfc = scores + gate_bias[None, :]
            grp = sfc.reshape(T, G, E // G)
            top2, _ = jax.lax.top_k(grp, 2)
            group_scores = top2.sum(-1)
            _, gidx = jax.lax.top_k(group_scores, TG)
            gmask = jnp.zeros((T, G), sfc.dtype).at[jnp.arange(T)[:, None], gidx].set(1.0)
            smask = jnp.repeat(gmask, E // G, axis=1) > 0
            tmp = jnp.where(smask, sfc, 0.0)
            _, topk_idx = jax.lax.top_k(tmp, K)
            topk_w = jnp.take_along_axis(scores, topk_idx, axis=1)
            topk_w = topk_w / (topk_w.sum(-1, keepdims=True) + 1e-20)
            return (topk_idx, topk_w * SCALE)
        orig_shape = hidden_states.shape
        x = hidden_states.reshape(-1, H)
        topk_idx, topk_w = _gate(x, gate_w, gate_bias)
        combine_w = (jax.nn.one_hot(topk_idx, E, dtype=x.dtype) * topk_w[..., None]).sum(1)
        g = jnp.einsum('th,eih->tei', x, gate_proj)
        u = jnp.einsum('th,eih->tei', x, up_proj)
        act = jax.nn.silu(g) * u
        y = jnp.einsum('tei,ehi,te->th', act, down_proj, combine_w)
        sg = x @ shared_gate_w.T
        su = x @ shared_up_w.T
        y = y + jax.nn.silu(sg) * su @ shared_down_w.T
        return y.reshape(orig_shape)
    x = L0_attn_x
    x = x + _layernorm(_L0_attn_ref(_layernorm(x, axis=-1), L0_attn_Wq, L0_attn_Wk, L0_attn_Wv, L0_attn_Wo, L0_attn_bo), axis=-1)
    x = x + _layernorm(_L0_ffn_ref(_layernorm(x, axis=-1), L0_ffn_q_w, L0_ffn_q_b, L0_ffn_k_w, L0_ffn_k_b, L0_ffn_v_w, L0_ffn_v_b, L0_ffn_o_w, L0_ffn_o_b, L0_ffn_router_w, L0_ffn_router_b, L0_ffn_w1, L0_ffn_b1, L0_ffn_w2, L0_ffn_b2), axis=-1)
    x = x + _layernorm(_L1_attn_ref(_layernorm(x, axis=-1), L1_attn_W_key, L1_attn_W_query, L1_attn_W_value, L1_attn_W_proj), axis=-1)
    x = x + _layernorm(_L1_ffn_ref(_layernorm(x, axis=-1), L1_ffn_gate_w, L1_ffn_gate_bias, L1_ffn_gate_proj, L1_ffn_up_proj, L1_ffn_down_proj, L1_ffn_shared_gate_w, L1_ffn_shared_up_w, L1_ffn_shared_down_w), axis=-1)
    return x

_drawn_inputs = setup_inputs


def setup_inputs(seed=0):
    import zlib

    import numpy as np

    out = dict(_drawn_inputs(seed))
    spreads = {'L0_attn_bo': (0.0, 0.1),
     'L0_ffn_q_b': (0.0, 0.8),
     'L0_ffn_k_b': (0.0, 0.8),
     'L0_ffn_v_b': (0.0, 0.8),
     'L0_ffn_o_b': (0.0, 0.522),
     'L0_ffn_router_b': (0.0, 0.587),
     'L0_ffn_b1': (0.0, 0.8),
     'L0_ffn_b2': (0.0, 0.677),
     'L1_ffn_gate_bias': (0.0, 0.1)}
    factors = {'L0_attn_Wq': 8.0,
     'L0_attn_Wk': 8.0,
     'L0_attn_Wv': 5.191,
     'L0_attn_Wo': 5.249,
     'L0_ffn_q_w': 8.0,
     'L0_ffn_k_w': 8.0,
     'L0_ffn_v_w': 8.0,
     'L0_ffn_o_w': 8.0,
     'L0_ffn_router_w': 5.117,
     'L0_ffn_w1': 8.0,
     'L0_ffn_w2': 8.0}
    for name, (base, spread) in spreads.items():
        noise = np.random.default_rng([zlib.crc32(name.encode()), seed]).standard_normal(out[name].shape)
        drawn = base * np.exp(spread * noise) if base else spread * noise
        out[name] = jnp.asarray(drawn.astype(out[name].dtype))
    for name, factor in factors.items():
        out[name] = (out[name] * factor).astype(out[name].dtype)
    return out
```

```python
import numpy as np
import concourse.bass as bass
from concourse import mybir
from contextlib import ExitStack

FP32 = mybir.dt.float32
BF16 = mybir.dt.bfloat16
I32 = mybir.dt.int32
ALU = mybir.AluOpType
ACT = mybir.ActivationFunctionType
AX = mybir.AxisListType

P = 128
BATCHES, SEQ, DIM = 4, 1024, 128
TOKENS = BATCHES * SEQ
TILES = TOKENS // P
CT = 4
CHUNK = CT * P
CHUNKS = TOKENS // CHUNK
KT = SEQ // P
HEADS = 16
QH = 4
QUADS = HEADS // QH * BATCHES
EPS = 1e-5
RANGE = 58.0
TERMS = 8
Q_PARTS = (0, 0, 0, 1, 1, 2)
K_PARTS = (0, 1, 2, 0, 1, 0)
MASKED = -1e30
RING = 4


class Attn:

    def __init__(self, hd, scale, causal, biased):
        self.hd, self.scale, self.causal, self.biased = hd, scale, causal, biased
        self.M = HEADS * hd
        self.slots = QH * hd * TERMS // P
        self.hps = QH // self.slots
        self.units = []
        for half in range(2):
            for kt in range(KT):
                off = max(0, kt * P - half * CHUNK) if causal else 0
                if off < CHUNK:
                    self.units.append((half, kt, off, CHUNK - off, causal and kt * P >= half * CHUNK))
        self.U = len(self.units)
        self.E = 2 * self.U
        self.half_end = [sum(u[0] == 0 for u in self.units), self.U]
        self.last_kt = [max(u[1] for u in self.units if u[0] == h) for h in range(2)]
        self.period = -(-(self.E + 1) // 3) * 3

    def slot_of(self, k):
        return k % 3


LAYERS = [Attn(4, float(8) ** -0.5, False, False), Attn(4, 0.5, False, True),
          Attn(8, float(8) ** -0.5 / 128.0, True, False)]

E0, F0 = 8, 2048
NF0 = F0 // P + 1
E1, I1, SH1 = 16, 176, 352
F1 = E1 * I1 + SH1
NF1 = -(-F1 // P)
ONES_ROW = 96


def by_chunks(eng, front, back):
    front(0, 0)
    with eng.Fori(0, CHUNKS // 2 - 1) as i:
        for s in range(2):
            front(i * 2 + (s + 1), 1 - s)
            back(i * 2 + s, s)
    front(CHUNKS - 1, 1)
    back(CHUNKS - 2, 0)
    back(CHUNKS - 1, 1)


def build_program(nc, t_in, out):
    ctx = ExitStack()
    with ctx:
        def sb(name, shape, dt=FP32):
            return ctx.enter_context(nc.sbuf_tensor(name, shape, dt))

        def sem(name):
            return ctx.enter_context(nc.semaphore(name))

        X = sb("X", [P, TILES, DIM])
        AO = sb("AO", [P, TILES, DIM])
        KG = [sb(f"KG{s}", [P, QH, SEQ], BF16) for s in range(2)]
        QG = [sb(f"QG{s}", [P, 2, SEQ], BF16) for s in range(2)]
        VG = [sb(f"VG{s}", [P, KT, QH, 32]) for s in range(2)]
        VT = sb("VT", [P, TILES, DIM])
        PR = sb("PR", [P, RING, QH, CHUNK])
        OSB = sb("OSB", [P, SEQ])
        XN = sb("XN", [P, 2, CT, DIM])
        XT = sb("XT", [P, 2, CHUNK])
        MTS = sb("MTS", [P, 2, CHUNK])
        EPSB = sb("EPSB", [P, 1])
        NB = sb("NB", [64, CHUNKS])
        NBM = sb("NBM", [64, 1])
        NBR = sb("NBR", [1, 64])
        NBP = sb("NBP", [1, 32])
        NBX = sb("NBX", [1, 1])
        FLAG = sb("FLAG", [1, len(LAYERS)], I32)
        ST = [sb(f"ST{k}", [P, TILES, 6]) for k in range(2)]
        MEAN = [sb(f"MEAN{k}", [P, TILES]) for k in range(2)]
        RSTD = [sb(f"RSTD{k}", [P, TILES]) for k in range(2)]
        TMP = [sb(f"TMP{k}", [P, TILES]) for k in range(4)]
        RC = sb("RC", [P, KT, QH])
        MX = sb("MX", [P, KT, QH])
        MXP = sb("MXP", [P, KT, QH], BF16)
        SHF = sb("SHF", [P, 2, KT, 16, TERMS], BF16)
        LG = sb("LG", [P, TILES, E1])
        WR = sb("WR", [P, TILES, E1])
        SC = sb("SC", [P, TILES, E1])
        RK = sb("RK", [P, TILES, E1])
        G4 = [sb(f"G4{k}", [P, TILES, 4]) for k in range(3)]
        T1 = sb("T1", [P, TILES])
        T2 = sb("T2", [P, TILES])
        YN = sb("YN", [P, CT, DIM])
        flat = PR[:, :, :, :].rearrange("p a b c -> p (a b c)")
        MT = flat[:, 0:TOKENS]
        WT = flat[:, TOKENS:TOKENS + TOKENS // 2].bitcast(BF16)
        HB = flat[:, 6144:8192].rearrange("p (a n) -> p a n", a=4)
        WP = HB[0:E1, 0, :]
        WPB = HB[0:E1, 1, :].bitcast(BF16).rearrange("p (a n) -> p a n", a=2)
        OT = OSB[:, 0:CHUNK]
        QKF = flat[:, 0:2048].rearrange("p (s a n) -> p s a n", s=2, a=2)
        SQ = flat[:, 2048:3072].bitcast(BF16).rearrange("p (s a n) -> p s a n", s=2, a=2)
        PT = flat[:, 3072:6144].bitcast(BF16).rearrange("p (s t a n) -> p s t a n", s=2, t=3, a=2)
        aof = AO[:, :, :].rearrange("p a b -> p (a b)")
        CONST0 = aof[:, 0:TOKENS // 2].bitcast(BF16)
        CONST1 = aof[:, TOKENS // 2:TOKENS].bitcast(BF16)
        RA = VT[:, :, :].rearrange("p a b -> p (a b)")[:, 0:2048]
        PS = ctx.enter_context(nc.psum_tensor("PS", [P, 8, CHUNK], FP32))

        w = {}
        for name, (shape, dt) in {
            "ident": ([P, P], FP32), "identb": ([P, P], BF16), "maskT": ([P, P], BF16), "mask": ([P, P], BF16),
            "blk4": ([P, 32], BF16), "blk8": ([P, 32], BF16), "later": ([P, E1], FP32),
            "wq0": ([P, P], FP32), "wk0": ([P, P], FP32), "wv0": ([P, 64], FP32), "wo0": ([P, P], FP32),
            "bo0": ([P, P], FP32),
            "wq1": ([P, P], FP32), "wk1": ([P, P], FP32), "wv1": ([P, 64], FP32), "qb1": ([P, 1], FP32),
            "kb1": ([P, 1], FP32), "vb1": ([P, 64], FP32), "wo1": ([P, P], FP32), "ob1": ([P, 1], FP32),
            "rw": ([P, E0], FP32), "rb": ([P, E0], FP32), "b1": ([P, NF0 - 1], FP32),
            "wq2": ([P, P], FP32), "wk2": ([P, P], FP32), "wv2": ([P, P], FP32), "wo2": ([P, P], FP32),
            "gw": ([P, E1], FP32), "gb": ([P, E1], FP32),
        }.items():
            w[name] = sb(name, shape, dt)
        n1 = NF1 * P
        MW = sb("MW", [P, 3 * n1 + n1 // 2])
        experts0 = {"w1": MW[:, 0:F0], "w2": MW[:, F0:F0 + NF0 * P].rearrange("p (j n) -> p j n", j=NF0),
                    "sel0": MW[:, F0 + NF0 * P:F0 + NF0 * P + NF0 * P // 2].bitcast(BF16)}
        experts1 = {"gp": MW[:, 0:n1], "up": MW[:, n1:2 * n1],
                    "dp": MW[:, 2 * n1:3 * n1].rearrange("p (j n) -> p j n", j=NF1),
                    "sel1": MW[:, 3 * n1:].bitcast(BF16)}
        QD = nc.dram_tensor("q_rows", [P, TERMS, TOKENS], BF16, kind="Internal").ap()
        KD = nc.dram_tensor("k_rows", [P, TERMS, TOKENS], BF16, kind="Internal").ap()
        QDR = QD.rearrange("r t n -> (r t) n")
        KDR = KD.rearrange("r t n -> (r t) n")

        x_in = sem("x_in")
        w_in = sem("w_in")
        e0_in, e1_in = sem("e0_in"), sem("e1_in")
        consts_set = sem("consts_set")
        consts_out = sem("consts_out")
        stats = sem("stats")
        roots = sem("roots")
        dv = sem("dv")
        out_done = sem("out_done")
        flag_col, flag_row, flag_set = sem("flag_col"), sem("flag_row"), sem("flag_set")

        def many(prefix, names):
            return {n: sem(f"{prefix}_{n}") for n in names.split()}

        pj = [many(f"pj{a}", "xn tr xt qk qkv ev vev nrm nb split w0 w1") for a in range(3)]
        at = [many(f"at{a}", "s exp pv qg0 qg1 v oev t tr mxr mxd sh sht shd mxs") for a in range(3)]
        po = [many(f"po{a}", names) for a, names in enumerate(
            ("xn tr xt m yd", "xn tr xt m mt mtc y yd", "xn tr xt m yd", "xn tr mt mtc y yd"))]
        cleared = sem("cleared")
        rt = [many(f"rt{a}", "lg e w wt wtd") for a in range(2)]
        mo = [many(f"mo{a}", "g a h dn oe yt yd") for a in range(2)]
        post = [sem(f"post{a}") for a in range(4)]
        block = ctx.enter_context(nc.Block())

        @block.sync
        def _(sp):
            x_v = t_in["x"].rearrange("(t p) c -> p t c", p=P)
            for b in range(BATCHES):
                sp.dma_start(X[:, b * KT:(b + 1) * KT, :], x_v[:, b * KT:(b + 1) * KT, :]).then_inc(x_in, 16)
            order = ["ident", "wq0", "wk0", "wv0", "identb", "blk4"]
            order += [n for n in w if n not in order]
            for name in order:
                t = w[name]
                sp.dma_start(t[tuple(slice(None) for _ in t.shape)], t_in[name]).then_inc(w_in, 16)
            for name, t in experts0.items():
                sp.dma_start(t, t_in[name]).then_inc(e0_in, 16)
            sp.wait_ge(consts_set, 3)
            for t in (6, 7):
                sp.dma_start(QD[:, t, :], CONST0).then_inc(consts_out, 16)
                sp.dma_start(KD[:, t, :], CONST1).then_inc(consts_out, 16)
            for a, L in enumerate(LAYERS):
                S, T = pj[a], at[a]
                for s in range(2):
                    sp.nop().then_inc(S[f"w{s}"], 16)
                if a:
                    for s in range(2):
                        sp.wait_ge(at[a - 1][f"qg{s}"], 16 * (QUADS // 2) * (LAYERS[a - 1].slots + QH))
                with sp.Fori(0, CHUNKS // 2) as i:
                    for s in range(2):
                        c = i * 2 + s
                        sp.wait_ge(S["split"], c + 3)
                        col = bass.ds(c * CHUNK, CHUNK)
                        for t, part in enumerate(Q_PARTS):
                            sp.dma_start(QD[0:L.M, t, col], PT[0:L.M, s, part, 0, :]).then_inc(S[f"w{s}"], 16)
                        for t0, n in ((0, 3), (3, 2), (5, 1)):
                            sp.dma_start(KD[0:L.M, t0:t0 + n, col], PT[0:L.M, s, 0:n, 1, :]).then_inc(S[f"w{s}"], 16)
                if a == 2:
                    sp.wait_ge(mo[0]["yd"], CHUNKS + 1)
                    for name, t in experts1.items():
                        sp.dma_start(t, t_in[name]).then_inc(e1_in, 16)
                for s in range(2):
                    sp.wait_ge(S[f"w{s}"], 16 + 9 * 16 * CHUNKS // 2)
                if a == 0:
                    sp.wait_ge(consts_out, 64)
                sp.wait_ge(consts_set, 3 + (1 if a < 2 else 2))
                rows = L.hd * TERMS
                with sp.Fori(0, BATCHES) as b:
                    with sp.Fori(0, 2) as p:
                        for s in range(2):
                            quad = p * 2 + s
                            sp.wait_ge(T["s"], (b * 4 + quad) * L.E + 1)
                            col = bass.ds(b * SEQ, SEQ)
                            for k in range(L.slots):
                                sp.dma_start(QG[s][:, k, :], QDR[bass.ds((quad * L.slots + k) * P, P), col])\
                                  .then_inc(T[f"qg{s}"], 16)
                            for h in range(QH):
                                r0 = (h % L.hps) * rows
                                sp.dma_start(KG[s][r0:r0 + rows, h, :],
                                             KDR[bass.ds(quad * QH * rows + h * rows, rows), col])\
                                  .then_inc(T[f"qg{s}"], 16)
            o_v = out.rearrange("(t p) c -> p t c", p=P)
            for c in range(CHUNKS):
                sp.wait_ge(post[3], c + 1)
                sp.dma_start(o_v[:, c * CT:(c + 1) * CT, :], X[:, c * CT:(c + 1) * CT, :]).then_inc(out_done, 16)
            sp.wait_ge(out_done, 16 * CHUNKS)

        @block.gpsimd
        def _(pool):
            pool.memset(CONST0, 0.0)
            pool.memset(CONST1, 1.0).then_inc(consts_set, 3)
            for s in range(2):
                pool.memset(KG[s][:, :, :], 0.0)
                pool.memset(VG[s][:, :, :, :], 0.0).then_inc(cleared, 1)
            pool.wait_ge(cleared, 2)
            for s in range(2):
                last = pool.memset(VG[s][:, :, :, 4:5], 1.0)
            last.then_inc(consts_set, 1)
            for a, L in enumerate(LAYERS):
                S, T = pj[a], at[a]
                if a == 2:
                    pool.wait_ge(at[1]["s"], (1 + QUADS) * LAYERS[1].E + 1)
                    pool.wait_ge(at[1]["pv"], (1 + QUADS) * LAYERS[1].U + 1)
                    for s in range(2):
                        pool.memset(KG[s][:, :, :], 0.0)
                        pool.memset(VG[s][:, :, :, :], 0.0).then_inc(cleared, 1)
                    pool.wait_ge(cleared, 4)
                    for s in range(2):
                        last = pool.memset(VG[s][:, :, :, 8:9], 1.0)
                    last.then_inc(consts_set, 1)
                pool.wait_ge(S["vev"], 2 + CHUNKS)
                with pool.Fori(0, BATCHES) as b:
                    with pool.Fori(0, 2) as p:
                        for s in range(2):
                            quad = p * 2 + s
                            pool.wait_ge(T["pv"], (b * 4 + quad) * L.U + 1)
                            src = VT[:, bass.ds(b * KT, KT), bass.ds(quad * QH * L.hd, QH * L.hd)]
                            pool.tensor_copy(VG[s][:, :, :, 0:L.hd],
                                             src.rearrange("p t (h d) -> p t h d", h=QH)).then_inc(T["v"], 1)
                S = po[a]
                pool.wait_ge(T["tr"], QUADS + 1)
                if L.M < P:
                    pool.memset(XN[:, :, :, L.M:P], 0.0)
                if a == 1:
                    pool.nop().then_inc(S["mtc"], 2)

                def front(c, s):
                    pool.wait_ge(S["tr"], c + 1)
                    pool.tensor_copy(XN[:, s, :, 0:L.M], AO[:, bass.ds(c * CT, CT), 0:L.M]).then_inc(S["xn"], 1)

                def back(c, s):
                    if a == 1:
                        pool.wait_ge(S["mt"], c + 3)
                        pool.tensor_copy(MT[:, bass.ds(c * CHUNK, CHUNK)], MTS[:, s, :]).then_inc(S["mtc"], 1)

                by_chunks(pool, front, back)
            S = po[3]
            pool.nop().then_inc(S["mtc"], 2)
            with pool.Fori(0, CHUNKS // 2) as i:
                for s in range(2):
                    c = i * 2 + s
                    pool.wait_ge(S["mt"], c + 3)
                    pool.tensor_copy(MT[:, bass.ds(c * CHUNK, CHUNK)], MTS[:, s, :]).then_inc(S["mtc"], 1)

        @block.scalar
        def _(act):
            n_roots = [0]

            def credit(s, n):
                act.nop().then_inc(s, n)

            def root(k):
                n_roots[0] += 1
                act.wait_ge(stats, n_roots[0])
                act.activation(TMP[3][:, :], TMP[2][:, :], ACT.Sqrt, bias=EPSB[:, 0:1], scale=1.0 / DIM).then_inc(roots, 1)

            def project(a):
                L, S = LAYERS[a], pj[a]
                credit(S["ev"], 2)

                def front(c, s):
                    act.wait_ge(S["tr"], c + 3)
                    act.wait_ge(S["qkv"], c + 1)
                    act.activation(XT[:, s, :], PS[:, 4 * s, :], ACT.Copy).then_inc(S["xt"], 1)

                def back(c, s):
                    act.wait_ge(S["qk"], c + 1)
                    act.wait_ge(S["split"], c + 1)
                    act.wait_ge(S["nrm"], c + 1)
                    for n, bias in enumerate(("qb1", "kb1")):
                        b = w[bias][:, 0:1] if L.biased else 0.0
                        act.activation(QKF[:, s, n, :], PS[:, 4 * s + 1 + n, :], ACT.Identity, bias=b)
                        last = act.activation(SQ[:, s, n, :], PS[:, 4 * s + 1 + n, :], ACT.Square, bias=b)
                    last.then_inc(S["ev"], 1)

                by_chunks(act, front, back)

            def softmax(a):
                L, T = LAYERS[a], at[a]
                credit(T["exp"], L.E)
                with act.Fori(0, QUADS) as n:
                    for u, (half, kt, off, width, diag) in enumerate(L.units):
                        for g in range(2):
                            e = 2 * u + g
                            act.wait_ge(T["s"], n * L.E + (e + 2 + L.E))
                            if g == 0:
                                act.wait_ge(T["pv"], n * L.U + (u + 2 - RING + L.U))
                            slot = ((e - 4) % L.E) % 3
                            act.activation(PR[:, u % RING, 2 * g:2 * g + 2, off:off + width],
                                           PS[:, 2 * slot:2 * slot + 2, off:off + width],
                                           ACT.Exp, scale=L.scale).then_inc(T["exp"], 1)

            def after_attention(a):
                S = po[a]
                for name in ("xt", "mt"):
                    if name in S:
                        credit(S[name], 2)
                with act.Fori(0, CHUNKS // 2) as i:
                    for s in range(2):
                        c = i * 2 + s
                        act.wait_ge(S["tr"], c + 3)
                        if a == 3:
                            act.wait_ge(S["y"], c + 1)
                            act.wait_ge(S["mtc"], c + 1)
                            act.activation(MTS[:, s, :], PS[:, 3 * s, :], ACT.Copy).then_inc(S["mt"], 1)
                            continue
                        act.wait_ge(S["m"], c + 1)
                        act.activation(XT[:, s, :], PS[:, 3 * s, :], ACT.Copy).then_inc(S["xt"], 1)
                        if a == 1:
                            act.wait_ge(S["m"], c + 3)
                            act.wait_ge(S["y"], c + 1)
                            act.wait_ge(S["mtc"], c + 1)
                            act.activation(MTS[:, s, :], PS[:, 3 * s + 1, :], ACT.Identity, bias=w["ob1"][:, 0:1])\
                               .then_inc(S["mt"], 1)

            def experts(m):
                S, NF = mo[m], (NF0, NF1)[m]
                credit(S["oe"], 1)
                with act.Fori(0, CHUNKS) as c:
                    for j in range(NF):
                        bank = 3 * (j % 2)
                        if m == 0 and j == NF - 1:
                            continue
                        act.wait_ge(S["g"], c * NF + (j + 1))
                        act.wait_ge(S["dn"], c * NF + (1 + max(0, j - 3)))
                        if m == 0:
                            act.activation(HB[:, j % 4, :], PS[:, bank, :], ACT.Gelu, bias=w["b1"][:, j:j + 1])\
                               .then_inc(S["a"], 1)
                        else:
                            act.activation(HB[:, j % 4, :], PS[:, bank, :], ACT.Silu).then_inc(S["a"], 1)
                    act.wait_ge(S["dn"], c * NF + (NF + 1))
                    act.wait_ge(S["yt"], c + 1)
                    act.activation(OT, PS[:, 6, :], ACT.Copy).then_inc(S["oe"], 1)

            act.wait_ge(dv, 1)
            act.wait_ge(w_in, 16 * len(w))
            root(0)
            project(0)
            softmax(0)
            after_attention(0)
            root(1)
            root(0)
            project(1)
            softmax(1)
            after_attention(1)
            act.wait_ge(rt[0]["lg"], CHUNKS + 1)
            act.activation(SC[:, :, 0:E0], LG[:, :, 0:E0], ACT.Exp).then_inc(rt[0]["e"], 1)
            experts(0)
            root(1)
            root(0)
            project(2)
            softmax(2)
            after_attention(2)
            root(1)
            root(0)
            after_attention(3)
            act.wait_ge(rt[1]["lg"], CHUNKS)
            act.activation(SC[:, :, :], LG[:, :, :], ACT.Sigmoid).then_inc(rt[1]["e"], 1)
            experts(1)
            root(1)

        @block.tensor
        def _(pe):
            def credit(s, n):
                pe.nop().then_inc(s, n)

            def transposes(dst_bank, s):
                for k in range(CT):
                    last = pe.transpose(PS[:, dst_bank, k * P:(k + 1) * P], XN[:, s, k, :], w["ident"][:, :])
                return last

            def project(a):
                L, S = LAYERS[a], pj[a]
                for name in ("tr", "qkv", "nrm"):
                    credit(S[name], 2)
                blk = w["blk4"] if L.hd == 4 else w["blk8"]

                def front(c, s):
                    pe.wait_ge(S["xn"], c + 1)
                    pe.wait_ge(S["nb"], c + 1)
                    transposes(4 * s, s).then_inc(S["tr"], 1)

                def back(c, s):
                    pe.wait_ge(S["xt"], c + 1)
                    pe.wait_ge(S["ev"], c + 1)
                    x_t = XT[:, s, :]
                    pe.matmul(PS[:, 4 * s + 1, :], w[f"wq{a}"][:, :], x_t, start=True, stop=True)
                    pe.matmul(PS[:, 4 * s + 2, :], w[f"wk{a}"][:, :], x_t, start=True, stop=True)\
                      .then_inc(S["qk"], 1)
                    pe.wait_ge(S["vev"], c + 1)
                    for k in range(CT):
                        last = pe.matmul(PS[:, 4 * s + 3, k * L.M:(k + 1) * L.M],
                                         XT[:, s, k * P:(k + 1) * P], w[f"wv{a}"][:, :],
                                         start=True, stop=True)
                    last.then_inc(S["qkv"], 1)
                    pe.wait_ge(S["ev"], c + 3)
                    for n in range(2):
                        last = pe.matmul(PS[32 * n:32 * n + 32, 4 * s, :], blk[:, :], SQ[:, s, n, :],
                                         start=True, stop=True)
                    last.then_inc(S["nrm"], 1)

                by_chunks(pe, front, back)
                pe.wait_ge(flag_col, a + 1)
                pe.transpose(PS[0:1, 0, 0:64], NBM[:, :], w["ident"][0:64, 0:64]).then_inc(flag_row, 1)
                pe.wait_ge(S["ev"], CHUNKS + 2)
                pe.wait_ge(S["vev"], CHUNKS + 2)
                pe.wait_ge(S["nb"], CHUNKS + 2)

            def attention(a):
                L, T = LAYERS[a], at[a]
                credit(T["pv"], L.U + 1)
                credit(T["sht"], 1)
                credit(T["s"], L.E + 1)
                pe.wait_ge(flag_set, a + 1)
                flag = pe.value_load(FLAG[0:1, a:a + 1], min_val=0, max_val=1)

                def exp_done(n, k):
                    pe.wait_ge(T["exp"], n * L.E + (4 + k + 1 + L.E))

                def free_slot(n, k, first):
                    if k >= 3:
                        return exp_done(n, k - 3)
                    j = k - 3 + L.period
                    while j > L.E:
                        j -= 3
                    if j == L.E:
                        pe.wait_ge(T["tr"], n + 1)
                        j -= 3
                    pe.wait_ge(T["exp"], n * L.E + (4 + j + 1))

                def maxima(n, s):
                    with pe.If(flag > 0):
                        pe.wait_ge(T["exp"], n * L.E + L.E)
                        for h in range(QH):
                            for qc in range(KT):
                                r = h * KT + qc
                                b0 = 2 * (r % 3)
                                if r >= 3:
                                    pe.wait_ge(T["mxd"], n * (QH * KT) + (r - 2))
                                keys = (qc + 1) * P if L.causal else SEQ
                                for k0 in range(0, keys, CHUNK):
                                    width = min(CHUNK, keys - k0)
                                    diag = L.causal and k0 + width == keys
                                    bank, queries = b0 + k0 // CHUNK, QG[s][:, h // L.hps, qc * P:(qc + 1) * P]
                                    plain = width - P if diag else width
                                    if plain:
                                        last = pe.matmul(PS[:, bank, 0:plain], queries, KG[s][:, h, k0:k0 + plain],
                                                         start=True, stop=True)
                                    if diag:
                                        pe.matmul(PS[:, bank, plain:width], queries, KG[s][:, h, k0 + plain:k0 + width],
                                                  start=True, stop=False)
                                        last = pe.matmul(PS[:, bank, plain:width], w["identb"][:, :], w["mask"][:, :],
                                                         start=False, stop=True)
                                last.then_inc(T["mxr"], 1)
                        pe.wait_ge(T["sh"], n + 1)
                        for k in range(L.slots):
                            sh = PS[:, 2 * k, :].bitcast(BF16)
                            for qc in range(KT):
                                last = pe.transpose(sh[:, qc * P:(qc + 1) * P],
                                                    SHF[:, k, qc, :, :].rearrange("p r t -> p (r t)"),
                                                    w["identb"][:, :])
                        last.then_inc(T["sht"], 1)
                        pe.wait_ge(T["shd"], n + 1)

                def scores(n, s, u):
                    half, kt, off, width, diag = L.units[u]
                    q0 = half * CHUNK + off
                    for h in range(QH):
                        e = 2 * u + h // 2
                        slot = ((e - 4) % L.E) % 3
                        yield h, e
                        bank, keys, queries = 2 * slot + h % 2, KG[s][:, h, kt * P:(kt + 1) * P], QG[s][:, h // L.hps, :]
                        if diag:
                            pe.matmul(PS[:, bank, off:off + P], keys, queries[:, q0:q0 + P], start=True, stop=False)
                            last = pe.matmul(PS[:, bank, off:off + P], w["identb"][:, :], w["maskT"][:, :],
                                             start=False, stop=True)
                            off_, q_ = off + P, q0 + P
                        else:
                            off_, q_ = off, q0
                        if off_ < CHUNK:
                            last = pe.matmul(PS[:, bank, off_:CHUNK], keys, queries[:, q_:(half + 1) * CHUNK],
                                             start=True, stop=True)
                        if h % 2:
                            last.then_inc(T["s"], 1)

                def products(n, s, u):
                    half, kt, off, width, diag = L.units[u]
                    pe.wait_ge(T["exp"], n * L.E + (2 * u + 2 + L.E))
                    for h in range(QH):
                        last = pe.matmul(PS[32 * h:32 * h + 32, 6 + half, off:CHUNK], VG[s][:, kt, h, :],
                                         PR[:, u % RING, h, off:CHUNK], start=(kt == 0), stop=(kt == L.last_kt[half]),
                                         skip_group_check=True, tile_position=(0, 32 * h))
                    last.then_inc(T["pv"], 1)

                def quad(n, s, final):
                    pe.wait_ge(T["v"], n + 1)
                    for u in range(L.U):
                        products(n, s, u)
                        nxt = u + 2 >= L.U
                        if nxt and final:
                            continue
                        if u + 2 == L.U:
                            pe.wait_ge(T[f"qg{1 - s}"], loads(n, 1 - s))
                            maxima(n + 1, 1 - s)
                        for h, e in scores(n, 1 - s if nxt else s, (u + 2) % L.U):
                            if h % 2 == 0:
                                free_slot(n, 2 * u + h // 2, False)
                    exp_done(n, L.E - 3) if not final else pe.wait_ge(T["exp"], n * L.E + (L.E + L.E))
                    pe.wait_ge(T["oev"], n * 2 + 2)
                    b0 = 2 * (L.E % 3)
                    for k in range(KT):
                        last = pe.transpose(PS[:, b0 + k // 4, (k % 4) * P:(k % 4 + 1) * P], OSB[:, k * P:(k + 1) * P],
                                            w["ident"][:, :])
                    last.then_inc(T["t"], 1)

                per = 16 * (L.slots + QH)
                pe.wait_ge(T["qg0"], per)
                maxima(0, 0)
                for u in range(2):
                    for h, e in scores(0, 0, u):
                        if e == 3 and h % 2 == 0:
                            pe.wait_ge(T["exp"], 1 + L.E)
                with pe.Fori(0, QUADS // 2 - 1) as i:
                    for s in range(2):
                        def loads(n, s_next, i=i):
                            return (i + (1 if s_next else 2)) * per
                        quad(i * 2 + s, s, False)
                i = QUADS // 2 - 1

                def loads(n, s_next):
                    return (QUADS // 2) * per
                quad(QUADS - 2, 0, False)
                quad(QUADS - 1, 1, True)
                pe.wait_ge(T["tr"], QUADS + 1)

            def output(a):
                L, S = LAYERS[a], po[a]
                credit(S["tr"], 2)
                credit(S["m"], 2)

                def front(c, s):
                    pe.wait_ge(S["xn"], c + 1)
                    pe.wait_ge(S["xt"], c + 1)
                    transposes(3 * s, s).then_inc(S["tr"], 1)

                def back(c, s):
                    pe.wait_ge(S["xt"], c + 3)
                    pe.wait_ge(S["yd"], c + 1)
                    for k in range(CT):
                        last = pe.matmul(PS[:, 3 * s + 1, k * P:(k + 1) * P], XT[:, s, k * P:(k + 1) * P],
                                         w[f"wo{a}"][:, :], start=True, stop=True)
                    last.then_inc(S["m"], 1)

                by_chunks(pe, front, back)
                pe.wait_ge(S["yd"], CHUNKS + 2)

            def routed_input(a):
                S = po[a]
                credit(S["tr"], 2)
                if a == 1:
                    credit(S["m"], 2)
                credit(S["y"], 2)
                E, rw = (E0, w["rw"]) if a == 1 else (E1, w["gw"])

                def front(c, s):
                    pe.wait_ge(S["xn"], c + 1)
                    pe.wait_ge(S["mt"], c + 1)
                    transposes(3 * s, s).then_inc(S["tr"], 1)
                    if a == 1:
                        pe.wait_ge(S["xt"], c + 3)
                        pe.matmul(PS[:, 3 * s + 1, :], w["wo1"][:, :], XT[:, s, :],
                                  start=True, stop=True).then_inc(S["m"], 1)

                def back(c, s):
                    pe.wait_ge(S["mt"], c + 3)
                    pe.wait_ge(S["yd"], c + 1)
                    for k in range(CT):
                        last = pe.matmul(PS[:, 3 * s + 2, k * E:(k + 1) * E], MTS[:, s, k * P:(k + 1) * P],
                                         rw[:, :], start=True, stop=True)
                    last.then_inc(S["y"], 1)

                by_chunks(pe, front, back)
                pe.wait_ge(S["yd"], CHUNKS + 2)

            def weights(m):
                S, E = rt[m], (E0, E1)[m]
                pe.wait_ge(S["w"], 1)
                for c in range(CHUNKS):
                    for k in range(CT):
                        last = pe.transpose(PS[0:E, c, k * P:(k + 1) * P], WR[:, c * CT + k, 0:E], w["ident"][:, :])
                    last.then_inc(S["wt"], 1)
                pe.wait_ge(S["wtd"], CHUNKS)

            def experts(m):
                S, NF = mo[m], (NF0, NF1)[m]
                sel = experts0["sel0"] if m == 0 else experts1["sel1"]
                down = experts0["w2"] if m == 0 else experts1["dp"]
                credit(S["dn"], 1)
                credit(S["yt"], 1)
                pe.wait_ge(po[3 if m else 1]["mtc"], 2 + CHUNKS)
                pe.wait_ge(e1_in if m else e0_in, 16 * len(experts1 if m else experts0))

                def rows_of(j):
                    return P if m == 0 or j < NF - 1 else F1 - (NF - 1) * P

                def down_product(c, j):
                    pe.wait_ge(S["h"], c * NF + (j + 2))
                    if j == 0:
                        pe.wait_ge(S["oe"], c + 1)
                    pe.matmul(PS[:, 6, :], down[:, j, :], HB[:, j % 4, :],
                              start=(j == 0), stop=(j == NF - 1)).then_inc(S["dn"], 1)

                with pe.Fori(0, CHUNKS) as c:
                    x_t = MT[:, bass.ds(c * CHUNK, CHUNK)]
                    w_t = WT[:, bass.ds(c * CHUNK, CHUNK)]
                    for j in range(NF):
                        bank = 3 * (j % 2)
                        pe.wait_ge(S["h"], c * NF + (1 + max(0, j - 1)))
                        col = slice(j * P, (j + 1) * P)
                        if m == 1:
                            pe.matmul(PS[:, bank, :], experts1["gp"][:, col], x_t, start=True, stop=True)
                            pe.matmul(PS[:, bank + 1, :], experts1["up"][:, col], x_t, start=True, stop=True)
                        elif j < NF - 1:
                            pe.matmul(PS[:, bank, :], experts0["w1"][:, col], x_t, start=True, stop=True)
                        pe.matmul(PS[:, bank + 2, :], sel[:, col], w_t, start=True, stop=True).then_inc(S["g"], 1)
                        if j:
                            down_product(c, j - 1)
                    down_product(c, NF - 1)
                    pe.wait_ge(S["oe"], c + 2)
                    pe.wait_ge(S["yd"], c + 1)
                    for k in range(CT):
                        last = pe.transpose(PS[:, 7, k * P:(k + 1) * P], OT[:, k * P:(k + 1) * P], w["ident"][:, :])
                    last.then_inc(S["yt"], 1)
                pe.wait_ge(S["yd"], CHUNKS + 1)

            pe.wait_ge(w_in, 16 * len(w))
            project(0)
            attention(0)
            output(0)
            project(1)
            attention(1)
            routed_input(1)
            weights(0)
            experts(0)
            project(2)
            attention(2)
            output(2)
            routed_input(3)
            weights(1)
            experts(1)

        @block.vector
        def _(v):
            n_dv = [0]

            def credit(s, n):
                v.nop().then_inc(s, n)

            def step(ins, at_=None):
                n_dv[0] += 1
                ins.then_inc(dv, 1)
                v.wait_ge(dv, n_dv[0])

            n_root = [0]

            def finish_stats(k):
                st = ST[k]
                step(v.tensor_tensor(TMP[0][:, :], st[:, :, 1], st[:, :, 4], ALU.add))
                step(v.tensor_tensor(TMP[1][:, :], st[:, :, 1], st[:, :, 4], ALU.subtract))
                step(v.tensor_tensor(TMP[1][:, :], TMP[1][:, :], TMP[1][:, :], ALU.mult))
                step(v.tensor_tensor(TMP[2][:, :], st[:, :, 2], st[:, :, 5], ALU.add))
                step(v.tensor_scalar(MEAN[k][:, :], TMP[0][:, :], 0.5, None, ALU.mult))
                v.scalar_tensor_tensor(TMP[2][:, :], TMP[1][:, :], DIM / 4.0, TMP[2][:, :], ALU.mult, ALU.add)\
                 .then_inc(stats, 1)
                n_root[0] += 1
                v.wait_ge(roots, n_root[0])
                step(v.reciprocal(RSTD[k][:, :], TMP[3][:, :]))

            def loop_steps(per, count):
                base = n_dv[0]
                n_dv[0] += per * count
                return base

            def normalise(dst, src, k, t0):
                for q in range(CT):
                    last = v.tensor_scalar(dst(q), src[:, bass.ds(t0 + q, 1), :].rearrange("p a c -> p (a c)"),
                                           MEAN[k][:, bass.ds(t0 + q, 1)], RSTD[k][:, bass.ds(t0 + q, 1)],
                                           ALU.subtract, ALU.mult)
                return last

            def chunk_stats(src, k, t0):
                for q in range(CT):
                    last = v.bn_stats(ST[k][:, bass.ds(t0 + q, 1), :].rearrange("p a c -> p (a c)"),
                                      src[:, bass.ds(t0 + q, 1), :].rearrange("p a c -> p (a c)"))
                return last

            def project(a):
                L, S = LAYERS[a], pj[a]
                for name in ("nb", "vev", "split"):
                    credit(S[name], 2)
                base = loop_steps(3, CHUNKS)

                def front(c, s):
                    v.wait_ge(S["tr"], c + 1)
                    normalise(lambda q: XN[:, s, q, :], X, 0, c * CT).then_inc(S["xn"], 1)

                def back(c, s):
                    v.wait_ge(S["ev"], c + 3)
                    v.wait_ge(S[f"w{s}"], (c - s) * (9 * 8) + 16)
                    f = QKF[:, s, :, :]
                    pt = [PT[:, s, part, :, :] for part in range(3)]
                    v.tensor_copy(pt[0], f).then_inc(dv, 1)
                    v.wait_ge(dv, c * 3 + (base + 1))
                    v.tensor_tensor(f, f, pt[0], ALU.subtract).then_inc(dv, 1)
                    v.wait_ge(dv, c * 3 + (base + 2))
                    v.tensor_copy(pt[1], f).then_inc(dv, 1)
                    v.wait_ge(dv, c * 3 + (base + 3))
                    v.tensor_tensor(pt[2], f, pt[1], ALU.subtract).then_inc(S["split"], 1)
                    v.wait_ge(S["qkv"], c + 3)
                    src = PS[:, 4 * s + 3, 0:CT * L.M].rearrange("p (t m) -> p t m", t=CT)
                    dst = VT[:, bass.ds(c * CT, CT), 0:L.M]
                    if L.biased:
                        ins = v.tensor_tensor(dst, src, w["vb1"][:, :].unsqueeze(1).broadcast_to([P, CT, L.M]), ALU.add)
                    else:
                        ins = v.tensor_copy(dst, src)
                    ins.then_inc(S["vev"], 1)
                    v.wait_ge(S["nrm"], c + 3)
                    v.tensor_reduce(NB[:, bass.ds(c, 1)], PS[0:64, 4 * s, :], AX.X, ALU.max).then_inc(S["nb"], 1)

                by_chunks(v, front, back)
                v.wait_ge(S["nb"], CHUNKS + 2)
                v.tensor_reduce(NBM[:, :], NB[:, :], AX.X, ALU.max).then_inc(flag_col, 1)
                v.wait_ge(flag_row, a + 1)
                step(v.tensor_copy(NBR[:, :], PS[0:1, 0, 0:64]))
                step(v.tensor_tensor(NBP[:, :], NBR[:, 0:32], NBR[:, 32:64], ALU.mult))
                step(v.tensor_reduce(NBX[:, :], NBP[:, :], AX.X, ALU.max))
                v.tensor_scalar(FLAG[:, a:a + 1], NBX[:, :], (RANGE / L.scale) ** 2, None, ALU.is_gt)\
                 .then_inc(flag_set, 1)
                v.wait_ge(flag_set, a + 1)

            def attention(a):
                L, T = LAYERS[a], at[a]
                flag = v.value_load(FLAG[0:1, a:a + 1], min_val=0, max_val=1)
                cols = L.hd
                credit(T["tr"], 1)

                def maxima(n, s):
                    with v.If(flag > 0):
                        for h in range(QH):
                            for qc in range(KT):
                                r = h * KT + qc
                                b0 = 2 * (r % 3)
                                v.wait_ge(T["mxr"], n * (QH * KT) + (r + 1))
                                keys = (qc + 1) * P if L.causal else SEQ
                                src = (PS[:, b0:b0 + 2, :].rearrange("p a b -> p (a b)"))[:, 0:keys]
                                v.tensor_reduce(MX[:, qc, h:h + 1], src, AX.X, ALU.max, negate=True).then_inc(T["mxd"], 1)
                        v.wait_ge(T["mxd"], n * (QH * KT) + QH * KT)
                        v.wait_ge(T["sht"], n + 1)

                        def part(k):
                            return [SHF[:, m, :, k:k + (L.hps - 1) * L.hd + 1:L.hd, 6] for m in range(L.slots)]

                        def heads(t, m):
                            return t[:, :, m * L.hps:(m + 1) * L.hps]

                        for k in range(3):
                            v.tensor_copy(MXP[:, :, :], MX[:, :, :]).then_inc(T["mxs"], 1)
                            v.wait_ge(T["mxs"], n * 6 + (2 * k + 1))
                            for m in range(L.slots):
                                last = v.tensor_copy(part(k)[m], heads(MXP, m))
                            if k < 2:
                                last = v.tensor_tensor(MX[:, :, :], MX[:, :, :], MXP[:, :, :], ALU.subtract)
                            last.then_inc(T["mxs"], 1)
                            v.wait_ge(T["mxs"], n * 6 + (2 * k + 2))
                        v.nop().then_inc(T["sh"], 1)
                        v.wait_ge(T["sht"], n + 2)
                        for m in range(L.slots):
                            last = v.tensor_tensor(QG[s][:, m, :], QG[s][:, m, :], PS[:, 2 * m, :].bitcast(BF16), ALU.add)
                        last.then_inc(T["shd"], 1)

                maxima(0, 0)
                base = loop_steps(1, QUADS)

                def quad(b, q, final):
                    n = b * 4 + q
                    for half in range(2):
                        v.wait_ge(T["pv"], n * L.U + (L.U + 1 + L.half_end[half]))
                        v.tensor_copy(OSB[:, half * CHUNK:(half + 1) * CHUNK], PS[:, 6 + half, :]).then_inc(T["oev"], 1)
                        if half == 0 and not final:
                            maxima(n + 1, (q + 1) % 2)
                    v.wait_ge(T["t"], n + 1)
                    b0 = 2 * (L.E % 3)
                    res = PS[:, b0:b0 + 2, :].rearrange("p a (k h r) -> p (a k) h r", k=4, h=QH)
                    v.reciprocal(RC[:, :, :], res[:, :, :, cols]).then_inc(dv, 1)
                    v.wait_ge(dv, n + (base + 1))
                    dst = AO[:, bass.ds(b * KT, KT), q * QH * L.hd:(q + 1) * QH * L.hd]
                    v.tensor_tensor(dst.rearrange("p t (h d) -> p t h d", h=QH), res[:, :, :, 0:cols],
                                    RC[:, :, :].unsqueeze(3).broadcast_to([P, KT, QH, cols]), ALU.mult)\
                     .then_inc(T["tr"], 1)

                with v.Fori(0, BATCHES - 1) as b:
                    for q in range(4):
                        quad(b, q, False)
                for q in range(4):
                    quad(BATCHES - 1, q, q == 3)

            def output(a):
                S = po[a]
                credit(S["yd"], 2)
                base = loop_steps(2, CHUNKS // 2)
                with v.Fori(0, CHUNKS // 2) as i:
                    for s in range(2):
                        c = i * 2 + s
                        v.wait_ge(S["m"], c + 3)
                        src = PS[:, 3 * s + 1, :].rearrange("p (t m) -> p t m", t=CT)
                        dst = AO[:, bass.ds(c * CT, CT), :]
                        if a == 0:
                            ins = v.tensor_tensor(dst, src, w["bo0"][:, :].unsqueeze(1).broadcast_to([P, CT, P]), ALU.add)
                        else:
                            ins = v.tensor_scalar(dst, src, 1.0 / 128.0, None, ALU.mult)
                        ins.then_inc(dv, 1)
                        v.wait_ge(dv, i * 2 + (base + s + 1))
                        chunk_stats(AO, 1, c * CT).then_inc(S["yd"], 1)
                v.wait_ge(S["yd"], 2 + CHUNKS)

            def residual(a):
                base = loop_steps(4, CHUNKS // 2)
                with v.Fori(0, CHUNKS // 2) as i:
                    for s in range(2):
                        c = i * 2 + s
                        normalise(lambda q: YN[:, q, :], AO, 1, c * CT).then_inc(dv, 1)
                        v.wait_ge(dv, i * 4 + (base + 2 * s + 1))
                        xs = X[:, bass.ds(c * CT, CT), :]
                        v.tensor_tensor(xs, xs, YN[:, :, :], ALU.add).then_inc(post[a], 1)
                        v.wait_ge(post[a], c + 1)
                        chunk_stats(X, 0, c * CT).then_inc(dv, 1)
                        v.wait_ge(dv, i * 4 + (base + 2 * s + 2))

            def routed_input(a):
                S = po[a]
                credit(S["yd"], 2)
                E, bias = (E0, w["rb"]) if a == 1 else (E1, None)

                def front(c, s):
                    if a == 3:
                        v.wait_ge(S["tr"], c + 1)
                        normalise(lambda q: XN[:, s, q, :], X, 0, c * CT).then_inc(S["xn"], 1)

                def back(c, s):
                    v.wait_ge(S["y"], c + 3)
                    src = PS[:, 3 * s + 2, 0:CT * E].rearrange("p (t m) -> p t m", t=CT)
                    dst = LG[:, bass.ds(c * CT, CT), 0:E]
                    if bias is not None:
                        ins = v.tensor_tensor(dst, src, bias[:, :].unsqueeze(1).broadcast_to([P, CT, E]), ALU.add)
                    else:
                        ins = v.tensor_copy(dst, src)
                    ins.then_inc(S["yd"], 1)

                by_chunks(v, front, back)
                v.wait_ge(S["yd"], 2 + CHUNKS)

            def rank(dst, val, E):
                step(v.tensor_copy(dst, w["later"][:, E1 - E:E1].unsqueeze(1).broadcast_to([P, TILES, E])))
                for d in range(1, E):
                    n = E - d
                    first = RA[:, 0:TILES * n].rearrange("p (t e) -> p t e", t=TILES)
                    step(v.tensor_tensor(first, val[:, :, 0:n], val[:, :, d:E], ALU.is_ge))
                    step(v.tensor_tensor(dst[:, :, d:E], dst[:, :, d:E], first, ALU.add))
                    step(v.tensor_tensor(dst[:, :, 0:n], dst[:, :, 0:n], first, ALU.subtract))

            def wide(t, E):
                return t[:, :].unsqueeze(2).broadcast_to([P, TILES, E])

            def finish_weights(m, scores, top, eps, E):
                rk, wr = RK[:, :, 0:E], WR[:, :, 0:E]
                step(v.tensor_scalar(rk, rk, top - 0.5, None, ALU.is_lt))
                step(v.tensor_tensor(wr, rk, scores, ALU.mult))
                step(v.tensor_reduce(T1[:, :], wr, AX.X, ALU.add))
                step(v.tensor_scalar(T1[:, :], T1[:, :], eps, None, ALU.add))
                step(v.reciprocal(T2[:, :], T1[:, :]))
                v.tensor_tensor(wr, wr, wide(T2, E), ALU.mult).then_inc(rt[m]["w"], 1)

            def spread_weights(m):
                S, E = rt[m], (E0, E1)[m]
                step(v.memset(WT, 0.0))
                step(v.memset(WT[ONES_ROW:ONES_ROW + 1, :], 1.0))
                for c in range(CHUNKS):
                    col = slice(c * CHUNK, (c + 1) * CHUNK)
                    v.wait_ge(S["wt"], c + 1)
                    step(v.tensor_copy(WPB[0:E, 0, :], PS[0:E, c, :]))
                    step(v.tensor_tensor(WP[0:E, :], PS[0:E, c, :], WPB[0:E, 0, :], ALU.subtract))
                    step(v.tensor_copy(WPB[0:E, 1, :], WP[0:E, :]))
                    v.tensor_copy(WT[0:E, col], WPB[0:E, 0, :])
                    v.tensor_copy(WT[32:32 + E, col], WPB[0:E, 1, :])
                    v.tensor_tensor(WT[64:64 + E, col], WP[0:E, :], WPB[0:E, 1, :], ALU.subtract).then_inc(S["wtd"], 1)
                    v.wait_ge(S["wtd"], c + 1)

            def route_softmax():
                lg, sc = LG[:, :, 0:E0], SC[:, :, 0:E0]
                step(v.tensor_reduce(T1[:, :], lg, AX.X, ALU.max))
                v.tensor_tensor(lg, lg, wide(T1, E0), ALU.subtract).then_inc(rt[0]["lg"], CHUNKS + 1)
                v.wait_ge(rt[0]["e"], 1)
                step(v.tensor_reduce(T1[:, :], sc, AX.X, ALU.add))
                step(v.reciprocal(T2[:, :], T1[:, :]))
                step(v.tensor_tensor(sc, sc, wide(T2, E0), ALU.mult))
                rank(RK[:, :, 0:E0], sc, E0)
                finish_weights(0, sc, 2, 1e-8, E0)

            def route_groups():
                v.nop().then_inc(rt[1]["lg"], CHUNKS)
                v.wait_ge(rt[1]["e"], 1)
                step(v.tensor_tensor(LG[:, :, :], SC[:, :, :], w["gb"][:, :].unsqueeze(1).broadcast_to([P, TILES, E1]),
                                     ALU.add))
                grp = LG[:, :, :].rearrange("p t (g k) -> p t g k", g=4)
                pairs = [(i, j) for i in range(4) for j in range(i + 1, 4)]
                for k, (i, j) in enumerate(pairs):
                    step(v.tensor_tensor(G4[0 if k == 0 else 1][:, :, :], grp[:, :, :, i], grp[:, :, :, j], ALU.add))
                    if k:
                        step(v.tensor_tensor(G4[0][:, :, :], G4[0][:, :, :], G4[1][:, :, :], ALU.max))
                rank(G4[2][:, :, :], G4[0][:, :, :], 4)
                step(v.tensor_scalar(G4[2][:, :, :], G4[2][:, :, :], 1.5, None, ALU.is_lt))
                step(v.tensor_tensor(grp, grp, G4[2][:, :, :].unsqueeze(3).broadcast_to([P, TILES, 4, 4]), ALU.mult))
                rank(RK[:, :, :], LG[:, :, :], E1)
                finish_weights(1, SC[:, :, :], 4, 1e-20, E1)

            def experts(m):
                S, NF = mo[m], (NF0, NF1)[m]
                credit(S["h"], 1)
                credit(S["yd"], 1)
                per = (0, NF)[m] + (2, 1)[m]
                base = loop_steps(per, CHUNKS)
                n_act = NF - 1 if m == 0 else NF
                with v.Fori(0, CHUNKS) as c:
                    k = 0
                    for j in range(NF):
                        bank = 3 * (j % 2)
                        h = HB[:, j % 4, :]
                        if m == 0 and j == NF - 1:
                            v.wait_ge(S["g"], c * NF + (j + 1))
                            v.wait_ge(S["dn"], c * NF + (1 + max(0, j - 3)))
                            v.tensor_copy(h, PS[:, bank + 2, :]).then_inc(S["h"], 1)
                            continue
                        v.wait_ge(S["a"], c * n_act + (j + 1))
                        if m == 1:
                            k += 1
                            v.tensor_tensor(h, h, PS[:, bank + 1, :], ALU.mult).then_inc(dv, 1)
                            v.wait_ge(dv, c * per + (base + k))
                        v.tensor_tensor(h, h, PS[:, bank + 2, :], ALU.mult).then_inc(S["h"], 1)
                    if m == 0:
                        k += 1
                        normalise(lambda q: YN[:, q, :], X, 0, c * CT).then_inc(dv, 1)
                        v.wait_ge(dv, c * per + (base + k))
                    v.wait_ge(S["yt"], c + 2)
                    dst = AO[:, bass.ds(c * CT, CT), :]
                    src = PS[:, 7, :].rearrange("p (t m) -> p t m", t=CT)
                    if m == 0:
                        ins = v.scalar_tensor_tensor(dst.rearrange("p t m -> p (t m)"), PS[:, 7, :], 0.3,
                                                     YN[:, :, :].rearrange("p t m -> p (t m)"), ALU.mult, ALU.add)
                    else:
                        ins = v.tensor_copy(dst, src)
                    k += 1
                    ins.then_inc(dv, 1)
                    v.wait_ge(dv, c * per + (base + k))
                    chunk_stats(AO, 1, c * CT).then_inc(S["yd"], 1)
                    assert k == per
                v.wait_ge(S["yd"], CHUNKS + 1)

            step(v.memset(EPSB[:, :], EPS))
            step(v.memset(SHF[:, :, :, :, :].rearrange("p a b c d -> p (a b c d)"), 0.0))
            v.wait_ge(x_in, 16 * BATCHES)
            base = loop_steps(1, CHUNKS)
            with v.Fori(0, CHUNKS) as c:
                chunk_stats(X, 0, c * CT).then_inc(dv, 1)
            v.wait_ge(dv, n_dv[0])
            finish_stats(0)
            v.wait_ge(w_in, 16 * len(w))
            project(0)
            attention(0)
            output(0)
            finish_stats(1)
            residual(0)
            finish_stats(0)
            project(1)
            attention(1)
            routed_input(1)
            route_softmax()
            spread_weights(0)
            experts(0)
            finish_stats(1)
            residual(1)
            step(v.memset(SHF[:, :, :, :, :].rearrange("p a b c d -> p (a b c d)"), 0.0))
            finish_stats(0)
            project(2)
            attention(2)
            output(2)
            finish_stats(1)
            residual(2)
            finish_stats(0)
            routed_input(3)
            route_groups()
            spread_weights(1)
            experts(1)
            finish_stats(1)
            residual(3)


def host_layout(i):
    bf = np.dtype("bfloat16")
    f = {k: np.asarray(v) for k, v in i.items()}

    def c(a):
        return np.ascontiguousarray(a)

    def row(a, n=P):
        return c(np.broadcast_to(a.reshape(1, -1), (n, a.size)))

    def padded(a, rows, cols):
        out = np.zeros((rows, cols), a.dtype)
        out[0:a.shape[0], 0:a.shape[1]] = a
        return out

    d = {"x": c(f["L0_attn_x"].reshape(TOKENS, DIM))}
    d["ident"] = np.eye(P, dtype=np.float32)
    d["identb"] = np.eye(P, dtype=np.float32).astype(bf)
    lower = np.arange(P)[:, None] > np.arange(P)[None, :]
    d["maskT"] = np.where(lower, np.float32(MASKED), np.float32(0)).astype(bf)
    d["mask"] = np.where(lower.T, np.float32(MASKED), np.float32(0)).astype(bf)
    for hd in (4, 8):
        d[f"blk{hd}"] = (np.arange(P)[:, None] // hd == np.arange(32)[None, :]).astype(bf)
    d["later"] = row(np.arange(E1 - 1, -1, -1).astype(np.float32))
    for name, owner, NF in (("sel0", np.repeat(np.arange(E0), F0 // E0), NF0), ("sel1", np.repeat(np.arange(E1), I1), NF1)):
        s = np.zeros((P, NF * P), np.float32)
        for part in range(3):
            s[32 * part + owner, np.arange(owner.size)] = 1
        if name == "sel0":
            for part in range(3):
                s[32 * part + np.arange(E0), F0 + np.arange(E0)] = 1
        else:
            s[ONES_ROW, owner.size:F1] = 1
        d[name] = s.astype(bf)
    d["wq0"], d["wk0"] = padded(f["L0_attn_Wq"].T, P, P), padded(f["L0_attn_Wk"].T, P, P)
    d["wv0"], d["wo0"] = padded(f["L0_attn_Wv"].T, P, 64), padded(f["L0_attn_Wo"].T, P, P)
    d["bo0"] = row(f["L0_attn_bo"])
    d["wq1"] = padded(f["L0_ffn_q_w"].reshape(DIM, HEADS, 8)[:, :, 0:4].reshape(DIM, 64), P, P)
    d["qb1"] = padded(f["L0_ffn_q_b"].reshape(HEADS, 8)[:, 0:4].reshape(64, 1), P, 1)
    d["wk1"], d["wv1"] = padded(f["L0_ffn_k_w"], P, P), c(f["L0_ffn_v_w"])
    d["kb1"], d["vb1"] = padded(f["L0_ffn_k_b"].reshape(64, 1), P, 1), row(f["L0_ffn_v_b"])
    d["wo1"], d["ob1"] = padded(f["L0_ffn_o_w"][0:64], P, P), c(f["L0_ffn_o_b"].reshape(P, 1))
    d["rw"], d["rb"] = c(f["L0_ffn_router_w"]), row(f["L0_ffn_router_b"])
    d["w1"] = c(f["L0_ffn_w1"].transpose(1, 0, 2).reshape(DIM, F0))
    d["b1"] = c(f["L0_ffn_b1"].reshape(F0 // P, P).T)
    w2 = np.zeros((NF0 * P, P), np.float32)
    w2[0:F0] = f["L0_ffn_w2"].reshape(F0, P)
    w2[F0:F0 + E0] = f["L0_ffn_b2"]
    d["w2"] = c(w2.reshape(NF0, P, P).transpose(1, 0, 2))
    for n, name in (("wq2", "query"), ("wk2", "key"), ("wv2", "value"), ("wo2", "proj")):
        d[n] = c(f[f"L1_attn_W_{name}"].T)
    d["gw"], d["gb"] = c(f["L1_ffn_gate_w"].T), row(f["L1_ffn_gate_bias"])
    for n, routed, shared in (("gp", "gate_proj", "shared_gate_w"), ("up", "up_proj", "shared_up_w")):
        a = np.zeros((DIM, NF1 * P), np.float32)
        a[:, 0:E1 * I1] = f[f"L1_ffn_{routed}"].reshape(E1 * I1, DIM).T
        a[:, E1 * I1:F1] = f[f"L1_ffn_{shared}"].T
        d[n] = a
    a = np.zeros((NF1 * P, P), np.float32)
    a[0:E1 * I1] = f["L1_ffn_down_proj"].transpose(0, 2, 1).reshape(E1 * I1, P)
    a[E1 * I1:F1] = f["L1_ffn_shared_down_w"].T
    d["dp"] = c(a.reshape(NF1, P, P).transpose(1, 0, 2))
    return d


def kernel(**inputs):
    from concourse import bacc
    from concourse.bass_utils import run_bass_kernel_spmd

    arrays = host_layout(inputs)
    nc = bacc.Bacc("TRN2", target_bir_lowering=False, num_devices=1)
    t_in = {n: nc.dram_tensor(f"in_{n}", a.shape, mybir.dt.from_np(a.dtype), kind="ExternalInput").ap()
            for n, a in arrays.items()}
    out = nc.dram_tensor("result", (TOKENS, DIM), FP32, kind="ExternalOutput").ap()
    build_program(nc, t_in, out)
    r = run_bass_kernel_spmd(nc, [{f"in_{n}": a for n, a in arrays.items()}], core_ids=[0])
    return r.results[0]["result"].reshape(BATCHES, SEQ, DIM)
```

```python
import numpy as np
import concourse.bass as bass
from concourse import mybir
from contextlib import ExitStack

FP32 = mybir.dt.float32
BF16 = mybir.dt.bfloat16
I32 = mybir.dt.int32
ALU = mybir.AluOpType
ACT = mybir.ActivationFunctionType
AX = mybir.AxisListType

P = 128
BATCHES, SEQ, DIM = 4, 1024, 128
TOKENS = BATCHES * SEQ
TILES = TOKENS // P
CT = 4
CHUNK = CT * P
CHUNKS = TOKENS // CHUNK
KT = SEQ // P
HEADS = 16
QH = 4
QUADS = HEADS // QH * BATCHES
EPS = 1e-5
RANGE = 58.0
TERMS = 8
Q_PARTS = (0, 0, 0, 1, 1, 2)
K_PARTS = (0, 1, 2, 0, 1, 0)
MASKED = -1e30
RING = 4


class Attn:

    def __init__(self, hd, scale, causal, biased):
        self.hd, self.scale, self.causal, self.biased = hd, scale, causal, biased
        self.M = HEADS * hd
        self.slots = QH * hd * TERMS // P
        self.hps = QH // self.slots
        self.units = []
        for half in range(2):
            for kt in range(KT):
                off = max(0, kt * P - half * CHUNK) if causal else 0
                if off < CHUNK:
                    self.units.append((half, kt, off, CHUNK - off, causal and kt * P >= half * CHUNK))
        self.U = len(self.units)
        self.E = 2 * self.U
        self.half_end = [sum(u[0] == 0 for u in self.units), self.U]
        self.last_kt = [max(u[1] for u in self.units if u[0] == h) for h in range(2)]
        self.period = -(-(self.E + 1) // 3) * 3

    def slot_of(self, k):
        return k % 3


LAYERS = [Attn(4, float(8) ** -0.5, False, False), Attn(4, 0.5, False, True),
          Attn(8, float(8) ** -0.5 / 128.0, True, False)]

E0, I0 = 8, 256
E1, I1, SH1 = 16, 176, 352
ROUTED = (E0 * I0 // P, E1 * I1 // P)
NT = (ROUTED[0], ROUTED[1] + -(-SH1 // P))
BANKS = (4, 2)
HRING = (4, 5)
LOOK = 2
MAGIC = 0x5F3759DF
FINISH_STEPS = (19, 17)


def by_chunks(eng, front, back, ahead=1):
    for c in range(ahead):
        front(c, c % 2)
    with eng.Fori(0, CHUNKS // 2 - 1) as i:
        for s in range(2):
            front(i * 2 + (s + ahead), (s + ahead) % 2)
            back(i * 2 + s, s)
    for c in range(CHUNKS - 2, CHUNKS):
        if c + ahead < CHUNKS:
            front(c + ahead, (c + ahead) % 2)
        back(c, c % 2)


def by_pipelined(eng, chunk):
    chunk(lambda k: k, 0, True, False)
    with eng.Fori(0, CHUNKS // 2 - 1) as i:
        for s in (1, 0):
            chunk(lambda k: i * 2 + (2 - s + k), s, False, False)
    chunk(lambda k: CHUNKS - 1 + k, 1, False, True)


def build_program(nc, t_in, out):
    ctx = ExitStack()
    with ctx:
        def sb(name, shape, dt=FP32):
            return ctx.enter_context(nc.sbuf_tensor(name, shape, dt))

        def sem(name):
            return ctx.enter_context(nc.semaphore(name))

        X = sb("X", [P, TILES, DIM])
        AO = sb("AO", [P, TILES, DIM])
        KG = [sb(f"KG{s}", [P, QH, SEQ], BF16) for s in range(2)]
        QG = [sb(f"QG{s}", [P, 2, SEQ], BF16) for s in range(2)]
        VG = [sb(f"VG{s}", [P, KT, QH, 32]) for s in range(2)]
        VT = sb("VT", [P, TILES, DIM])
        PR = sb("PR", [P, RING, QH, CHUNK])
        OSB = sb("OSB", [P, SEQ])
        XN = sb("XN", [P, 2, CT, DIM])
        XT = sb("XT", [P, 2, CHUNK])
        MTS = sb("MTS", [P, 2, CHUNK])
        NB = sb("NB", [64, CHUNKS])
        NBM = sb("NBM", [64, 1])
        NBR = sb("NBR", [1, 64])
        NBP = sb("NBP", [1, 32])
        NBX = sb("NBX", [1, 1])
        FLAG = sb("FLAG", [1, len(LAYERS)], I32)
        ST = [sb(f"ST{k}", [P, TILES, 6]) for k in range(2)]
        MEAN = [sb(f"MEAN{k}", [P, TILES]) for k in range(2)]
        RSTD = [sb(f"RSTD{k}", [P, TILES]) for k in range(2)]
        TMP = [sb(f"TMP{k}", [P, TILES]) for k in range(4)]
        RC = sb("RC", [P, KT, QH])
        MX = sb("MX", [P, KT, QH])
        MXP = sb("MXP", [P, KT, QH], BF16)
        SHF = sb("SHF", [P, 2, KT, 16, TERMS], BF16)
        LG = sb("LG", [P, TILES, E1])
        WR = sb("WR", [P, TILES, E1])
        SC = sb("SC", [P, TILES, E1])
        RK = sb("RK", [P, TILES, E1])
        G4 = [sb(f"G4{k}", [P, TILES, 4]) for k in range(3)]
        T1 = sb("T1", [P, TILES])
        T2 = sb("T2", [P, TILES])
        YN = sb("YN", [P, CT, DIM])
        flat = PR[:, :, :, :].rearrange("p a b c -> p (a b c)")
        MT = flat[:, 0:TOKENS]
        HB = flat[:, TOKENS:2 * TOKENS].rearrange("p (a n) -> p a n", n=CHUNK)
        WT = VT[:, :, :].rearrange("p a b -> p (a b)")
        OT = OSB[:, 0:CHUNK]
        QKF = flat[:, 0:2048].rearrange("p (s a n) -> p s a n", s=2, a=2)
        SQ = flat[:, 2048:3072].bitcast(BF16).rearrange("p (s a n) -> p s a n", s=2, a=2)
        PT = flat[:, 3072:6144].bitcast(BF16).rearrange("p (s t a n) -> p s t a n", s=2, t=3, a=2)
        aof = AO[:, :, :].rearrange("p a b -> p (a b)")
        CONST0 = aof[:, 0:TOKENS // 2].bitcast(BF16)
        CONST1 = aof[:, TOKENS // 2:TOKENS].bitcast(BF16)
        RA = VT[:, :, :].rearrange("p a b -> p (a b)")[:, 0:2048]
        PS = ctx.enter_context(nc.psum_tensor("PS", [P, 8, CHUNK], FP32))

        w = {}
        for name, (shape, dt) in {
            "ident": ([P, P], FP32), "identb": ([P, P], BF16), "maskT": ([P, P], BF16), "mask": ([P, P], BF16),
            "blk4": ([P, 32], BF16), "blk8": ([P, 32], BF16), "later": ([P, E1], FP32),
            "wq0": ([P, P], FP32), "wk0": ([P, P], FP32), "wv0": ([P, 64], FP32), "wo0": ([P, P], FP32),
            "bo0": ([P, P], FP32),
            "wq1": ([P, P], FP32), "wk1": ([P, P], FP32), "wv1": ([P, 64], FP32), "qb1": ([P, 1], FP32),
            "kb1": ([P, 1], FP32), "vb1": ([P, 64], FP32), "wo1": ([P, P], FP32), "ob1": ([P, 1], FP32),
            "rw": ([P, E0], FP32), "rb": ([P, E0], FP32), "b1": ([P, NT[0]], FP32),
            "wq2": ([P, P], FP32), "wk2": ([P, P], FP32), "wv2": ([P, P], FP32), "wo2": ([P, P], FP32),
            "gw": ([P, E1], FP32), "gb": ([P, E1], FP32),
        }.items():
            w[name] = sb(name, shape, dt)
        n0, n1 = NT[0] * P, NT[1] * P
        MW = sb("MW", [P, 3 * n1])
        experts0 = {"w1": MW[:, 0:n0], "w2": MW[:, n0:2 * n0 + P].rearrange("p (j n) -> p j n", j=NT[0] + 1)}
        experts1 = {"gp": MW[:, 0:n1], "up": MW[:, n1:2 * n1],
                    "dp": MW[:, 2 * n1:3 * n1].rearrange("p (j n) -> p j n", j=NT[1])}
        QD = nc.dram_tensor("q_rows", [P, TERMS, TOKENS], BF16, kind="Internal").ap()
        KD = nc.dram_tensor("k_rows", [P, TERMS, TOKENS], BF16, kind="Internal").ap()
        QDR = QD.rearrange("r t n -> (r t) n")
        KDR = KD.rearrange("r t n -> (r t) n")

        x_in = sem("x_in")
        w_in = sem("w_in")
        e0_in, e1_in = sem("e0_in"), sem("e1_in")
        consts_set = sem("consts_set")
        consts_out = sem("consts_out")
        dv = sem("dv")
        out_done = sem("out_done")
        flag_col, flag_row, flag_set = sem("flag_col"), sem("flag_row"), sem("flag_set")

        def many(prefix, names):
            return {n: sem(f"{prefix}_{n}") for n in names.split()}

        pj = [many(f"pj{a}", "xn tr xt qk qkv sq ev vev nrm nb split w0 w1") for a in range(3)]
        at = [many(f"at{a}", "s exp pv qg0 qg1 v oev t tr mxr mxd sh sht shd mxs") for a in range(3)]
        po = [many(f"po{a}", names) for a, names in enumerate(
            ("xn tr xt m yd yn", "xn tr xt m mt mtc y yd", "xn tr xt m yd yn", "xn tr mt mtc y yd"))]
        cleared = sem("cleared")
        rt = [many(f"rt{a}", "lg e w wt wtd") for a in range(2)]
        mo = [many(f"mo{a}", "g a u h dn oe yt yd f") for a in range(2)]
        post = [sem(f"post{a}") for a in range(4)]
        block = ctx.enter_context(nc.Block())

        @block.sync
        def _(sp):
            x_v = t_in["x"].rearrange("(t p) c -> p t c", p=P)
            for b in range(BATCHES):
                sp.dma_start(X[:, b * KT:(b + 1) * KT, :], x_v[:, b * KT:(b + 1) * KT, :]).then_inc(x_in, 16)
            order = ["ident", "wq0", "wk0", "wv0", "identb", "blk4"]
            order += [n for n in w if n not in order]
            for name in order:
                t = w[name]
                sp.dma_start(t[tuple(slice(None) for _ in t.shape)], t_in[name]).then_inc(w_in, 16)
            for name, t in experts0.items():
                sp.dma_start(t, t_in[name]).then_inc(e0_in, 16)
            sp.wait_ge(consts_set, 3)
            for t in (6, 7):
                sp.dma_start(QD[:, t, :], CONST0).then_inc(consts_out, 16)
                sp.dma_start(KD[:, t, :], CONST1).then_inc(consts_out, 16)
            for a, L in enumerate(LAYERS):
                S, T = pj[a], at[a]
                for s in range(2):
                    sp.nop().then_inc(S[f"w{s}"], 16)
                if a:
                    for s in range(2):
                        sp.wait_ge(at[a - 1][f"qg{s}"], 16 * (QUADS // 2) * (LAYERS[a - 1].slots + QH))
                with sp.Fori(0, CHUNKS // 2) as i:
                    for s in range(2):
                        c = i * 2 + s
                        sp.wait_ge(S["split"], c + 3)
                        col = bass.ds(c * CHUNK, CHUNK)
                        for t0, n, part in ((0, 3, 0), (3, 2, 1), (5, 1, 2)):
                            sp.dma_start(QD[0:L.M, t0:t0 + n, col],
                                         PT[0:L.M, s, part:part + 1, 0, :].broadcast_to([L.M, n, CHUNK]))\
                              .then_inc(S[f"w{s}"], 16)
                        for t0, n in ((0, 3), (3, 2), (5, 1)):
                            sp.dma_start(KD[0:L.M, t0:t0 + n, col], PT[0:L.M, s, 0:n, 1, :]).then_inc(S[f"w{s}"], 16)
                if a == 2:
                    sp.wait_ge(mo[0]["dn"], HRING[0] + CHUNKS * NT[0])
                    for name, t in experts1.items():
                        sp.dma_start(t, t_in[name]).then_inc(e1_in, 16)
                for s in range(2):
                    sp.wait_ge(S[f"w{s}"], 16 + 6 * 16 * CHUNKS // 2)
                if a == 0:
                    sp.wait_ge(consts_out, 64)
                sp.wait_ge(consts_set, 3 + (1 if a < 2 else 2))
                rows = L.hd * TERMS
                with sp.Fori(0, BATCHES) as b:
                    with sp.Fori(0, 2) as p:
                        for s in range(2):
                            quad = p * 2 + s
                            sp.wait_ge(T["s"], (b * 4 + quad) * L.E + 1)
                            col = bass.ds(b * SEQ, SEQ)
                            for k in range(L.slots):
                                sp.dma_start(QG[s][:, k, :], QDR[bass.ds((quad * L.slots + k) * P, P), col])\
                                  .then_inc(T[f"qg{s}"], 16)
                            for h in range(QH):
                                r0 = (h % L.hps) * rows
                                sp.dma_start(KG[s][r0:r0 + rows, h, :],
                                             KDR[bass.ds(quad * QH * rows + h * rows, rows), col])\
                                  .then_inc(T[f"qg{s}"], 16)
            o_v = out.rearrange("(t p) c -> p t c", p=P)
            for c in range(CHUNKS):
                sp.wait_ge(post[3], c + 1)
                sp.dma_start(o_v[:, c * CT:(c + 1) * CT, :], X[:, c * CT:(c + 1) * CT, :]).then_inc(out_done, 16)
            sp.wait_ge(out_done, 16 * CHUNKS)

        @block.gpsimd
        def _(pool):
            pool.memset(CONST0, 0.0)
            pool.memset(CONST1, 1.0).then_inc(consts_set, 3)
            for s in range(2):
                pool.memset(KG[s][:, :, :], 0.0)
                pool.memset(VG[s][:, :, :, :], 0.0).then_inc(cleared, 1)
            pool.wait_ge(cleared, 2)
            for s in range(2):
                last = pool.memset(VG[s][:, :, :, 4:5], 1.0)
            last.then_inc(consts_set, 1)
            for a, L in enumerate(LAYERS):
                S, T = pj[a], at[a]
                if a == 2:
                    pool.wait_ge(at[1]["s"], (1 + QUADS) * LAYERS[1].E + 1)
                    pool.wait_ge(at[1]["pv"], (1 + QUADS) * LAYERS[1].U + 1)
                    for s in range(2):
                        pool.memset(KG[s][:, :, :], 0.0)
                        pool.memset(VG[s][:, :, :, :], 0.0).then_inc(cleared, 1)
                    pool.wait_ge(cleared, 4)
                    for s in range(2):
                        last = pool.memset(VG[s][:, :, :, 8:9], 1.0)
                    last.then_inc(consts_set, 1)
                pool.wait_ge(S["vev"], 2 + CHUNKS)
                with pool.Fori(0, BATCHES) as b:
                    with pool.Fori(0, 2) as p:
                        for s in range(2):
                            quad = p * 2 + s
                            pool.wait_ge(T["pv"], (b * 4 + quad) * L.U + 1)
                            src = VT[:, bass.ds(b * KT, KT), bass.ds(quad * QH * L.hd, QH * L.hd)]
                            pool.tensor_copy(VG[s][:, :, :, 0:L.hd],
                                             src.rearrange("p t (h d) -> p t h d", h=QH)).then_inc(T["v"], 1)
                S = po[a]
                pool.wait_ge(T["tr"], QUADS + 1)
                if L.M < P:
                    pool.memset(XN[:, :, :, L.M:P], 0.0)
                if a == 1:
                    pool.nop().then_inc(S["mtc"], 2)

                def front(c, s):
                    pool.wait_ge(S["tr"], c + 1)
                    pool.tensor_copy(XN[:, s, :, 0:L.M], AO[:, bass.ds(c * CT, CT), 0:L.M]).then_inc(S["xn"], 1)

                def back(c, s):
                    if a == 1:
                        pool.wait_ge(S["mt"], c + 3)
                        pool.tensor_copy(MT[:, bass.ds(c * CHUNK, CHUNK)], MTS[:, s, :]).then_inc(S["mtc"], 1)

                by_chunks(pool, front, back)
                if a != 1:
                    pool.nop().then_inc(post[a], 2)
                    with pool.Fori(0, CHUNKS // 2) as i:
                        for s in range(2):
                            c = i * 2 + s
                            pool.wait_ge(S["yn"], c + 1)
                            xs = X[:, bass.ds(c * CT, CT), :]
                            pool.tensor_tensor(xs, xs, XN[:, s, :, :], ALU.add).then_inc(post[a], 1)
            S = po[3]
            pool.nop().then_inc(S["mtc"], 2)
            with pool.Fori(0, CHUNKS // 2) as i:
                for s in range(2):
                    c = i * 2 + s
                    pool.wait_ge(S["mt"], c + 3)
                    pool.tensor_copy(MT[:, bass.ds(c * CHUNK, CHUNK)], MTS[:, s, :]).then_inc(S["mtc"], 1)

        @block.scalar
        def _(act):
            def credit(s, n):
                act.nop().then_inc(s, n)

            def project(a):
                L, S = LAYERS[a], pj[a]
                for name in ("sq", "ev") if L.biased else ("sq", "ev", "vev"):
                    credit(S[name], 2)

                def transposed(c, s):
                    act.wait_ge(S["tr"], c + 3)
                    act.wait_ge(S["qkv"], c + 1)
                    act.activation(XT[:, s, :], PS[:, 4 * s, :], ACT.Copy).then_inc(S["xt"], 1)

                def chunk(at, s, first, last):
                    c = at(0)
                    if first:
                        transposed(c, s)
                    act.wait_ge(S["nrm"], c + 1)
                    act.wait_ge(S["split"], c + 1)
                    for n, bias in enumerate(("qb1", "kb1")):
                        b = w[bias][:, 0:1] if L.biased else 0.0
                        act.wait_ge(S["qk"], c * 2 + (n + 1))
                        ins = act.activation(SQ[:, s, n, :], PS[:, 4 * s + 1 + n, :], ACT.Square, bias=b)
                        if n:
                            ins.then_inc(S["sq"], 1)
                        act.activation(QKF[:, s, n, :], PS[:, 4 * s + 1 + n, :], ACT.Identity, bias=b)
                        if n == 0:
                            act.wait_ge(S[f"w{s}"], (c - s) * (6 * 8) + 16)
                        if L.biased:
                            last_part = act.activation(PT[:, s, 0, n, :], PS[:, 4 * s + 1 + n, :], ACT.Identity, bias=b)
                    if not L.biased:
                        last_part = act.activation(PT[:, s, 0, :, :], PS[:, 4 * s + 1:4 * s + 3, :], ACT.Copy)
                    last_part.then_inc(S["ev"], 1)
                    if not last:
                        transposed(at(1), 1 - s)
                    if not L.biased:
                        act.wait_ge(S["qkv"], c + 3)
                        act.activation(VT[:, bass.ds(c * CT, CT), 0:L.M],
                                       PS[:, 4 * s + 3, 0:CT * L.M].rearrange("p (t m) -> p t m", t=CT),
                                       ACT.Copy).then_inc(S["vev"], 1)

                by_pipelined(act, chunk)

            def softmax(a):
                L, T = LAYERS[a], at[a]
                credit(T["exp"], L.E)
                with act.Fori(0, QUADS) as n:
                    for u, (half, kt, off, width, diag) in enumerate(L.units):
                        for g in range(2):
                            e = 2 * u + g
                            act.wait_ge(T["s"], n * L.E + (e + 2 + L.E))
                            if g == 0:
                                act.wait_ge(T["pv"], n * L.U + (u + 2 - RING + L.U))
                            slot = ((e - 4) % L.E) % 3
                            act.activation(PR[:, u % RING, 2 * g:2 * g + 2, off:off + width],
                                           PS[:, 2 * slot:2 * slot + 2, off:off + width],
                                           ACT.Exp, scale=L.scale).then_inc(T["exp"], 1)

            def after_attention(a):
                S = po[a]
                for name in ("xt", "mt"):
                    if name in S:
                        credit(S[name], 2)
                with act.Fori(0, CHUNKS // 2) as i:
                    for s in range(2):
                        c = i * 2 + s
                        act.wait_ge(S["tr"], c + 3)
                        if a == 3:
                            act.wait_ge(S["y"], c + 1)
                            act.wait_ge(S["mtc"], c + 1)
                            act.activation(MTS[:, s, :], PS[:, 3 * s, :], ACT.Copy).then_inc(S["mt"], 1)
                            continue
                        act.wait_ge(S["m"], c + 1)
                        act.activation(XT[:, s, :], PS[:, 3 * s, :], ACT.Copy).then_inc(S["xt"], 1)
                        if a == 1:
                            act.wait_ge(S["m"], c + 3)
                            act.wait_ge(S["y"], c + 1)
                            act.wait_ge(S["mtc"], c + 1)
                            act.activation(MTS[:, s, :], PS[:, 3 * s + 1, :], ACT.Identity, bias=w["ob1"][:, 0:1])\
                               .then_inc(S["mt"], 1)

            def experts(m):
                S, T = mo[m], NT[m]
                credit(S["oe"], 2)

                def output(c, s):
                    act.wait_ge(S["dn"], c * T + (T + HRING[m]))
                    act.wait_ge(S["yt"], c + 1)
                    act.activation(OT, PS[:, 6 + s, :], ACT.Copy).then_inc(S["oe"], 1)

                def chunk(at, s, first, last):
                    for j in range(T):
                        pos = s * T + j
                        act.wait_ge(S["g"], at(0) * T + (j + 1))
                        act.wait_ge(S["dn"], at(0) * T + (j + 1))
                        h = HB[:, pos % HRING[m], :]
                        if m == 0:
                            act.activation(h, PS[:, pos % 4, :], ACT.Gelu, bias=w["b1"][:, j:j + 1]).then_inc(S["a"], 1)
                        else:
                            act.activation(h, PS[:, 2 * (pos % 2), :], ACT.Silu).then_inc(S["a"], 1)
                        if j == LOOK - 1 and not first:
                            output(at(-1), 1 - s)
                    if last:
                        output(at(0), s)

                by_pipelined(act, chunk)

            def weights(m):
                S = rt[m]
                for c in range(CHUNKS):
                    act.wait_ge(S["wt"], c + 1)
                    act.activation(WT[:, c * CHUNK:(c + 1) * CHUNK], PS[:, c, :], ACT.Copy).then_inc(S["wtd"], 1)

            act.wait_ge(w_in, 16 * len(w))
            project(0)
            softmax(0)
            after_attention(0)
            project(1)
            softmax(1)
            after_attention(1)
            act.wait_ge(rt[0]["lg"], CHUNKS + 1)
            act.activation(SC[:, :, 0:E0], LG[:, :, 0:E0], ACT.Exp).then_inc(rt[0]["e"], 1)
            weights(0)
            experts(0)
            project(2)
            softmax(2)
            after_attention(2)
            after_attention(3)
            act.wait_ge(rt[1]["lg"], CHUNKS)
            act.activation(SC[:, :, :], LG[:, :, :], ACT.Sigmoid).then_inc(rt[1]["e"], 1)
            weights(1)
            experts(1)

        @block.tensor
        def _(pe):
            def credit(s, n):
                pe.nop().then_inc(s, n)

            def transposes(dst_bank, s):
                for k in range(CT):
                    last = pe.transpose(PS[:, dst_bank, k * P:(k + 1) * P], XN[:, s, k, :], w["ident"][:, :])
                return last

            def project(a):
                L, S = LAYERS[a], pj[a]
                for name in ("tr", "qkv", "nrm"):
                    credit(S[name], 2)
                blk = w["blk4"] if L.hd == 4 else w["blk8"]

                def transposed(c, s):
                    pe.wait_ge(S["xn"], c + 1)
                    pe.wait_ge(S["nb"], c + 1)
                    transposes(4 * s, s).then_inc(S["tr"], 1)

                def chunk(at, s, first, last):
                    c = at(0)
                    if first:
                        transposed(c, s)
                    pe.wait_ge(S["xt"], c + 1)
                    pe.wait_ge(S["ev"], c + 1)
                    for n, name in enumerate(("wq", "wk")):
                        pe.matmul(PS[:, 4 * s + 1 + n, :], w[f"{name}{a}"][:, :], XT[:, s, :],
                                  start=True, stop=True).then_inc(S["qk"], 1)
                    if not last:
                        transposed(at(1), 1 - s)
                    pe.wait_ge(S["vev"], c + 1)
                    for k in range(CT):
                        ins = pe.matmul(PS[:, 4 * s + 3, k * L.M:(k + 1) * L.M],
                                        XT[:, s, k * P:(k + 1) * P], w[f"wv{a}"][:, :],
                                        start=True, stop=True)
                    ins.then_inc(S["qkv"], 1)
                    pe.wait_ge(S["sq"], c + 3)
                    for n in range(2):
                        ins = pe.matmul(PS[32 * n:32 * n + 32, 4 * s, :], blk[:, :], SQ[:, s, n, :],
                                        start=True, stop=True)
                    ins.then_inc(S["nrm"], 1)

                by_pipelined(pe, chunk)
                pe.wait_ge(flag_col, a + 1)
                pe.transpose(PS[0:1, 0, 0:64], NBM[:, :], w["ident"][0:64, 0:64]).then_inc(flag_row, 1)
                pe.wait_ge(S["ev"], CHUNKS + 2)
                pe.wait_ge(S["vev"], CHUNKS + 2)
                pe.wait_ge(S["nb"], CHUNKS + 2)

            def attention(a):
                L, T = LAYERS[a], at[a]
                credit(T["pv"], L.U + 1)
                credit(T["sht"], 1)
                credit(T["s"], L.E + 1)
                pe.wait_ge(flag_set, a + 1)
                flag = pe.value_load(FLAG[0:1, a:a + 1], min_val=0, max_val=1)

                def exp_done(n, k):
                    pe.wait_ge(T["exp"], n * L.E + (4 + k + 1 + L.E))

                def free_slot(n, k, first):
                    if k >= 3:
                        return exp_done(n, k - 3)
                    j = k - 3 + L.period
                    while j > L.E:
                        j -= 3
                    if j == L.E:
                        pe.wait_ge(T["tr"], n + 1)
                        j -= 3
                    pe.wait_ge(T["exp"], n * L.E + (4 + j + 1))

                def maxima(n, s):
                    with pe.If(flag > 0):
                        pe.wait_ge(T["exp"], n * L.E + L.E)
                        for h in range(QH):
                            for qc in range(KT):
                                r = h * KT + qc
                                b0 = 2 * (r % 3)
                                if r >= 3:
                                    pe.wait_ge(T["mxd"], n * (QH * KT) + (r - 2))
                                keys = (qc + 1) * P if L.causal else SEQ
                                for k0 in range(0, keys, CHUNK):
                                    width = min(CHUNK, keys - k0)
                                    diag = L.causal and k0 + width == keys
                                    bank, queries = b0 + k0 // CHUNK, QG[s][:, h // L.hps, qc * P:(qc + 1) * P]
                                    plain = width - P if diag else width
                                    if plain:
                                        last = pe.matmul(PS[:, bank, 0:plain], queries, KG[s][:, h, k0:k0 + plain],
                                                         start=True, stop=True)
                                    if diag:
                                        pe.matmul(PS[:, bank, plain:width], queries, KG[s][:, h, k0 + plain:k0 + width],
                                                  start=True, stop=False)
                                        last = pe.matmul(PS[:, bank, plain:width], w["identb"][:, :], w["mask"][:, :],
                                                         start=False, stop=True)
                                last.then_inc(T["mxr"], 1)
                        pe.wait_ge(T["sh"], n + 1)
                        for k in range(L.slots):
                            sh = PS[:, 2 * k, :].bitcast(BF16)
                            for qc in range(KT):
                                last = pe.transpose(sh[:, qc * P:(qc + 1) * P],
                                                    SHF[:, k, qc, :, :].rearrange("p r t -> p (r t)"),
                                                    w["identb"][:, :])
                        last.then_inc(T["sht"], 1)
                        pe.wait_ge(T["shd"], n + 1)

                def scores(n, s, u):
                    half, kt, off, width, diag = L.units[u]
                    q0 = half * CHUNK + off
                    for h in range(QH):
                        e = 2 * u + h // 2
                        slot = ((e - 4) % L.E) % 3
                        yield h, e
                        bank, keys, queries = 2 * slot + h % 2, KG[s][:, h, kt * P:(kt + 1) * P], QG[s][:, h // L.hps, :]
                        if diag:
                            pe.matmul(PS[:, bank, off:off + P], keys, queries[:, q0:q0 + P], start=True, stop=False)
                            last = pe.matmul(PS[:, bank, off:off + P], w["identb"][:, :], w["maskT"][:, :],
                                             start=False, stop=True)
                            off_, q_ = off + P, q0 + P
                        else:
                            off_, q_ = off, q0
                        if off_ < CHUNK:
                            last = pe.matmul(PS[:, bank, off_:CHUNK], keys, queries[:, q_:(half + 1) * CHUNK],
                                             start=True, stop=True)
                        if h % 2:
                            last.then_inc(T["s"], 1)

                def products(n, s, u):
                    half, kt, off, width, diag = L.units[u]
                    pe.wait_ge(T["exp"], n * L.E + (2 * u + 2 + L.E))
                    for h in range(QH):
                        last = pe.matmul(PS[32 * h:32 * h + 32, 6 + half, off:CHUNK], VG[s][:, kt, h, :],
                                         PR[:, u % RING, h, off:CHUNK], start=(kt == 0), stop=(kt == L.last_kt[half]),
                                         skip_group_check=True, tile_position=(0, 32 * h))
                    last.then_inc(T["pv"], 1)

                def quad(n, s, final):
                    pe.wait_ge(T["v"], n + 1)
                    for u in range(L.U):
                        products(n, s, u)
                        nxt = u + 2 >= L.U
                        if nxt and final:
                            continue
                        if u + 2 == L.U:
                            pe.wait_ge(T[f"qg{1 - s}"], loads(n, 1 - s))
                            maxima(n + 1, 1 - s)
                        for h, e in scores(n, 1 - s if nxt else s, (u + 2) % L.U):
                            if h % 2 == 0:
                                free_slot(n, 2 * u + h // 2, False)
                    exp_done(n, L.E - 3) if not final else pe.wait_ge(T["exp"], n * L.E + (L.E + L.E))
                    pe.wait_ge(T["oev"], n * 2 + 2)
                    b0 = 2 * (L.E % 3)
                    for k in range(KT):
                        last = pe.transpose(PS[:, b0 + k // 4, (k % 4) * P:(k % 4 + 1) * P], OSB[:, k * P:(k + 1) * P],
                                            w["ident"][:, :])
                    last.then_inc(T["t"], 1)

                per = 16 * (L.slots + QH)
                pe.wait_ge(T["qg0"], per)
                maxima(0, 0)
                for u in range(2):
                    for h, e in scores(0, 0, u):
                        if e == 3 and h % 2 == 0:
                            pe.wait_ge(T["exp"], 1 + L.E)
                with pe.Fori(0, QUADS // 2 - 1) as i:
                    for s in range(2):
                        def loads(n, s_next, i=i):
                            return (i + (1 if s_next else 2)) * per
                        quad(i * 2 + s, s, False)
                i = QUADS // 2 - 1

                def loads(n, s_next):
                    return (QUADS // 2) * per
                quad(QUADS - 2, 0, False)
                quad(QUADS - 1, 1, True)
                pe.wait_ge(T["tr"], QUADS + 1)

            def output(a):
                L, S = LAYERS[a], po[a]
                credit(S["tr"], 2)
                credit(S["m"], 2)

                def front(c, s):
                    pe.wait_ge(S["xn"], c + 1)
                    pe.wait_ge(S["xt"], c + 1)
                    transposes(3 * s, s).then_inc(S["tr"], 1)

                def back(c, s):
                    pe.wait_ge(S["xt"], c + 3)
                    pe.wait_ge(S["yd"], c + 1)
                    for k in range(CT):
                        last = pe.matmul(PS[:, 3 * s + 1, k * P:(k + 1) * P], XT[:, s, k * P:(k + 1) * P],
                                         w[f"wo{a}"][:, :], start=True, stop=True)
                    last.then_inc(S["m"], 1)

                by_chunks(pe, front, back)
                pe.wait_ge(S["yd"], CHUNKS + 2)

            def routed_input(a):
                S = po[a]
                credit(S["tr"], 2)
                if a == 1:
                    credit(S["m"], 2)
                credit(S["y"], 2)
                E, rw = (E0, w["rw"]) if a == 1 else (E1, w["gw"])

                def front(c, s):
                    pe.wait_ge(S["xn"], c + 1)
                    pe.wait_ge(S["mt"], c + 1)
                    transposes(3 * s, s).then_inc(S["tr"], 1)
                    if a == 1:
                        pe.wait_ge(S["xt"], c + 3)
                        pe.matmul(PS[:, 3 * s + 1, :], w["wo1"][:, :], XT[:, s, :],
                                  start=True, stop=True).then_inc(S["m"], 1)

                def back(c, s):
                    pe.wait_ge(S["mt"], c + 3)
                    pe.wait_ge(S["yd"], c + 1)
                    for k in range(CT):
                        last = pe.matmul(PS[:, 3 * s + 2, k * E:(k + 1) * E], MTS[:, s, k * P:(k + 1) * P],
                                         rw[:, :], start=True, stop=True)
                    last.then_inc(S["y"], 1)

                by_chunks(pe, front, back)
                pe.wait_ge(S["yd"], CHUNKS + 2)

            def weights(m):
                S = rt[m]
                for c in range(CHUNKS):
                    pe.wait_ge(S["w"], c + 1)
                    for k in range(CT):
                        last = pe.transpose(PS[:, c, k * P:(k + 1) * P], AO[:, c * CT + k, :], w["ident"][:, :])
                    last.then_inc(S["wt"], 1)
                pe.wait_ge(S["wtd"], CHUNKS)

            def experts(m):
                S, T = mo[m], NT[m]
                down = experts0["w2"] if m == 0 else experts1["dp"]
                credit(S["h"], BANKS[m])
                credit(S["dn"], HRING[m])
                credit(S["yt"], 1)
                pe.wait_ge(po[3 if m else 1]["mtc"], 2 + CHUNKS)
                pe.wait_ge(e1_in if m else e0_in, 16 * len(experts1 if m else experts0))

                def up_products(c, s, j):
                    pos = s * T + j
                    x_t, col = MT[:, bass.ds(c * CHUNK, CHUNK)], slice(j * P, (j + 1) * P)
                    pe.wait_ge(S["h"], c * T + (j + 1))
                    if m == 0:
                        last = pe.matmul(PS[:, pos % 4, :], experts0["w1"][:, col], x_t, start=True, stop=True)
                    else:
                        bank = 2 * (pos % 2)
                        pe.matmul(PS[:, bank, :], experts1["gp"][:, col], x_t, start=True, stop=True)
                        last = pe.matmul(PS[:, bank + 1, :], experts1["up"][:, col], x_t, start=True, stop=True)
                    last.then_inc(S["g"], 1)

                def down_product(c, s, j):
                    if j == 0:
                        pe.wait_ge(S["oe"], c + 1)
                        if m == 0:
                            pe.matmul(PS[:, 6 + s, :], down[:, T, :], WT[:, bass.ds(c * CHUNK, CHUNK)],
                                      start=True, stop=False)
                    pe.wait_ge(S["h"], c * T + (j + 1 + BANKS[m]))
                    pe.matmul(PS[:, 6 + s, :], down[:, j, :], HB[:, (s * T + j) % HRING[m], :],
                              start=(j == 0 and m == 1), stop=(j == T - 1)).then_inc(S["dn"], 1)

                def output(c, s):
                    pe.wait_ge(S["oe"], c + 3)
                    pe.wait_ge(S["yd"], c + 1)
                    for k in range(CT):
                        last = pe.transpose(PS[:, 4 + s, k * P:(k + 1) * P], OT[:, k * P:(k + 1) * P], w["ident"][:, :])
                    last.then_inc(S["yt"], 1)

                def chunk(at, s, first, last):
                    if first:
                        for j in range(LOOK):
                            up_products(at(0), s, j)
                    for j in range(T):
                        if j + LOOK < T:
                            up_products(at(0), s, j + LOOK)
                        elif not last:
                            up_products(at(1), 1 - s, j + LOOK - T)
                        down_product(at(0), s, j)
                        if j == 2 and not first:
                            output(at(-1), 1 - s)
                    if last:
                        output(at(0), s)

                by_pipelined(pe, chunk)
                pe.wait_ge(S["yd"], CHUNKS + 2)

            pe.wait_ge(w_in, 16 * len(w))
            project(0)
            attention(0)
            output(0)
            project(1)
            attention(1)
            routed_input(1)
            weights(0)
            experts(0)
            project(2)
            attention(2)
            output(2)
            routed_input(3)
            weights(1)
            experts(1)

        @block.vector
        def _(v):
            n_dv = [0]

            def credit(s, n):
                v.nop().then_inc(s, n)

            def step(ins, at_=None):
                n_dv[0] += 1
                ins.then_inc(dv, 1)
                v.wait_ge(dv, n_dv[0])

            def deviations(k, tiles, n, done):
                st, (a, b, x, y) = ST[k], [TMP[q][:, 0:n] for q in range(4)]
                mean, rstd = MEAN[k][:, tiles], RSTD[k][:, tiles]
                v.tensor_tensor(a, st[:, tiles, 1], st[:, tiles, 4], ALU.add)
                v.tensor_tensor(b, st[:, tiles, 1], st[:, tiles, 4], ALU.subtract)
                done(v.tensor_tensor(x, st[:, tiles, 2], st[:, tiles, 5], ALU.add))
                v.tensor_scalar(mean, a, 0.5, None, ALU.mult)
                done(v.tensor_tensor(b, b, b, ALU.mult))
                done(v.scalar_tensor_tensor(x, b, DIM / 4.0, x, ALU.mult, ALU.add))
                done(v.tensor_scalar(x, x, 1.0 / DIM, EPS, ALU.mult, ALU.add))
                v.tensor_scalar(a, x, -0.5, None, ALU.mult)
                done(v.tensor_scalar(y.bitcast(I32), x.bitcast(I32), 1, None, ALU.logical_shift_right))
                done(v.tensor_scalar(y.bitcast(I32), y.bitcast(I32), -1.0, float(MAGIC), ALU.mult, ALU.add))
                for step_ in range(3):
                    done(v.tensor_tensor(b, y, a, ALU.mult))
                    done(v.tensor_tensor(b, b, y, ALU.mult))
                    done(v.scalar_tensor_tensor(rstd if step_ == 2 else y, b, 1.5, y, ALU.add, ALU.mult))

            def finish_stats(k):
                deviations(k, slice(0, TILES), TILES, step)

            def loop_steps(per, count):
                base = n_dv[0]
                n_dv[0] += per * count
                return base

            def normalise(dst, src, k, t0):
                for q in range(CT):
                    last = v.tensor_scalar(dst(q), src[:, bass.ds(t0 + q, 1), :].rearrange("p a c -> p (a c)"),
                                           MEAN[k][:, bass.ds(t0 + q, 1)], RSTD[k][:, bass.ds(t0 + q, 1)],
                                           ALU.subtract, ALU.mult)
                return last

            def chunk_stats(src, k, t0):
                for q in range(CT):
                    last = v.bn_stats(ST[k][:, bass.ds(t0 + q, 1), :].rearrange("p a c -> p (a c)"),
                                      src[:, bass.ds(t0 + q, 1), :].rearrange("p a c -> p (a c)"))
                return last

            def project(a):
                L, S = LAYERS[a], pj[a]
                for name in ("nb", "vev", "split") if L.biased else ("nb", "split"):
                    credit(S[name], 2)
                base = loop_steps(2, CHUNKS)

                def front(c, s):
                    v.wait_ge(S["tr"], c + 1)
                    normalise(lambda q: XN[:, s, q, :], X, 0, c * CT).then_inc(S["xn"], 1)

                def back(c, s):
                    f = QKF[:, s, :, :]
                    pt = [PT[:, s, part, :, :] for part in range(3)]
                    v.wait_ge(S["ev"], c + 3)
                    v.tensor_tensor(f, f, pt[0], ALU.subtract).then_inc(dv, 1)
                    v.wait_ge(S["nrm"], c + 3)
                    v.tensor_reduce(NB[:, bass.ds(c, 1)], PS[0:64, 4 * s, :], AX.X, ALU.max).then_inc(S["nb"], 1)
                    v.wait_ge(dv, c * 2 + (base + 1))
                    v.tensor_copy(pt[1], f).then_inc(dv, 1)
                    v.wait_ge(dv, c * 2 + (base + 2))
                    v.tensor_tensor(pt[2], f, pt[1], ALU.subtract).then_inc(S["split"], 1)
                    if L.biased:
                        v.wait_ge(S["qkv"], c + 3)
                        v.tensor_tensor(VT[:, bass.ds(c * CT, CT), 0:L.M],
                                        PS[:, 4 * s + 3, 0:CT * L.M].rearrange("p (t m) -> p t m", t=CT),
                                        w["vb1"][:, :].unsqueeze(1).broadcast_to([P, CT, L.M]), ALU.add)\
                         .then_inc(S["vev"], 1)

                by_chunks(v, front, back, ahead=2)
                v.wait_ge(S["nb"], CHUNKS + 2)
                v.tensor_reduce(NBM[:, :], NB[:, :], AX.X, ALU.max).then_inc(flag_col, 1)
                v.wait_ge(flag_row, a + 1)
                step(v.tensor_copy(NBR[:, :], PS[0:1, 0, 0:64]))
                step(v.tensor_tensor(NBP[:, :], NBR[:, 0:32], NBR[:, 32:64], ALU.mult))
                step(v.tensor_reduce(NBX[:, :], NBP[:, :], AX.X, ALU.max))
                v.tensor_scalar(FLAG[:, a:a + 1], NBX[:, :], (RANGE / L.scale) ** 2, None, ALU.is_gt)\
                 .then_inc(flag_set, 1)
                v.wait_ge(flag_set, a + 1)

            def attention(a):
                L, T = LAYERS[a], at[a]
                flag = v.value_load(FLAG[0:1, a:a + 1], min_val=0, max_val=1)
                cols = L.hd
                credit(T["tr"], 1)

                def maxima(n, s):
                    with v.If(flag > 0):
                        for h in range(QH):
                            for qc in range(KT):
                                r = h * KT + qc
                                b0 = 2 * (r % 3)
                                v.wait_ge(T["mxr"], n * (QH * KT) + (r + 1))
                                keys = (qc + 1) * P if L.causal else SEQ
                                src = (PS[:, b0:b0 + 2, :].rearrange("p a b -> p (a b)"))[:, 0:keys]
                                v.tensor_reduce(MX[:, qc, h:h + 1], src, AX.X, ALU.max, negate=True).then_inc(T["mxd"], 1)
                        v.wait_ge(T["mxd"], n * (QH * KT) + QH * KT)
                        v.wait_ge(T["sht"], n + 1)

                        def part(k):
                            return [SHF[:, m, :, k:k + (L.hps - 1) * L.hd + 1:L.hd, 6] for m in range(L.slots)]

                        def heads(t, m):
                            return t[:, :, m * L.hps:(m + 1) * L.hps]

                        for k in range(3):
                            v.tensor_copy(MXP[:, :, :], MX[:, :, :]).then_inc(T["mxs"], 1)
                            v.wait_ge(T["mxs"], n * 6 + (2 * k + 1))
                            for m in range(L.slots):
                                last = v.tensor_copy(part(k)[m], heads(MXP, m))
                            if k < 2:
                                last = v.tensor_tensor(MX[:, :, :], MX[:, :, :], MXP[:, :, :], ALU.subtract)
                            last.then_inc(T["mxs"], 1)
                            v.wait_ge(T["mxs"], n * 6 + (2 * k + 2))
                        v.nop().then_inc(T["sh"], 1)
                        v.wait_ge(T["sht"], n + 2)
                        for m in range(L.slots):
                            last = v.tensor_tensor(QG[s][:, m, :], QG[s][:, m, :], PS[:, 2 * m, :].bitcast(BF16), ALU.add)
                        last.then_inc(T["shd"], 1)

                maxima(0, 0)
                base = loop_steps(1, QUADS)

                def quad(b, q, final):
                    n = b * 4 + q
                    for half in range(2):
                        v.wait_ge(T["pv"], n * L.U + (L.U + 1 + L.half_end[half]))
                        v.tensor_copy(OSB[:, half * CHUNK:(half + 1) * CHUNK], PS[:, 6 + half, :]).then_inc(T["oev"], 1)
                        if half == 0 and not final:
                            maxima(n + 1, (q + 1) % 2)
                    v.wait_ge(T["t"], n + 1)
                    b0 = 2 * (L.E % 3)
                    res = PS[:, b0:b0 + 2, :].rearrange("p a (k h r) -> p (a k) h r", k=4, h=QH)
                    v.reciprocal(RC[:, :, :], res[:, :, :, cols]).then_inc(dv, 1)
                    v.wait_ge(dv, n + (base + 1))
                    dst = AO[:, bass.ds(b * KT, KT), q * QH * L.hd:(q + 1) * QH * L.hd]
                    v.tensor_tensor(dst.rearrange("p t (h d) -> p t h d", h=QH), res[:, :, :, 0:cols],
                                    RC[:, :, :].unsqueeze(3).broadcast_to([P, KT, QH, cols]), ALU.mult)\
                     .then_inc(T["tr"], 1)

                with v.Fori(0, BATCHES - 1) as b:
                    for q in range(4):
                        quad(b, q, False)
                for q in range(4):
                    quad(BATCHES - 1, q, q == 3)

            def output(a):
                S = po[a]
                credit(S["yd"], 2)
                base = loop_steps(2, CHUNKS // 2)
                with v.Fori(0, CHUNKS // 2) as i:
                    for s in range(2):
                        c = i * 2 + s
                        v.wait_ge(S["m"], c + 3)
                        src = PS[:, 3 * s + 1, :].rearrange("p (t m) -> p t m", t=CT)
                        dst = AO[:, bass.ds(c * CT, CT), :]
                        if a == 0:
                            ins = v.tensor_tensor(dst, src, w["bo0"][:, :].unsqueeze(1).broadcast_to([P, CT, P]), ALU.add)
                        else:
                            ins = v.tensor_scalar(dst, src, 1.0 / 128.0, None, ALU.mult)
                        ins.then_inc(dv, 1)
                        v.wait_ge(dv, i * 2 + (base + s + 1))
                        chunk_stats(AO, 1, c * CT).then_inc(S["yd"], 1)
                v.wait_ge(S["yd"], 2 + CHUNKS)

            def residual(a):
                S = po[a]
                base = loop_steps(1, CHUNKS)

                def front(c, s):
                    v.wait_ge(post[a], c + 1)
                    normalise(lambda q: XN[:, s, q, :], AO, 1, c * CT).then_inc(S["yn"], 1)

                def back(c, s):
                    v.wait_ge(post[a], c + 3)
                    chunk_stats(X, 0, c * CT).then_inc(dv, 1)

                by_chunks(v, front, back, ahead=2)
                v.wait_ge(dv, base + CHUNKS)

            def routed_input(a):
                S = po[a]
                credit(S["yd"], 2)
                E, bias = (E0, w["rb"]) if a == 1 else (E1, None)

                def front(c, s):
                    if a == 3:
                        v.wait_ge(S["tr"], c + 1)
                        normalise(lambda q: XN[:, s, q, :], X, 0, c * CT).then_inc(S["xn"], 1)

                def back(c, s):
                    v.wait_ge(S["y"], c + 3)
                    src = PS[:, 3 * s + 2, 0:CT * E].rearrange("p (t m) -> p t m", t=CT)
                    dst = LG[:, bass.ds(c * CT, CT), 0:E]
                    if bias is not None:
                        ins = v.tensor_tensor(dst, src, bias[:, :].unsqueeze(1).broadcast_to([P, CT, E]), ALU.add)
                    else:
                        ins = v.tensor_copy(dst, src)
                    ins.then_inc(S["yd"], 1)

                by_chunks(v, front, back)
                v.wait_ge(S["yd"], 2 + CHUNKS)

            def rank(dst, val, E):
                step(v.tensor_copy(dst, w["later"][:, E1 - E:E1].unsqueeze(1).broadcast_to([P, TILES, E])))
                for d in range(1, E):
                    n = E - d
                    first = RA[:, 0:TILES * n].rearrange("p (t e) -> p t e", t=TILES)
                    step(v.tensor_tensor(first, val[:, :, 0:n], val[:, :, d:E], ALU.is_ge))
                    step(v.tensor_tensor(dst[:, :, d:E], dst[:, :, d:E], first, ALU.add))
                    step(v.tensor_tensor(dst[:, :, 0:n], dst[:, :, 0:n], first, ALU.subtract))

            def wide(t, E):
                return t[:, :].unsqueeze(2).broadcast_to([P, TILES, E])

            def finish_weights(m, scores, top, eps, E):
                rk, wr = RK[:, :, 0:E], WR[:, :, 0:E]
                step(v.tensor_scalar(rk, rk, top - 0.5, None, ALU.is_lt))
                step(v.tensor_tensor(wr, rk, scores, ALU.mult))
                step(v.tensor_reduce(T1[:, :], wr, AX.X, ALU.add))
                step(v.tensor_scalar(T1[:, :], T1[:, :], eps, None, ALU.add))
                step(v.reciprocal(T2[:, :], T1[:, :]))
                for c in range(CHUNKS):
                    tiles = slice(c * CT, (c + 1) * CT)
                    v.tensor_tensor(AO[:, tiles, :].rearrange("p t (e r) -> p t e r", e=E),
                                    wr[:, tiles, :].unsqueeze(3).broadcast_to([P, CT, E, P // E]),
                                    T2[:, tiles].unsqueeze(2).unsqueeze(3).broadcast_to([P, CT, E, P // E]),
                                    ALU.mult).then_inc(rt[m]["w"], 1)

            def route_softmax():
                lg, sc = LG[:, :, 0:E0], SC[:, :, 0:E0]
                step(v.tensor_reduce(T1[:, :], lg, AX.X, ALU.max))
                v.tensor_tensor(lg, lg, wide(T1, E0), ALU.subtract).then_inc(rt[0]["lg"], CHUNKS + 1)
                v.wait_ge(rt[0]["e"], 1)
                step(v.tensor_reduce(T1[:, :], sc, AX.X, ALU.add))
                step(v.reciprocal(T2[:, :], T1[:, :]))
                step(v.tensor_tensor(sc, sc, wide(T2, E0), ALU.mult))
                rank(RK[:, :, 0:E0], sc, E0)
                finish_weights(0, sc, 2, 1e-8, E0)

            def route_groups():
                v.nop().then_inc(rt[1]["lg"], CHUNKS)
                v.wait_ge(rt[1]["e"], 1)
                step(v.tensor_tensor(LG[:, :, :], SC[:, :, :], w["gb"][:, :].unsqueeze(1).broadcast_to([P, TILES, E1]),
                                     ALU.add))
                grp = LG[:, :, :].rearrange("p t (g k) -> p t g k", g=4)
                pairs = [(i, j) for i in range(4) for j in range(i + 1, 4)]
                for k, (i, j) in enumerate(pairs):
                    step(v.tensor_tensor(G4[0 if k == 0 else 1][:, :, :], grp[:, :, :, i], grp[:, :, :, j], ALU.add))
                    if k:
                        step(v.tensor_tensor(G4[0][:, :, :], G4[0][:, :, :], G4[1][:, :, :], ALU.max))
                rank(G4[2][:, :, :], G4[0][:, :, :], 4)
                step(v.tensor_scalar(G4[2][:, :, :], G4[2][:, :, :], 1.5, None, ALU.is_lt))
                step(v.tensor_tensor(grp, grp, G4[2][:, :, :].unsqueeze(3).broadcast_to([P, TILES, 4, 4]), ALU.mult))
                rank(RK[:, :, :], LG[:, :, :], E1)
                finish_weights(1, SC[:, :, :], 4, 1e-20, E1)

            def experts(m):
                S, T = mo[m], NT[m]
                credit(S["yd"], 2)
                v.wait_ge(rt[m]["wtd"], CHUNKS)
                steps = []

                def finish(c, s, parts):
                    y_ps = PS[:, 4 + s, :]
                    tiles, t0 = bass.ds(c * CT, CT), c * CT

                    def done(ins):
                        steps[-1] += 1
                        ins.then_inc(S["f"], 1)
                        v.wait_ge(S["f"], c * FINISH_STEPS[m] + steps[-1])

                    for part in parts:
                        if part == 0:
                            steps.append(0)
                            if m == 0:
                                done(normalise(lambda q: YN[:, q, :], X, 0, t0))
                        if part == 1:
                            v.wait_ge(S["yt"], c + 2)
                            dst = AO[:, tiles, :].rearrange("p t m -> p (t m)")
                            if m == 0:
                                ins = v.scalar_tensor_tensor(dst, y_ps, 0.3, YN[:, :, :].rearrange("p t m -> p (t m)"),
                                                             ALU.mult, ALU.add)
                            else:
                                ins = v.tensor_copy(dst, y_ps)
                            ins.then_inc(S["yd"], 1)
                            v.wait_ge(S["yd"], c + 3)
                        if part == 2:
                            done(chunk_stats(AO, 1, t0))
                        if part == 3:
                            deviations(1, tiles, CT, done)
                        if part == 4:
                            done(normalise(lambda q: YN[:, q, :], AO, 1, t0))
                        if part == 5:
                            v.tensor_tensor(X[:, tiles, :], X[:, tiles, :], YN[:, :, :], ALU.add)\
                             .then_inc(post[2 * m + 1], 1)
                            if m == 0:
                                v.wait_ge(post[1], c + 1)
                        if part == 6:
                            if m == 0:
                                done(chunk_stats(X, 0, t0))
                            assert steps[-1] == FINISH_STEPS[m]

                def chunk(at, s, first, last):
                    for j in range(T):
                        pos = s * T + j
                        h = HB[:, pos % HRING[m], :]
                        v.wait_ge(S["a"], at(0) * T + (j + 1))
                        if m == 1:
                            v.tensor_tensor(h, h, PS[:, 2 * (pos % 2) + 1, :], ALU.mult)\
                             .then_inc(S["u" if j < ROUTED[m] else "h"], 1)
                            if j < ROUTED[m]:
                                v.wait_ge(S["u"], at(0) * ROUTED[m] + (j + 1))
                        if j < ROUTED[m]:
                            v.tensor_tensor(h, h, WT[:, bass.ds(at(0) * CHUNK, CHUNK)], ALU.mult).then_inc(S["h"], 1)
                        if not first and 4 <= j < 11:
                            finish(at(-1), 1 - s, [j - 4])
                    if last:
                        finish(at(0), s, range(7))

                by_pipelined(v, chunk)

            step(v.memset(SHF[:, :, :, :, :].rearrange("p a b c d -> p (a b c d)"), 0.0))
            v.wait_ge(x_in, 16 * BATCHES)
            base = loop_steps(1, CHUNKS)
            with v.Fori(0, CHUNKS) as c:
                chunk_stats(X, 0, c * CT).then_inc(dv, 1)
            v.wait_ge(dv, n_dv[0])
            finish_stats(0)
            v.wait_ge(w_in, 16 * len(w))
            project(0)
            attention(0)
            output(0)
            finish_stats(1)
            residual(0)
            finish_stats(0)
            project(1)
            attention(1)
            routed_input(1)
            route_softmax()
            experts(0)
            step(v.memset(SHF[:, :, :, :, :].rearrange("p a b c d -> p (a b c d)"), 0.0))
            finish_stats(0)
            project(2)
            attention(2)
            output(2)
            finish_stats(1)
            residual(2)
            finish_stats(0)
            routed_input(3)
            route_groups()
            experts(1)


def host_layout(i):
    bf = np.dtype("bfloat16")
    f = {k: np.asarray(v) for k, v in i.items()}

    def c(a):
        return np.ascontiguousarray(a)

    def row(a, n=P):
        return c(np.broadcast_to(a.reshape(1, -1), (n, a.size)))

    def padded(a, rows, cols):
        out = np.zeros((rows, cols), a.dtype)
        out[0:a.shape[0], 0:a.shape[1]] = a
        return out

    d = {"x": c(f["L0_attn_x"].reshape(TOKENS, DIM))}
    d["ident"] = np.eye(P, dtype=np.float32)
    d["identb"] = np.eye(P, dtype=np.float32).astype(bf)
    lower = np.arange(P)[:, None] > np.arange(P)[None, :]
    d["maskT"] = np.where(lower, np.float32(MASKED), np.float32(0)).astype(bf)
    d["mask"] = np.where(lower.T, np.float32(MASKED), np.float32(0)).astype(bf)
    for hd in (4, 8):
        d[f"blk{hd}"] = (np.arange(P)[:, None] // hd == np.arange(32)[None, :]).astype(bf)
    d["later"] = row(np.arange(E1 - 1, -1, -1).astype(np.float32))
    d["wq0"], d["wk0"] = padded(f["L0_attn_Wq"].T, P, P), padded(f["L0_attn_Wk"].T, P, P)
    d["wv0"], d["wo0"] = padded(f["L0_attn_Wv"].T, P, 64), padded(f["L0_attn_Wo"].T, P, P)
    d["bo0"] = row(f["L0_attn_bo"])
    d["wq1"] = padded(f["L0_ffn_q_w"].reshape(DIM, HEADS, 8)[:, :, 0:4].reshape(DIM, 64), P, P)
    d["qb1"] = padded(f["L0_ffn_q_b"].reshape(HEADS, 8)[:, 0:4].reshape(64, 1), P, 1)
    d["wk1"], d["wv1"] = padded(f["L0_ffn_k_w"], P, P), c(f["L0_ffn_v_w"])
    d["kb1"], d["vb1"] = padded(f["L0_ffn_k_b"].reshape(64, 1), P, 1), row(f["L0_ffn_v_b"])
    d["wo1"], d["ob1"] = padded(f["L0_ffn_o_w"][0:64], P, P), c(f["L0_ffn_o_b"].reshape(P, 1))
    d["rw"], d["rb"] = c(f["L0_ffn_router_w"]), row(f["L0_ffn_router_b"])
    r = P // E0
    d["w1"] = c(f["L0_ffn_w1"].reshape(E0, DIM, NT[0], r).transpose(1, 2, 0, 3).reshape(DIM, NT[0] * P))
    d["b1"] = c(f["L0_ffn_b1"].reshape(E0, NT[0], r).transpose(0, 2, 1).reshape(P, NT[0]))
    w2 = np.zeros((P, NT[0] + 1, P), np.float32)
    w2[:, 0:NT[0]] = f["L0_ffn_w2"].reshape(E0, NT[0], r, P).transpose(0, 2, 1, 3).reshape(P, NT[0], P)
    w2[::r, NT[0]] = f["L0_ffn_b2"]
    d["w2"] = w2
    for n, name in (("wq2", "query"), ("wk2", "key"), ("wv2", "value"), ("wo2", "proj")):
        d[n] = c(f[f"L1_attn_W_{name}"].T)
    d["gw"], d["gb"] = c(f["L1_ffn_gate_w"].T), row(f["L1_ffn_gate_bias"])
    r = P // E1
    for n, routed, shared in (("gp", "gate_proj", "shared_gate_w"), ("up", "up_proj", "shared_up_w")):
        a = np.zeros((DIM, NT[1] * P), np.float32)
        a[:, 0:E1 * I1] = f[f"L1_ffn_{routed}"].reshape(E1, ROUTED[1], r, DIM).transpose(3, 1, 0, 2).reshape(DIM, E1 * I1)
        a[:, E1 * I1:E1 * I1 + SH1] = f[f"L1_ffn_{shared}"].T
        d[n] = a
    a = np.zeros((P, NT[1], P), np.float32)
    a[:, 0:ROUTED[1]] = f["L1_ffn_down_proj"].reshape(E1, P, ROUTED[1], r).transpose(0, 3, 2, 1).reshape(P, ROUTED[1], P)
    shared = padded(f["L1_ffn_shared_down_w"].T, (NT[1] - ROUTED[1]) * P, P)
    a[:, ROUTED[1]:] = shared.reshape(NT[1] - ROUTED[1], P, P).transpose(1, 0, 2)
    d["dp"] = a
    return d


def kernel(**inputs):
    from concourse import bacc
    from concourse.bass_utils import run_bass_kernel_spmd

    arrays = host_layout(inputs)
    nc = bacc.Bacc("TRN2", target_bir_lowering=False, num_devices=1)
    t_in = {n: nc.dram_tensor(f"in_{n}", a.shape, mybir.dt.from_np(a.dtype), kind="ExternalInput").ap()
            for n, a in arrays.items()}
    out = nc.dram_tensor("result", (TOKENS, DIM), FP32, kind="ExternalOutput").ap()
    build_program(nc, t_in, out)
    r = run_bass_kernel_spmd(nc, [{f"in_{n}": a for n, a in arrays.items()}], core_ids=[0])
    return r.results[0]["result"].reshape(BATCHES, SEQ, DIM)
```

```python
import numpy as np
import concourse.bass as bass
from concourse import mybir
from contextlib import ExitStack

FP32 = mybir.dt.float32
BF16 = mybir.dt.bfloat16
I32 = mybir.dt.int32
ALU = mybir.AluOpType
ACT = mybir.ActivationFunctionType
AX = mybir.AxisListType

P = 128
BATCHES, SEQ, DIM = 4, 1024, 128
TOKENS = BATCHES * SEQ
TILES = TOKENS // P
CT = 4
CHUNK = CT * P
CHUNKS = TOKENS // CHUNK
KT = SEQ // P
HEADS = 16
QH = 4
QUADS = HEADS // QH * BATCHES
EPS = 1e-5
RANGE = 58.0
TERMS = 8
Q_TERMS = (slice(0, 3), slice(3, 6, 2), slice(4, 5))
K_TERMS = (slice(2, 5), slice(1, 6, 4), slice(0, 1))
MASKED = -1e30
FIRST = ("ident", "wq0", "wk0", "wv0", "blk4")
T_PLACE = 2
RING = 4


class Attn:

    def __init__(self, hd, scale, causal, biased):
        self.hd, self.scale, self.causal, self.biased = hd, scale, causal, biased
        self.M = HEADS * hd
        self.slots = QH * hd * TERMS // P
        self.hps = QH // self.slots
        if causal:
            order = [[(1, 0)], [(0, 0)], [(1, 1)], [(0, 1), (0, 3)], [(1, 2)], [(0, 2), (1, 6)], [(1, 3)],
                     [(1, 5), (1, 7)], [(1, 4)]]
        else:
            order = [[(half, kt)] for half in range(2) for kt in range(KT)]
        self.units = []
        for pieces in order:
            unit, col = [], 0
            for half, kt in pieces:
                off = max(0, kt * P - half * CHUNK) if causal else 0
                unit.append((half, kt, off, col, causal and kt * P >= half * CHUNK))
                col += CHUNK - off
            assert col == CHUNK
            self.units.append(unit)
        self.U = len(self.units)
        self.E = 2 * self.U
        self.ring = 4 if self.U % 4 == 0 else 3
        where = [[u for u in range(self.U) for piece in self.units[u] if piece[0] == h] for h in range(2)]
        self.half_start = [min(us) for us in where]
        self.half_end = [max(us) + 1 for us in where]
        self.period = -(-(self.E + 1) // 3) * 3

    def place(self, e):
        k = (e - 4) % self.E
        return k if k < T_PLACE else k + 1

    def before(self, place):
        turn, q = 0, place - 3
        if q < 0:
            turn, q = 1, q + self.period
            while q > self.E:
                q -= 3
        return turn, "t" if q == T_PLACE else q if q < T_PLACE else q - 1


LAYERS = [Attn(4, float(8) ** -0.5, False, False), Attn(4, 0.5, False, True),
          Attn(8, float(8) ** -0.5 / 128.0, True, False)]

E0, I0 = 8, 256
E1, I1, SH1 = 16, 176, 352
ROUTED = (E0 * I0 // P, E1 * I1 // P)
NT = (ROUTED[0], ROUTED[1] + -(-SH1 // P))
BANKS = (4, 2)
HRING = (4, 5)
LOOK = 2
MAGIC = 0x5F3759DF
FINISH_STEPS = (19, 17)


def by_chunks(eng, front, back, ahead=1):
    for c in range(ahead):
        front(c, c % 2)
    with eng.Fori(0, CHUNKS // 2 - 1) as i:
        for s in range(2):
            front(i * 2 + (s + ahead), (s + ahead) % 2)
            back(i * 2 + s, s)
    for c in range(CHUNKS - 2, CHUNKS):
        if c + ahead < CHUNKS:
            front(c + ahead, (c + ahead) % 2)
        back(c, c % 2)


def by_pipelined(eng, chunk):
    chunk(lambda k: k, 0, True, False)
    with eng.Fori(0, CHUNKS // 2 - 1) as i:
        for s in (1, 0):
            chunk(lambda k: i * 2 + (2 - s + k), s, False, False)
    chunk(lambda k: CHUNKS - 1 + k, 1, False, True)


def build_program(nc, t_in, out):
    ctx = ExitStack()
    with ctx:
        def sb(name, shape, dt=FP32):
            return ctx.enter_context(nc.sbuf_tensor(name, shape, dt))

        def sem(name):
            return ctx.enter_context(nc.semaphore(name))

        X = sb("X", [P, TILES, DIM])
        AO = sb("AO", [P, TILES, DIM])
        KG = [sb(f"KG{s}", [P, QH, SEQ], BF16) for s in range(2)]
        QG = [sb(f"QG{s}", [P, 2, SEQ], BF16) for s in range(2)]
        VG = [sb(f"VG{s}", [P, KT, QH, 32]) for s in range(2)]
        VT = sb("VT", [P, TILES, DIM])
        PR = sb("PR", [P, RING, QH, CHUNK])
        OSB = sb("OSB", [P, SEQ])
        XN = sb("XN", [P, 2, CT, DIM])
        XT = sb("XT", [P, 2, CHUNK])
        MTS = sb("MTS", [P, 2, CHUNK])
        WARM = sb("WARM", [1, 1])
        NB = sb("NB", [64, CHUNKS])
        NBM = sb("NBM", [64, 1])
        NBR = sb("NBR", [1, 64])
        NBP = sb("NBP", [1, 32])
        NBX = sb("NBX", [1, 1])
        FLAG = sb("FLAG", [1, len(LAYERS)], I32)
        ST = [sb(f"ST{k}", [P, TILES, 6]) for k in range(2)]
        MEAN = [sb(f"MEAN{k}", [P, TILES]) for k in range(2)]
        RSTD = [sb(f"RSTD{k}", [P, TILES]) for k in range(2)]
        TMP = [sb(f"TMP{k}", [P, TILES]) for k in range(4)]
        SHIFT = sb("SHIFT", [P, TILES])
        RC = sb("RC", [P, KT, QH])
        MX = sb("MX", [P, KT, QH])
        MXP = sb("MXP", [P, KT, QH], BF16)
        SHF = sb("SHF", [P, 2, KT, 16, TERMS], BF16)
        LG = sb("LG", [P, TILES, E1])
        WR = sb("WR", [P, TILES, E1])
        SC = sb("SC", [P, TILES, E1])
        RK = sb("RK", [P, TILES, E1])
        G4 = [sb(f"G4{k}", [P, TILES, 4]) for k in range(3)]
        TOP8 = sb("TOP8", [P, TILES, 8])
        T1 = sb("T1", [P, TILES])
        T2 = sb("T2", [P, TILES])
        YN = sb("YN", [P, CT, DIM])
        flat = PR[:, :, :, :].rearrange("p a b c -> p (a b c)")
        MT = flat[:, 0:TOKENS]
        HB = flat[:, TOKENS:2 * TOKENS].rearrange("p (a n) -> p a n", n=CHUNK)
        WT = VT[:, :, :].rearrange("p a b -> p (a b)")
        OT = OSB[:, 0:CHUNK]
        QKF = flat[:, 0:2048].rearrange("p (s a n) -> p s a n", s=2, a=2)
        SQ = flat[:, 2048:3072].bitcast(BF16).rearrange("p (s a n) -> p s a n", s=2, a=2)
        PT = flat[:, 3072:6144].bitcast(BF16).rearrange("p (s t a n) -> p s t a n", s=2, t=3, a=2)
        aof = AO[:, :, :].rearrange("p a b -> p (a b)")
        CONST0 = aof[:, 0:TOKENS // 2].bitcast(BF16)
        CONST1 = aof[:, TOKENS // 2:TOKENS].bitcast(BF16)
        RA = VT[:, :, :].rearrange("p a b -> p (a b)")[:, 0:2048]
        PS = ctx.enter_context(nc.psum_tensor("PS", [P, 8, CHUNK], FP32))

        w = {}
        for name, (shape, dt) in {
            "ident": ([P, P], FP32), "identb": ([P, P], BF16), "maskT": ([P, P], BF16), "mask": ([P, P], BF16),
            "blk4": ([P, 32], BF16), "blk8": ([P, 32], BF16), "later": ([P, E1], FP32),
            "wq0": ([P, P], FP32), "wk0": ([P, P], FP32), "wv0": ([P, 64], FP32), "wo0": ([P, P], FP32),
            "bo0": ([P, P], FP32),
            "wq1": ([P, P], FP32), "wk1": ([P, P], FP32), "wv1": ([P, 64], FP32), "qb1": ([P, 1], FP32),
            "kb1": ([P, 1], FP32), "vb1": ([P, 64], FP32), "wo1": ([P, P], FP32), "ob1": ([P, 1], FP32),
            "rw": ([P, E0], FP32), "rb": ([P, E0], FP32), "b1": ([P, NT[0]], FP32),
            "wq2": ([P, P], FP32), "wk2": ([P, P], FP32), "wv2": ([P, P], FP32), "wo2": ([P, P], FP32),
            "gw": ([P, E1], FP32), "gb": ([P, E1], FP32),
        }.items():
            w[name] = sb(name, shape, dt)
        n0, n1 = NT[0] * P, NT[1] * P
        MW = sb("MW", [P, 3 * n1])
        experts0 = {"w1": MW[:, 0:n0], "w2": MW[:, n0:2 * n0 + P].rearrange("p (j n) -> p j n", j=NT[0] + 1)}
        experts1 = {"gp": MW[:, 0:n1], "up": MW[:, n1:2 * n1],
                    "dp": MW[:, 2 * n1:3 * n1].rearrange("p (j n) -> p j n", j=NT[1])}
        QD = nc.dram_tensor("q_rows", [P, TERMS, TOKENS], BF16, kind="Internal").ap()
        KD = nc.dram_tensor("k_rows", [P, TERMS, TOKENS], BF16, kind="Internal").ap()
        QDR = QD.rearrange("r t n -> (r t) n")
        KDR = KD.rearrange("r t n -> (r t) n")

        x_in = [sem(f"x_in{b}") for b in range(2)]
        w_first = sem("w_first")
        w_in = sem("w_in")
        e0_in, e1_in = sem("e0_in"), sem("e1_in")
        consts_set = sem("consts_set")
        consts_out = sem("consts_out")
        dv = sem("dv")
        out_done = sem("out_done")
        flag_col, flag_row, flag_set = sem("flag_col"), sem("flag_row"), sem("flag_set")

        def many(prefix, names):
            return {n: sem(f"{prefix}_{n}") for n in names.split()}

        pj = [many(f"pj{a}", "xn tr xt qk qkv sq ev vev nrm nb split") for a in range(3)]
        at = [many(f"at{a}", "s exp pv qg0 qg1 v oev t tr mxr mxd sh sht shd mxs") for a in range(3)]
        po = [many(f"po{a}", names) for a, names in enumerate(
            ("xn tr xt m yd yn", "xn tr xt m mt y yd", "xn tr xt m yd yn", "xn tr mt y yd"))]
        cleared = sem("cleared")
        moments = sem("moments")
        first_out = [sem(f"first_out{s}") for s in range(2)]
        rest_out = [sem(f"rest_out{s}") for s in range(2)]
        rt = [many(f"rt{a}", "lg e w wt wtd") for a in range(2)]
        mo = [many(f"mo{a}", "g a u h dn oe yt yd f") for a in range(2)]
        post = [sem(f"post{a}") for a in range(4)]
        block = ctx.enter_context(nc.Block())

        @block.sync
        def _(sp):
            x_v = t_in["x"].rearrange("(t p) c -> p t c", p=P)
            for b in range(BATCHES):
                sp.dma_start(X[:, b * KT:(b + 1) * KT, :], x_v[:, b * KT:(b + 1) * KT, :]).then_inc(x_in[b // 2], 16)
            for name in list(FIRST) + [n for n in w if n not in FIRST]:
                t = w[name]
                sp.dma_start(t[tuple(slice(None) for _ in t.shape)], t_in[name])\
                  .then_inc(w_first if name in FIRST else w_in, 16)
            for name, t in experts0.items():
                sp.dma_start(t, t_in[name]).then_inc(e0_in, 16)
            for s in range(2):
                sp.nop().then_inc(first_out[s], 16)
                sp.nop().then_inc(rest_out[s], 16)
            sp.wait_ge(consts_set, 3)
            for t in (6, 7):
                sp.dma_start(QD[:, t, :], CONST0).then_inc(consts_out, 16)
                sp.dma_start(KD[:, t, :], CONST1).then_inc(consts_out, 16)
            for a, L in enumerate(LAYERS):
                S, T = pj[a], at[a]
                if a:
                    for s in range(2):
                        sp.wait_ge(at[a - 1][f"qg{s}"], 16 * (QUADS // 2) * (LAYERS[a - 1].slots + QH))

                def store(c, s):
                    col = bass.ds(c * CHUNK, CHUNK)
                    for part in range(3):
                        if part == 0:
                            sp.wait_ge(S["ev"], c + 3)
                        if part == 1:
                            sp.wait_ge(S["split"], c + 3)
                        for n, (rows_of, terms) in enumerate(((QD, Q_TERMS[part]), (KD, K_TERMS[part]))):
                            count = len(range(TERMS)[terms])
                            sp.dma_start(rows_of[0:L.M, terms, col],
                                         PT[0:L.M, s, part:part + 1, n, :].broadcast_to([L.M, count, CHUNK]))\
                              .then_inc((rest_out if part else first_out)[s], 16)

                def stored(chunks):
                    for s in range(2):
                        sp.wait_ge(first_out[s], 16 + (a * CHUNKS + chunks) * 16)
                        sp.wait_ge(rest_out[s], 16 + (a * CHUNKS + chunks) * 32)

                rows = L.hd * TERMS

                def load(b, quad, s):
                    if not (isinstance(b, int) and quad < 2):
                        sp.wait_ge(T["s"], (b * 4 + quad) * L.E + 1)
                    col = bass.ds(b * SEQ, SEQ)
                    for k in range(L.slots):
                        sp.dma_start(QG[s][:, k, :], QDR[bass.ds((quad * L.slots + k) * P, P), col])\
                          .then_inc(T[f"qg{s}"], 16)
                    for h in range(QH):
                        r0 = (h % L.hps) * rows
                        sp.dma_start(KG[s][r0:r0 + rows, h, :],
                                     KDR[bass.ds(quad * QH * rows + h * rows, rows), col])\
                          .then_inc(T[f"qg{s}"], 16)

                with sp.Fori(0, CHUNKS // 2 - 1) as i:
                    for s in range(2):
                        store(i * 2 + s, s)
                if a == 0:
                    sp.wait_ge(consts_out, 64)
                else:
                    sp.wait_ge(at[a - 1]["s"], (1 + QUADS) * LAYERS[a - 1].E + 1)
                sp.wait_ge(consts_set, 3 + (1 if a < 2 else 2))
                stored(2)
                load(0, 0, 0)
                for c in range(CHUNKS - 2, CHUNKS):
                    store(c, c % 2)
                load(0, 1, 1)
                stored(CHUNKS)
                for quad in range(2, 4):
                    load(0, quad, quad % 2)
                    if a == 2 and quad == 2:
                        sp.wait_ge(mo[0]["dn"], HRING[0] + CHUNKS * NT[0])
                        for name, t in experts1.items():
                            sp.dma_start(t, t_in[name]).then_inc(e1_in, 16)
                with sp.Fori(1, BATCHES) as b:
                    with sp.Fori(0, 2) as p:
                        for s in range(2):
                            load(b, p * 2 + s, s)
            o_v = out.rearrange("(t p) c -> p t c", p=P)
            for c in range(CHUNKS):
                sp.wait_ge(post[3], c + 1)
                sp.dma_start(o_v[:, c * CT:(c + 1) * CT, :], X[:, c * CT:(c + 1) * CT, :]).then_inc(out_done, 16)
            sp.wait_ge(out_done, 16 * CHUNKS)

        @block.gpsimd
        def _(pool):
            pool.memset(CONST0, 0.0)
            pool.memset(CONST1, 1.0).then_inc(consts_set, 3)
            for s in range(2):
                pool.memset(KG[s][:, :, :], 0.0)
                pool.memset(VG[s][:, :, :, :], 0.0).then_inc(cleared, 1)
            pool.wait_ge(cleared, 2)
            for s in range(2):
                last = pool.memset(VG[s][:, :, :, 4:5], 1.0)
            last.then_inc(consts_set, 1)
            for a, L in enumerate(LAYERS):
                S, T = pj[a], at[a]
                if a == 2:
                    pool.wait_ge(at[1]["s"], (1 + QUADS) * LAYERS[1].E + 1)
                    pool.wait_ge(at[1]["pv"], (1 + QUADS) * LAYERS[1].U + 1)
                    for s in range(2):
                        pool.memset(KG[s][:, :, :], 0.0)
                        pool.memset(VG[s][:, :, :, :], 0.0).then_inc(cleared, 1)
                    pool.wait_ge(cleared, 4)
                    for s in range(2):
                        last = pool.memset(VG[s][:, :, :, 8:9], 1.0)
                    last.then_inc(consts_set, 1)

                def values(b, quad, s):
                    src = VT[:, bass.ds(b * KT, KT), bass.ds(quad * QH * L.hd, QH * L.hd)]
                    pool.tensor_copy(VG[s][:, :, :, 0:L.hd],
                                     src.rearrange("p t (h d) -> p t h d", h=QH)).then_inc(T["v"], 1)

                if a:
                    pool.wait_ge(at[a - 1]["pv"], (1 + QUADS) * LAYERS[a - 1].U + 1)
                pool.wait_ge(S["vev"], 2 + 2)
                values(0, 0, 0)
                values(0, 1, 1)
                pool.wait_ge(S["vev"], 2 + CHUNKS)
                for s in range(2):
                    pool.wait_ge(T["pv"], (2 + s) * L.U + 1)
                    values(0, 2 + s, s)
                with pool.Fori(1, BATCHES) as b:
                    with pool.Fori(0, 2) as p:
                        for s in range(2):
                            pool.wait_ge(T["pv"], (b * 4 + p * 2 + s) * L.U + 1)
                            values(b, p * 2 + s, s)
                S = po[a]
                pool.wait_ge(T["tr"], QUADS + 1)
                if L.M < P:
                    pool.memset(XN[:, :, :, L.M:P], 0.0)
                def front(c, s):
                    pool.wait_ge(S["tr"], c + 1)
                    pool.tensor_copy(XN[:, s, :, 0:L.M], AO[:, bass.ds(c * CT, CT), 0:L.M]).then_inc(S["xn"], 1)

                for c in range(2):
                    front(c, c)
                with pool.Fori(0, CHUNKS // 2 - 1) as i:
                    for s in range(2):
                        front(i * 2 + (s + 2), s)
                if a != 1:
                    pool.nop().then_inc(post[a], 2)
                    with pool.Fori(0, CHUNKS // 2) as i:
                        for s in range(2):
                            c = i * 2 + s
                            pool.wait_ge(S["yn"], c + 1)
                            xs = X[:, bass.ds(c * CT, CT), :]
                            pool.tensor_tensor(xs, xs, XN[:, s, :, :], ALU.add).then_inc(post[a], 1)
        @block.scalar
        def _(act):
            def credit(s, n):
                act.nop().then_inc(s, n)

            def project(a):
                L, S = LAYERS[a], pj[a]
                for name in ("sq", "ev") if L.biased else ("sq", "ev", "vev"):
                    credit(S[name], 2)

                def transposed(c, s):
                    act.wait_ge(S["tr"], c + 3)
                    act.wait_ge(S["qkv"], c + 1)
                    act.activation(XT[:, s, :], PS[:, 4 * s, :], ACT.Copy).then_inc(S["xt"], 1)

                def chunk(at, s, first, last):
                    c = at(0)
                    if first:
                        transposed(c, s)
                    act.wait_ge(S["nrm"], c + 1)
                    act.wait_ge(S["split"], c + 1)
                    for n, bias in enumerate(("qb1", "kb1")):
                        b = w[bias][:, 0:1] if L.biased else 0.0
                        act.wait_ge(S["qk"], c * 2 + (n + 1))
                        ins = act.activation(SQ[:, s, n, :], PS[:, 4 * s + 1 + n, :], ACT.Square, bias=b)
                        if n:
                            ins.then_inc(S["sq"], 1)
                        act.activation(QKF[:, s, n, :], PS[:, 4 * s + 1 + n, :], ACT.Identity, bias=b)
                        if n == 0:
                            act.wait_ge(first_out[s], (c - s) * 16 + (16 + a * CHUNKS * 16))
                        if L.biased:
                            last_part = act.activation(PT[:, s, 0, n, :], PS[:, 4 * s + 1 + n, :], ACT.Identity, bias=b)
                    if not L.biased:
                        last_part = act.activation(PT[:, s, 0, :, :], PS[:, 4 * s + 1:4 * s + 3, :], ACT.Copy)
                    last_part.then_inc(S["ev"], 1)
                    if not last:
                        transposed(at(1), 1 - s)
                    if not L.biased:
                        act.wait_ge(S["qkv"], c + 3)
                        act.activation(VT[:, bass.ds(c * CT, CT), 0:L.M],
                                       PS[:, 4 * s + 3, 0:CT * L.M].rearrange("p (t m) -> p t m", t=CT),
                                       ACT.Copy).then_inc(S["vev"], 1)

                by_pipelined(act, chunk)

            def residual(a, use):
                S = po[a]
                act.wait_ge(moments, use)
                with act.Fori(0, CHUNKS // 2) as i:
                    for s in range(2):
                        c = i * 2 + s
                        act.wait_ge(post[a], c + 1)
                        for q in range(CT):
                            t = bass.ds(c * CT + q, 1)
                            last = act.activation(XN[:, s, q, :], AO[:, t, :].rearrange("p a c -> p (a c)"), ACT.Identity,
                                                  bias=SHIFT[:, t], scale=RSTD[1][:, t])
                        last.then_inc(S["yn"], 1)

            def softmax(a):
                L, T = LAYERS[a], at[a]
                act.activation(WARM[:, :], WARM[:, :], ACT.Exp)
                for s in range(2):
                    act.wait_ge(first_out[s], 16 + (a + 1) * CHUNKS * 16)
                    act.wait_ge(rest_out[s], 16 + (a + 1) * CHUNKS * 32)
                credit(T["exp"], L.E)
                with act.Fori(0, QUADS) as n:
                    for u in range(L.U):
                        for g in range(2):
                            e = 2 * u + g
                            act.wait_ge(T["s"], n * L.E + (e + 2 + L.E))
                            if g == 0:
                                act.wait_ge(T["pv"], n * L.U + (u + 2 - L.ring + L.U))
                            slot = L.place(e) % 3
                            act.activation(PR[:, u % L.ring, 2 * g:2 * g + 2, :], PS[:, 2 * slot:2 * slot + 2, :],
                                           ACT.Exp, scale=L.scale).then_inc(T["exp"], 1)

            def after_attention(a):
                S = po[a]
                for name in ("xt", "mt"):
                    if name in S:
                        credit(S[name], 2)

                def front(c, s):
                    act.wait_ge(S["tr"], c + 3)
                    act.wait_ge(S["m"], c + 1)
                    act.activation(XT[:, s, :], PS[:, 3 * s, :], ACT.Copy).then_inc(S["xt"], 1)

                def back(c, s):
                    src = PS[:, 3 * s + (1 if a == 1 else 0), :]
                    act.wait_ge(S["m"] if a == 1 else S["tr"], c + 3)
                    act.wait_ge(S["y"], c + 1)
                    bias = w["ob1"][:, 0:1] if a == 1 else 0.0
                    act.activation(MT[:, bass.ds(c * CHUNK, CHUNK)], src, ACT.Identity, bias=bias)
                    act.activation(MTS[:, s, :], src, ACT.Identity, bias=bias).then_inc(S["mt"], 1)

                if a == 1:
                    by_chunks(act, front, back)
                else:
                    with act.Fori(0, CHUNKS // 2) as i:
                        for s in range(2):
                            (back if a == 3 else front)(i * 2 + s, s)

            def experts(m):
                S, T = mo[m], NT[m]
                credit(S["oe"], 2)

                def output(c, s):
                    act.wait_ge(S["dn"], c * T + (T + HRING[m]))
                    act.wait_ge(S["yt"], c + 1)
                    act.activation(OT, PS[:, 6 + s, :], ACT.Copy).then_inc(S["oe"], 1)

                def chunk(at, s, first, last):
                    for j in range(T):
                        pos = s * T + j
                        act.wait_ge(S["g"], at(0) * T + (j + 1))
                        act.wait_ge(S["dn"], at(0) * T + (j + 1))
                        h = HB[:, pos % HRING[m], :]
                        if m == 0:
                            act.activation(h, PS[:, pos % 4, :], ACT.Gelu, bias=w["b1"][:, j:j + 1]).then_inc(S["a"], 1)
                        else:
                            act.activation(h, PS[:, 2 * (pos % 2), :], ACT.Silu).then_inc(S["a"], 1)
                        if j == LOOK - 1 and not first:
                            output(at(-1), 1 - s)
                    if last:
                        output(at(0), s)

                by_pipelined(act, chunk)

            def weights(m):
                S = rt[m]
                for c in range(CHUNKS):
                    act.wait_ge(S["wt"], c + 1)
                    act.activation(WT[:, c * CHUNK:(c + 1) * CHUNK], PS[:, c, :], ACT.Copy).then_inc(S["wtd"], 1)

            project(0)
            act.wait_ge(dv, 1)
            act.wait_ge(w_in, 16 * (len(w) - len(FIRST)))
            softmax(0)
            after_attention(0)
            residual(0, 2)
            project(1)
            softmax(1)
            after_attention(1)
            act.wait_ge(rt[0]["lg"], CHUNKS + 1)
            act.activation(SC[:, :, 0:E0], LG[:, :, 0:E0], ACT.Exp).then_inc(rt[0]["e"], 1)
            weights(0)
            experts(0)
            project(2)
            softmax(2)
            after_attention(2)
            residual(2, 5)
            after_attention(3)
            act.wait_ge(rt[1]["lg"], CHUNKS)
            act.activation(SC[:, :, :], LG[:, :, :], ACT.Sigmoid).then_inc(rt[1]["e"], 1)
            weights(1)
            experts(1)

        @block.tensor
        def _(pe):
            def credit(s, n):
                pe.nop().then_inc(s, n)

            def transposes(dst_bank, s):
                for k in range(CT):
                    last = pe.transpose(PS[:, dst_bank, k * P:(k + 1) * P], XN[:, s, k, :], w["ident"][:, :])
                return last

            def project(a):
                L, S = LAYERS[a], pj[a]
                for name in ("tr", "qkv", "nrm"):
                    credit(S[name], 2)
                blk = w["blk4"] if L.hd == 4 else w["blk8"]

                def transposed(c, s):
                    pe.wait_ge(S["xn"], c + 1)
                    pe.wait_ge(S["nb"], c + 1)
                    transposes(4 * s, s).then_inc(S["tr"], 1)

                def chunk(at, s, first, last):
                    c = at(0)
                    if first:
                        transposed(c, s)
                    pe.wait_ge(S["xt"], c + 1)
                    pe.wait_ge(S["ev"], c + 1)
                    for n, name in enumerate(("wq", "wk")):
                        pe.matmul(PS[:, 4 * s + 1 + n, :], w[f"{name}{a}"][:, :], XT[:, s, :],
                                  start=True, stop=True).then_inc(S["qk"], 1)
                    if not last:
                        transposed(at(1), 1 - s)
                    pe.wait_ge(S["vev"], c + 1)
                    for k in range(CT):
                        ins = pe.matmul(PS[:, 4 * s + 3, k * L.M:(k + 1) * L.M],
                                        XT[:, s, k * P:(k + 1) * P], w[f"wv{a}"][:, :],
                                        start=True, stop=True)
                    ins.then_inc(S["qkv"], 1)
                    pe.wait_ge(S["sq"], c + 3)
                    for n in range(2):
                        ins = pe.matmul(PS[32 * n:32 * n + 32, 4 * s, :], blk[:, :], SQ[:, s, n, :],
                                        start=True, stop=True)
                    ins.then_inc(S["nrm"], 1)

                by_pipelined(pe, chunk)
                pe.wait_ge(flag_col, a + 1)
                pe.transpose(PS[0:1, 0, 0:64], NBM[:, :], w["ident"][0:64, 0:64]).then_inc(flag_row, 1)
                pe.wait_ge(S["ev"], CHUNKS + 2)
                pe.wait_ge(S["vev"], CHUNKS + 2)
                pe.wait_ge(S["nb"], CHUNKS + 2)

            def attention(a):
                L, T = LAYERS[a], at[a]
                credit(T["pv"], L.U + 1)
                credit(T["sht"], 1)
                credit(T["s"], L.E + 1)
                pe.wait_ge(flag_set, a + 1)
                flag = pe.value_load(FLAG[0:1, a:a + 1], min_val=0, max_val=1)

                def exp_done(n, k):
                    pe.wait_ge(T["exp"], n * L.E + (4 + k + 1 + L.E))

                def free_slot(n, place, first):
                    turn, what = L.before(place)
                    if what == "t":
                        pe.wait_ge(T["tr"], n + 1)
                        if first:
                            free_slot(n, T_PLACE, first)
                    elif turn:
                        pe.wait_ge(T["exp"], n * L.E + (4 + what + 1))
                    else:
                        exp_done(n, what)

                def maxima(n, s):
                    with pe.If(flag > 0):
                        pe.wait_ge(T["exp"], n * L.E + L.E)
                        for h in range(QH):
                            for qc in range(KT):
                                r = h * KT + qc
                                b0 = 2 * (r % 3)
                                if r >= 3:
                                    pe.wait_ge(T["mxd"], n * (QH * KT) + (r - 2))
                                keys = (qc + 1) * P if L.causal else SEQ
                                for k0 in range(0, keys, CHUNK):
                                    width = min(CHUNK, keys - k0)
                                    diag = L.causal and k0 + width == keys
                                    bank, queries = b0 + k0 // CHUNK, QG[s][:, h // L.hps, qc * P:(qc + 1) * P]
                                    plain = width - P if diag else width
                                    if plain:
                                        last = pe.matmul(PS[:, bank, 0:plain], queries, KG[s][:, h, k0:k0 + plain],
                                                         start=True, stop=True)
                                    if diag:
                                        pe.matmul(PS[:, bank, plain:width], queries, KG[s][:, h, k0 + plain:k0 + width],
                                                  start=True, stop=False)
                                        last = pe.matmul(PS[:, bank, plain:width], w["identb"][:, :], w["mask"][:, :],
                                                         start=False, stop=True)
                                last.then_inc(T["mxr"], 1)
                        pe.wait_ge(T["sh"], n + 1)
                        for k in range(L.slots):
                            sh = PS[:, 2 * k, :].bitcast(BF16)
                            for qc in range(KT):
                                last = pe.transpose(sh[:, qc * P:(qc + 1) * P],
                                                    SHF[:, k, qc, :, :].rearrange("p r t -> p (r t)"),
                                                    w["identb"][:, :])
                        last.then_inc(T["sht"], 1)
                        pe.wait_ge(T["shd"], n + 1)

                def scores(n, s, u):
                    for h in range(QH):
                        e = 2 * u + h // 2
                        slot = L.place(e) % 3
                        yield h, e
                        bank, queries = 2 * slot + h % 2, QG[s][:, h // L.hps, :]
                        for half, kt, off, col, diag in L.units[u]:
                            keys = KG[s][:, h, kt * P:(kt + 1) * P]
                            q0, end = half * CHUNK + off, col + CHUNK - off
                            if diag:
                                pe.matmul(PS[:, bank, col:col + P], keys, queries[:, q0:q0 + P], start=True, stop=False)
                                last = pe.matmul(PS[:, bank, col:col + P], w["identb"][:, :], w["maskT"][:, :],
                                                 start=False, stop=True)
                                col, q0 = col + P, q0 + P
                            if col < end:
                                last = pe.matmul(PS[:, bank, col:end], keys, queries[:, q0:(half + 1) * CHUNK],
                                                 start=True, stop=True)
                        if h % 2:
                            last.then_inc(T["s"], 1)

                def products(n, s, u):
                    pe.wait_ge(T["exp"], n * L.E + (2 * u + 2 + L.E))
                    for half, kt, off, col, diag in L.units[u]:
                        if u == L.half_start[half]:
                            pe.wait_ge(T["oev"], n * 2 + (half + 1))
                        for h in range(QH):
                            last = pe.matmul(PS[32 * h:32 * h + 32, 6 + half, off:CHUNK], VG[s][:, kt, h, :],
                                             PR[:, u % L.ring, h, col:col + CHUNK - off],
                                             start=(u == L.half_start[half]), stop=(u + 1 == L.half_end[half]),
                                             skip_group_check=True, tile_position=(0, 32 * h))
                    last.then_inc(T["pv"], 1)

                def output(n):
                    pe.wait_ge(T["oev"], n * 2 + 4)
                    for k in range(KT):
                        last = pe.transpose(PS[:, 2 * T_PLACE + k // 4, (k % 4) * P:(k % 4 + 1) * P],
                                            OSB[:, k * P:(k + 1) * P], w["ident"][:, :])
                    last.then_inc(T["t"], 1)

                def quad(at, s, first, final):
                    n = at(0)
                    pe.wait_ge(T["v"], n + 1)
                    for u in range(L.U):
                        products(n, s, u)
                        nxt = u + 2 >= L.U
                        if nxt and final:
                            continue
                        if u + 2 == L.U:
                            pe.wait_ge(T[f"qg{1 - s}"], (n + (2 + s)) * (per // 2))
                            maxima(n + 1, 1 - s)
                        for h, e in scores(n, 1 - s if nxt else s, (u + 2) % L.U):
                            if h % 2 == 0:
                                free_slot(n, L.place(e), first)
                        if u == 0 and not first:
                            free_slot(n, T_PLACE, first)
                            output(at(-1))

                per = 16 * (L.slots + QH)
                pe.wait_ge(T["qg0"], per)
                maxima(0, 0)
                for u in range(2):
                    for h, e in scores(0, 0, u):
                        if e == 3 and h % 2 == 0:
                            pe.wait_ge(T["exp"], 1 + L.E)
                quad(lambda k: k, 0, True, False)
                with pe.Fori(0, QUADS // 2 - 1) as i:
                    for s in (1, 0):
                        quad(lambda k: i * 2 + (2 - s + k), s, False, False)
                quad(lambda k: QUADS - 1 + k, 1, False, True)
                pe.wait_ge(T["exp"], QUADS * L.E + L.E)
                output(QUADS - 1)
                pe.wait_ge(T["tr"], QUADS + 1)

            def output(a):
                L, S = LAYERS[a], po[a]
                credit(S["tr"], 2)
                credit(S["m"], 2)

                def front(c, s):
                    pe.wait_ge(S["xn"], c + 1)
                    pe.wait_ge(S["xt"], c + 1)
                    transposes(3 * s, s).then_inc(S["tr"], 1)

                def back(c, s):
                    pe.wait_ge(S["xt"], c + 3)
                    pe.wait_ge(S["yd"], c + 1)
                    for k in range(CT):
                        last = pe.matmul(PS[:, 3 * s + 1, k * P:(k + 1) * P], XT[:, s, k * P:(k + 1) * P],
                                         w[f"wo{a}"][:, :], start=True, stop=True)
                    last.then_inc(S["m"], 1)

                by_chunks(pe, front, back)
                pe.wait_ge(S["yd"], CHUNKS + 2)

            def routed_input(a):
                S = po[a]
                credit(S["tr"], 2)
                if a == 1:
                    credit(S["m"], 2)
                credit(S["y"], 2)
                E, rw = (E0, w["rw"]) if a == 1 else (E1, w["gw"])

                def transposed(c, s):
                    pe.wait_ge(S["xn"], c + 1)
                    pe.wait_ge(S["xt"] if a == 1 else S["mt"], c + 1)
                    transposes(3 * s, s).then_inc(S["tr"], 1)

                def projected(c, s):
                    pe.wait_ge(S["xt"], c + 3)
                    pe.wait_ge(S["mt"], c + 1)
                    pe.matmul(PS[:, 3 * s + 1, :], w["wo1"][:, :], XT[:, s, :],
                              start=True, stop=True).then_inc(S["m"], 1)

                def logits(c, s):
                    pe.wait_ge(S["mt"], c + 3)
                    pe.wait_ge(S["yd"], c + 1)
                    for k in range(CT):
                        last = pe.matmul(PS[:, 3 * s + 2, k * E:(k + 1) * E], MTS[:, s, k * P:(k + 1) * P],
                                         rw[:, :], start=True, stop=True)
                    last.then_inc(S["y"], 1)

                if a == 1:
                    transposed(0, 0)

                    def front(c, s):
                        if isinstance(c, int) and c == CHUNKS - 1:
                            projected(c, s)
                            return
                        transposed(c + 1, 1 - s)
                        projected(c, s)

                    by_chunks(pe, front, logits)
                else:
                    by_chunks(pe, transposed, logits)
                pe.wait_ge(S["yd"], CHUNKS + 2)

            def weights(m):
                S = rt[m]
                for c in range(CHUNKS):
                    pe.wait_ge(S["w"], c + 1)
                    for k in range(CT):
                        last = pe.transpose(PS[:, c, k * P:(k + 1) * P], AO[:, c * CT + k, :], w["ident"][:, :])
                    last.then_inc(S["wt"], 1)
                pe.wait_ge(S["wtd"], CHUNKS)

            def experts(m):
                S, T = mo[m], NT[m]
                down = experts0["w2"] if m == 0 else experts1["dp"]
                credit(S["h"], BANKS[m])
                credit(S["dn"], HRING[m])
                credit(S["yt"], 1)
                pe.wait_ge(po[3 if m else 1]["mt"], 2 + CHUNKS)
                pe.wait_ge(e1_in if m else e0_in, 16 * len(experts1 if m else experts0))

                def up_products(c, s, j):
                    pos = s * T + j
                    x_t, col = MT[:, bass.ds(c * CHUNK, CHUNK)], slice(j * P, (j + 1) * P)
                    pe.wait_ge(S["h"], c * T + (j + 1))
                    if m == 0:
                        last = pe.matmul(PS[:, pos % 4, :], experts0["w1"][:, col], x_t, start=True, stop=True)
                    else:
                        bank = 2 * (pos % 2)
                        pe.matmul(PS[:, bank, :], experts1["gp"][:, col], x_t, start=True, stop=True)
                        last = pe.matmul(PS[:, bank + 1, :], experts1["up"][:, col], x_t, start=True, stop=True)
                    last.then_inc(S["g"], 1)

                def down_product(c, s, j):
                    if j == 0:
                        pe.wait_ge(S["oe"], c + 1)
                        if m == 0:
                            pe.matmul(PS[:, 6 + s, :], down[:, T, :], WT[:, bass.ds(c * CHUNK, CHUNK)],
                                      start=True, stop=False)
                    pe.wait_ge(S["h"], c * T + (j + 1 + BANKS[m]))
                    pe.matmul(PS[:, 6 + s, :], down[:, j, :], HB[:, (s * T + j) % HRING[m], :],
                              start=(j == 0 and m == 1), stop=(j == T - 1)).then_inc(S["dn"], 1)

                def output(c, s):
                    pe.wait_ge(S["oe"], c + 3)
                    pe.wait_ge(S["yd"], c + 1)
                    for k in range(CT):
                        last = pe.transpose(PS[:, 4 + s, k * P:(k + 1) * P], OT[:, k * P:(k + 1) * P], w["ident"][:, :])
                    last.then_inc(S["yt"], 1)

                def chunk(at, s, first, last):
                    if first:
                        for j in range(LOOK):
                            up_products(at(0), s, j)
                    for j in range(T):
                        if j + LOOK < T:
                            up_products(at(0), s, j + LOOK)
                        elif not last:
                            up_products(at(1), 1 - s, j + LOOK - T)
                        down_product(at(0), s, j)
                        if j == 2 and not first:
                            output(at(-1), 1 - s)
                    if last:
                        output(at(0), s)

                by_pipelined(pe, chunk)
                pe.wait_ge(S["yd"], CHUNKS + 2)

            pe.wait_ge(w_first, 16 * len(FIRST))
            project(0)
            pe.wait_ge(w_in, 16 * (len(w) - len(FIRST)))
            attention(0)
            output(0)
            project(1)
            attention(1)
            routed_input(1)
            weights(0)
            experts(0)
            project(2)
            attention(2)
            output(2)
            routed_input(3)
            weights(1)
            experts(1)

        @block.vector
        def _(v):
            n_dv = [0]

            def credit(s, n):
                v.nop().then_inc(s, n)

            def step(ins, at_=None):
                n_dv[0] += 1
                ins.then_inc(dv, 1)
                v.wait_ge(dv, n_dv[0])

            def deviations(k, tiles, n, done):
                st, (a, b, x, y) = ST[k], [TMP[q][:, 0:n] for q in range(4)]
                mean, rstd = MEAN[k][:, tiles], RSTD[k][:, tiles]
                v.tensor_tensor(a, st[:, tiles, 1], st[:, tiles, 4], ALU.add)
                v.tensor_tensor(b, st[:, tiles, 1], st[:, tiles, 4], ALU.subtract)
                done(v.tensor_tensor(x, st[:, tiles, 2], st[:, tiles, 5], ALU.add))
                v.tensor_scalar(mean, a, 0.5, None, ALU.mult)
                done(v.tensor_tensor(b, b, b, ALU.mult))
                done(v.scalar_tensor_tensor(x, b, DIM / 4.0, x, ALU.mult, ALU.add))
                done(v.tensor_scalar(x, x, 1.0 / DIM, EPS, ALU.mult, ALU.add))
                v.tensor_scalar(a, x, -0.5, None, ALU.mult)
                done(v.tensor_scalar(y.bitcast(I32), x.bitcast(I32), 1, None, ALU.logical_shift_right))
                done(v.tensor_scalar(y.bitcast(I32), y.bitcast(I32), -1.0, float(MAGIC), ALU.mult, ALU.add))
                for step_ in range(3):
                    done(v.tensor_tensor(b, y, a, ALU.mult))
                    done(v.tensor_tensor(b, b, y, ALU.mult))
                    done(v.scalar_tensor_tensor(rstd if step_ == 2 else y, b, 1.5, y, ALU.add, ALU.mult))

            def finish_stats(k):
                deviations(k, slice(0, TILES), TILES, step)
                if k:
                    step(v.scalar_tensor_tensor(SHIFT[:, :], MEAN[k][:, :], -1.0, RSTD[k][:, :], ALU.mult, ALU.mult))
                v.nop().then_inc(moments, 1)

            def loop_steps(per, count):
                base = n_dv[0]
                n_dv[0] += per * count
                return base

            def normalise(dst, src, k, t0):
                for q in range(CT):
                    last = v.tensor_scalar(dst(q), src[:, bass.ds(t0 + q, 1), :].rearrange("p a c -> p (a c)"),
                                           MEAN[k][:, bass.ds(t0 + q, 1)], RSTD[k][:, bass.ds(t0 + q, 1)],
                                           ALU.subtract, ALU.mult)
                return last

            def chunk_stats(src, k, t0):
                for q in range(CT):
                    last = v.bn_stats(ST[k][:, bass.ds(t0 + q, 1), :].rearrange("p a c -> p (a c)"),
                                      src[:, bass.ds(t0 + q, 1), :].rearrange("p a c -> p (a c)"))
                return last

            def project(a):
                L, S = LAYERS[a], pj[a]
                for name in ("nb", "vev", "split") if L.biased else ("nb", "split"):
                    credit(S[name], 2)
                base = loop_steps(2, CHUNKS)

                def front(c, s):
                    v.wait_ge(S["tr"], c + 1)
                    normalise(lambda q: XN[:, s, q, :], X, 0, c * CT).then_inc(S["xn"], 1)

                def back(c, s):
                    f = QKF[:, s, :, :]
                    pt = [PT[:, s, part, :, :] for part in range(3)]
                    v.wait_ge(S["ev"], c + 3)
                    v.tensor_tensor(f, f, pt[0], ALU.subtract).then_inc(dv, 1)
                    v.wait_ge(S["nrm"], c + 3)
                    v.tensor_reduce(NB[:, bass.ds(c, 1)], PS[0:64, 4 * s, :], AX.X, ALU.max).then_inc(S["nb"], 1)
                    v.wait_ge(dv, c * 2 + (base + 1))
                    v.wait_ge(rest_out[s], (c - s) * 32 + (16 + a * CHUNKS * 32))
                    v.tensor_copy(pt[1], f).then_inc(dv, 1)
                    v.wait_ge(dv, c * 2 + (base + 2))
                    v.tensor_tensor(pt[2], f, pt[1], ALU.subtract).then_inc(S["split"], 1)
                    if L.biased:
                        v.wait_ge(S["qkv"], c + 3)
                        v.tensor_tensor(VT[:, bass.ds(c * CT, CT), 0:L.M],
                                        PS[:, 4 * s + 3, 0:CT * L.M].rearrange("p (t m) -> p t m", t=CT),
                                        w["vb1"][:, :].unsqueeze(1).broadcast_to([P, CT, L.M]), ALU.add)\
                         .then_inc(S["vev"], 1)

                by_chunks(v, front, back, ahead=2)
                v.wait_ge(S["nb"], CHUNKS + 2)
                v.tensor_reduce(NBM[:, :], NB[:, :], AX.X, ALU.max).then_inc(flag_col, 1)
                v.wait_ge(flag_row, a + 1)
                step(v.tensor_copy(NBR[:, :], PS[0:1, 0, 0:64]))
                step(v.tensor_tensor(NBP[:, :], NBR[:, 0:32], NBR[:, 32:64], ALU.mult))
                step(v.tensor_reduce(NBX[:, :], NBP[:, :], AX.X, ALU.max))
                v.tensor_scalar(FLAG[:, a:a + 1], NBX[:, :], (RANGE / L.scale) ** 2, None, ALU.is_gt)\
                 .then_inc(flag_set, 1)
                v.wait_ge(flag_set, a + 1)

            def attention(a):
                L, T = LAYERS[a], at[a]
                flag = v.value_load(FLAG[0:1, a:a + 1], min_val=0, max_val=1)
                cols = L.hd
                credit(T["tr"], 1)
                credit(T["oev"], 2)

                def maxima(n, s):
                    with v.If(flag > 0):
                        for h in range(QH):
                            for qc in range(KT):
                                r = h * KT + qc
                                b0 = 2 * (r % 3)
                                v.wait_ge(T["mxr"], n * (QH * KT) + (r + 1))
                                keys = (qc + 1) * P if L.causal else SEQ
                                src = (PS[:, b0:b0 + 2, :].rearrange("p a b -> p (a b)"))[:, 0:keys]
                                v.tensor_reduce(MX[:, qc, h:h + 1], src, AX.X, ALU.max, negate=True).then_inc(T["mxd"], 1)
                        v.wait_ge(T["mxd"], n * (QH * KT) + QH * KT)
                        v.wait_ge(T["sht"], n + 1)

                        def part(k):
                            return [SHF[:, m, :, k:k + (L.hps - 1) * L.hd + 1:L.hd, 6] for m in range(L.slots)]

                        def heads(t, m):
                            return t[:, :, m * L.hps:(m + 1) * L.hps]

                        for k in range(3):
                            v.tensor_copy(MXP[:, :, :], MX[:, :, :]).then_inc(T["mxs"], 1)
                            v.wait_ge(T["mxs"], n * 6 + (2 * k + 1))
                            for m in range(L.slots):
                                last = v.tensor_copy(part(k)[m], heads(MXP, m))
                            if k < 2:
                                last = v.tensor_tensor(MX[:, :, :], MX[:, :, :], MXP[:, :, :], ALU.subtract)
                            last.then_inc(T["mxs"], 1)
                            v.wait_ge(T["mxs"], n * 6 + (2 * k + 2))
                        v.nop().then_inc(T["sh"], 1)
                        v.wait_ge(T["sht"], n + 2)
                        for m in range(L.slots):
                            last = v.tensor_tensor(QG[s][:, m, :], QG[s][:, m, :], PS[:, 2 * m, :].bitcast(BF16), ALU.add)
                        last.then_inc(T["shd"], 1)

                maxima(0, 0)
                base = loop_steps(1, QUADS)

                def quad(b, q, final):
                    n = b * 4 + q
                    for half in range(2):
                        v.wait_ge(T["pv"], n * L.U + (L.U + 1 + L.half_end[half]))
                        v.tensor_copy(OSB[:, half * CHUNK:(half + 1) * CHUNK], PS[:, 6 + half, :]).then_inc(T["oev"], 1)
                        if half == 0 and not final:
                            maxima(n + 1, (q + 1) % 2)
                    v.wait_ge(T["t"], n + 1)
                    b0 = 2 * T_PLACE
                    res = PS[:, b0:b0 + 2, :].rearrange("p a (k h r) -> p (a k) h r", k=4, h=QH)
                    v.reciprocal(RC[:, :, :], res[:, :, :, cols]).then_inc(dv, 1)
                    v.wait_ge(dv, n + (base + 1))
                    dst = AO[:, bass.ds(b * KT, KT), q * QH * L.hd:(q + 1) * QH * L.hd]
                    v.tensor_tensor(dst.rearrange("p t (h d) -> p t h d", h=QH), res[:, :, :, 0:cols],
                                    RC[:, :, :].unsqueeze(3).broadcast_to([P, KT, QH, cols]), ALU.mult)\
                     .then_inc(T["tr"], 1)

                with v.Fori(0, BATCHES - 1) as b:
                    for q in range(4):
                        quad(b, q, False)
                for q in range(4):
                    quad(BATCHES - 1, q, q == 3)

            def output(a):
                S = po[a]
                credit(S["yd"], 2)
                base = loop_steps(1, CHUNKS)

                def front(c, s):
                    v.wait_ge(S["m"], c + 3)
                    src = PS[:, 3 * s + 1, :].rearrange("p (t m) -> p t m", t=CT)
                    dst = AO[:, bass.ds(c * CT, CT), :]
                    if a == 0:
                        ins = v.tensor_tensor(dst, src, w["bo0"][:, :].unsqueeze(1).broadcast_to([P, CT, P]), ALU.add)
                    else:
                        ins = v.tensor_scalar(dst, src, 1.0 / 128.0, None, ALU.mult)
                    ins.then_inc(S["yd"], 1)

                def back(c, s):
                    v.wait_ge(S["yd"], c + 3)
                    chunk_stats(AO, 1, c * CT).then_inc(dv, 1)

                by_chunks(v, front, back)
                v.wait_ge(dv, base + CHUNKS)
                v.wait_ge(S["yd"], 2 + CHUNKS)

            def residual(a):
                base = loop_steps(1, CHUNKS)
                with v.Fori(0, CHUNKS) as c:
                    v.wait_ge(post[a], c + 3)
                    chunk_stats(X, 0, c * CT).then_inc(dv, 1)
                v.wait_ge(dv, base + CHUNKS)

            def routed_input(a):
                S = po[a]
                credit(S["yd"], 2)
                E, bias = (E0, w["rb"]) if a == 1 else (E1, None)

                def front(c, s):
                    if a == 3:
                        v.wait_ge(S["tr"], c + 1)
                        normalise(lambda q: XN[:, s, q, :], X, 0, c * CT).then_inc(S["xn"], 1)

                def back(c, s):
                    v.wait_ge(S["y"], c + 3)
                    src = PS[:, 3 * s + 2, 0:CT * E].rearrange("p (t m) -> p t m", t=CT)
                    dst = LG[:, bass.ds(c * CT, CT), 0:E]
                    if bias is not None:
                        ins = v.tensor_tensor(dst, src, bias[:, :].unsqueeze(1).broadcast_to([P, CT, E]), ALU.add)
                    else:
                        ins = v.tensor_copy(dst, src)
                    ins.then_inc(S["yd"], 1)

                by_chunks(v, front, back, ahead=2)
                v.wait_ge(S["yd"], 2 + CHUNKS)

            def rank(dst, val, E):
                step(v.tensor_copy(dst, w["later"][:, E1 - E:E1].unsqueeze(1).broadcast_to([P, TILES, E])))
                for d in range(1, E):
                    n = E - d
                    first = RA[:, 0:TILES * n].rearrange("p (t e) -> p t e", t=TILES)
                    step(v.tensor_tensor(first, val[:, :, 0:n], val[:, :, d:E], ALU.is_ge))
                    step(v.tensor_tensor(dst[:, :, d:E], dst[:, :, d:E], first, ALU.add))
                    step(v.tensor_tensor(dst[:, :, 0:n], dst[:, :, 0:n], first, ALU.subtract))

            def choose(dst, val, E, top):
                for t in range(TILES):
                    last = v.max(TOP8[:, t, :], val[:, t, :])
                step(last)
                kth = TOP8[:, :, top - 1:top].broadcast_to([P, TILES, E])
                equal, a, b = [RA[:, q * TILES * E:(q + 1) * TILES * E].rearrange("p (t e) -> p t e", t=TILES)
                               for q in range(3)]
                v.tensor_tensor(equal, val, kth, ALU.is_equal)
                step(v.tensor_tensor(dst, val, kth, ALU.is_gt))
                v.tensor_reduce(T1[:, :], dst, AX.X, ALU.add)
                src, d = equal, 1
                while d < E:
                    v.tensor_copy(a[:, :, 0:d], src[:, :, 0:d])
                    step(v.tensor_tensor(a[:, :, d:E], src[:, :, d:E], src[:, :, 0:E - d], ALU.add))
                    src, a, b, d = a, b, a, 2 * d
                step(v.tensor_tensor(a, src, wide(T1, E), ALU.add))
                step(v.scalar_tensor_tensor(a, a, top + 0.5, equal, ALU.is_lt, ALU.mult))
                step(v.tensor_tensor(dst, dst, a, ALU.add))

            def wide(t, E):
                return t[:, :].unsqueeze(2).broadcast_to([P, TILES, E])

            def finish_weights(m, scores, eps, E):
                rk, wr = RK[:, :, 0:E], WR[:, :, 0:E]
                step(v.tensor_tensor(wr, rk, scores, ALU.mult))
                step(v.tensor_reduce(T1[:, :], wr, AX.X, ALU.add))
                step(v.tensor_scalar(T1[:, :], T1[:, :], eps, None, ALU.add))
                step(v.reciprocal(T2[:, :], T1[:, :]))
                for c in range(CHUNKS):
                    tiles = slice(c * CT, (c + 1) * CT)
                    v.tensor_tensor(AO[:, tiles, :].rearrange("p t (e r) -> p t e r", e=E),
                                    wr[:, tiles, :].unsqueeze(3).broadcast_to([P, CT, E, P // E]),
                                    T2[:, tiles].unsqueeze(2).unsqueeze(3).broadcast_to([P, CT, E, P // E]),
                                    ALU.mult).then_inc(rt[m]["w"], 1)

            def route_softmax():
                lg, sc = LG[:, :, 0:E0], SC[:, :, 0:E0]
                step(v.tensor_reduce(T1[:, :], lg, AX.X, ALU.max))
                v.tensor_tensor(lg, lg, wide(T1, E0), ALU.subtract).then_inc(rt[0]["lg"], CHUNKS + 1)
                v.wait_ge(rt[0]["e"], 1)
                step(v.tensor_reduce(T1[:, :], sc, AX.X, ALU.add))
                step(v.reciprocal(T2[:, :], T1[:, :]))
                step(v.tensor_tensor(sc, sc, wide(T2, E0), ALU.mult))
                choose(RK[:, :, 0:E0], sc, E0, 2)
                finish_weights(0, sc, 1e-8, E0)

            def route_groups():
                v.nop().then_inc(rt[1]["lg"], CHUNKS)
                v.wait_ge(rt[1]["e"], 1)
                step(v.tensor_tensor(LG[:, :, :], SC[:, :, :], w["gb"][:, :].unsqueeze(1).broadcast_to([P, TILES, E1]),
                                     ALU.add))
                grp = LG[:, :, :].rearrange("p t (g k) -> p t g k", g=4)
                pairs = [(i, j) for i in range(4) for j in range(i + 1, 4)]
                for k, (i, j) in enumerate(pairs):
                    step(v.tensor_tensor(G4[0 if k == 0 else 1][:, :, :], grp[:, :, :, i], grp[:, :, :, j], ALU.add))
                    if k:
                        step(v.tensor_tensor(G4[0][:, :, :], G4[0][:, :, :], G4[1][:, :, :], ALU.max))
                rank(G4[2][:, :, :], G4[0][:, :, :], 4)
                step(v.tensor_scalar(G4[2][:, :, :], G4[2][:, :, :], 1.5, None, ALU.is_lt))
                step(v.tensor_tensor(grp, grp, G4[2][:, :, :].unsqueeze(3).broadcast_to([P, TILES, 4, 4]), ALU.mult))
                choose(RK[:, :, :], LG[:, :, :], E1, 4)
                finish_weights(1, SC[:, :, :], 1e-20, E1)

            def experts(m):
                S, T = mo[m], NT[m]
                credit(S["yd"], 2)
                v.wait_ge(rt[m]["wtd"], CHUNKS)
                steps = []

                def finish(c, s, parts):
                    y_ps = PS[:, 4 + s, :]
                    tiles, t0 = bass.ds(c * CT, CT), c * CT

                    def done(ins):
                        steps[-1] += 1
                        ins.then_inc(S["f"], 1)
                        v.wait_ge(S["f"], c * FINISH_STEPS[m] + steps[-1])

                    for part in parts:
                        if part == 0:
                            steps.append(0)
                            if m == 0:
                                done(normalise(lambda q: YN[:, q, :], X, 0, t0))
                        if part == 1:
                            v.wait_ge(S["yt"], c + 2)
                            dst = AO[:, tiles, :].rearrange("p t m -> p (t m)")
                            if m == 0:
                                ins = v.scalar_tensor_tensor(dst, y_ps, 0.3, YN[:, :, :].rearrange("p t m -> p (t m)"),
                                                             ALU.mult, ALU.add)
                            else:
                                ins = v.tensor_copy(dst, y_ps)
                            ins.then_inc(S["yd"], 1)
                            v.wait_ge(S["yd"], c + 3)
                        if part == 2:
                            done(chunk_stats(AO, 1, t0))
                        if part == 3:
                            deviations(1, tiles, CT, done)
                        if part == 4:
                            done(normalise(lambda q: YN[:, q, :], AO, 1, t0))
                        if part == 5:
                            v.tensor_tensor(X[:, tiles, :], X[:, tiles, :], YN[:, :, :], ALU.add)\
                             .then_inc(post[2 * m + 1], 1)
                            if m == 0:
                                v.wait_ge(post[1], c + 1)
                        if part == 6:
                            if m == 0:
                                done(chunk_stats(X, 0, t0))
                            assert steps[-1] == FINISH_STEPS[m]

                def chunk(at, s, first, last):
                    for j in range(T):
                        pos = s * T + j
                        h = HB[:, pos % HRING[m], :]
                        v.wait_ge(S["a"], at(0) * T + (j + 1))
                        if m == 1:
                            v.tensor_tensor(h, h, PS[:, 2 * (pos % 2) + 1, :], ALU.mult)\
                             .then_inc(S["u" if j < ROUTED[m] else "h"], 1)
                            if j < ROUTED[m]:
                                v.wait_ge(S["u"], at(0) * ROUTED[m] + (j + 1))
                        if j < ROUTED[m]:
                            v.tensor_tensor(h, h, WT[:, bass.ds(at(0) * CHUNK, CHUNK)], ALU.mult).then_inc(S["h"], 1)
                        if not first and 4 <= j < 11:
                            finish(at(-1), 1 - s, [j - 4])
                    if last:
                        finish(at(0), s, range(7))

                by_pipelined(v, chunk)

            v.memset(WARM[:, :], 0.0)
            step(v.memset(SHF[:, :, :, :, :].rearrange("p a b c d -> p (a b c d)"), 0.0))
            for b in range(2):
                v.wait_ge(x_in[b], 32)
                for c in range(b * CHUNKS // 2, (b + 1) * CHUNKS // 2):
                    step_ = chunk_stats(X, 0, c * CT)
            step(step_)
            finish_stats(0)
            project(0)
            v.wait_ge(w_in, 16 * (len(w) - len(FIRST)))
            attention(0)
            output(0)
            finish_stats(1)
            residual(0)
            finish_stats(0)
            project(1)
            attention(1)
            routed_input(1)
            route_softmax()
            experts(0)
            step(v.memset(SHF[:, :, :, :, :].rearrange("p a b c d -> p (a b c d)"), 0.0))
            finish_stats(0)
            project(2)
            attention(2)
            output(2)
            finish_stats(1)
            residual(2)
            finish_stats(0)
            routed_input(3)
            route_groups()
            experts(1)


def host_layout(i):
    bf = np.dtype("bfloat16")
    f = {k: np.asarray(v) for k, v in i.items()}

    def c(a):
        return np.ascontiguousarray(a)

    def row(a, n=P):
        return c(np.broadcast_to(a.reshape(1, -1), (n, a.size)))

    def padded(a, rows, cols):
        out = np.zeros((rows, cols), a.dtype)
        out[0:a.shape[0], 0:a.shape[1]] = a
        return out

    d = {"x": c(f["L0_attn_x"].reshape(TOKENS, DIM))}
    d["ident"] = np.eye(P, dtype=np.float32)
    d["identb"] = np.eye(P, dtype=np.float32).astype(bf)
    lower = np.arange(P)[:, None] > np.arange(P)[None, :]
    d["maskT"] = np.where(lower, np.float32(MASKED), np.float32(0)).astype(bf)
    d["mask"] = np.where(lower.T, np.float32(MASKED), np.float32(0)).astype(bf)
    for hd in (4, 8):
        d[f"blk{hd}"] = (np.arange(P)[:, None] // hd == np.arange(32)[None, :]).astype(bf)
    d["later"] = row(np.arange(E1 - 1, -1, -1).astype(np.float32))
    d["wq0"], d["wk0"] = padded(f["L0_attn_Wq"].T, P, P), padded(f["L0_attn_Wk"].T, P, P)
    d["wv0"], d["wo0"] = padded(f["L0_attn_Wv"].T, P, 64), padded(f["L0_attn_Wo"].T, P, P)
    d["bo0"] = row(f["L0_attn_bo"])
    d["wq1"] = padded(f["L0_ffn_q_w"].reshape(DIM, HEADS, 8)[:, :, 0:4].reshape(DIM, 64), P, P)
    d["qb1"] = padded(f["L0_ffn_q_b"].reshape(HEADS, 8)[:, 0:4].reshape(64, 1), P, 1)
    d["wk1"], d["wv1"] = padded(f["L0_ffn_k_w"], P, P), c(f["L0_ffn_v_w"])
    d["kb1"], d["vb1"] = padded(f["L0_ffn_k_b"].reshape(64, 1), P, 1), row(f["L0_ffn_v_b"])
    d["wo1"], d["ob1"] = padded(f["L0_ffn_o_w"][0:64], P, P), c(f["L0_ffn_o_b"].reshape(P, 1))
    d["rw"], d["rb"] = c(f["L0_ffn_router_w"]), row(f["L0_ffn_router_b"])
    r = P // E0
    d["w1"] = c(f["L0_ffn_w1"].reshape(E0, DIM, NT[0], r).transpose(1, 2, 0, 3).reshape(DIM, NT[0] * P))
    d["b1"] = c(f["L0_ffn_b1"].reshape(E0, NT[0], r).transpose(0, 2, 1).reshape(P, NT[0]))
    w2 = np.zeros((P, NT[0] + 1, P), np.float32)
    w2[:, 0:NT[0]] = f["L0_ffn_w2"].reshape(E0, NT[0], r, P).transpose(0, 2, 1, 3).reshape(P, NT[0], P)
    w2[::r, NT[0]] = f["L0_ffn_b2"]
    d["w2"] = w2
    for n, name in (("wq2", "query"), ("wk2", "key"), ("wv2", "value"), ("wo2", "proj")):
        d[n] = c(f[f"L1_attn_W_{name}"].T)
    d["gw"], d["gb"] = c(f["L1_ffn_gate_w"].T), row(f["L1_ffn_gate_bias"])
    r = P // E1
    for n, routed, shared in (("gp", "gate_proj", "shared_gate_w"), ("up", "up_proj", "shared_up_w")):
        a = np.zeros((DIM, NT[1] * P), np.float32)
        a[:, 0:E1 * I1] = f[f"L1_ffn_{routed}"].reshape(E1, ROUTED[1], r, DIM).transpose(3, 1, 0, 2).reshape(DIM, E1 * I1)
        a[:, E1 * I1:E1 * I1 + SH1] = f[f"L1_ffn_{shared}"].T
        d[n] = a
    a = np.zeros((P, NT[1], P), np.float32)
    a[:, 0:ROUTED[1]] = f["L1_ffn_down_proj"].reshape(E1, P, ROUTED[1], r).transpose(0, 3, 2, 1).reshape(P, ROUTED[1], P)
    shared = padded(f["L1_ffn_shared_down_w"].T, (NT[1] - ROUTED[1]) * P, P)
    a[:, ROUTED[1]:] = shared.reshape(NT[1] - ROUTED[1], P, P).transpose(1, 0, 2)
    d["dp"] = a
    return d


def kernel(**inputs):
    from concourse import bacc
    from concourse.bass_utils import run_bass_kernel_spmd

    arrays = host_layout(inputs)
    nc = bacc.Bacc("TRN2", target_bir_lowering=False, num_devices=1)
    t_in = {n: nc.dram_tensor(f"in_{n}", a.shape, mybir.dt.from_np(a.dtype), kind="ExternalInput").ap()
            for n, a in arrays.items()}
    out = nc.dram_tensor("result", (TOKENS, DIM), FP32, kind="ExternalOutput").ap()
    build_program(nc, t_in, out)
    r = run_bass_kernel_spmd(nc, [{f"in_{n}": a for n, a in arrays.items()}], core_ids=[0])
    return r.results[0]["result"].reshape(BATCHES, SEQ, DIM)
```
